# Optimizing a Trainium2 kernel written in Bass

```python
import numpy as np
import jax
import jax.numpy as jnp

def _softmax(x, axis=-1):
    return jax.nn.softmax(x, axis=axis)

def _gelu(x):
    return jax.nn.gelu(x, approximate=True)

def _silu(x):
    return jax.nn.silu(x)

def _sigmoid(x):
    return jax.nn.sigmoid(x)

def _layernorm(x, axis=-1, eps=1e-05):
    m = jnp.mean(x, axis=axis, keepdims=True)
    v = jnp.var(x, axis=axis, keepdims=True)
    return (x - m) / jnp.sqrt(v + eps)

def _scatter_add(tgt, idx, src, axis=0):
    return tgt.at[idx].add(src)

def _segment_sum(src, seg, n):
    return jax.ops.segment_sum(src, seg, n)
kernel_name = 'mk_gnn_preln_d4_gnn_r32_75bfef'

def setup_inputs(seed: int=0):
    np.random.seed(seed)
    _w = jnp.asarray

    def _rec_inputs():
        import jax
        import jax.numpy as jnp
        _gk = jax.random.key(seed)
        x = -0.0002117 + 1 * jax.random.normal(jax.random.fold_in(_gk, 1), (3125, 256), jnp.float32)
        src = jax.random.randint(jax.random.fold_in(_gk, 2), (50000,), 0, 3125, jnp.int32)
        dst = jnp.minimum((3125 * jax.random.uniform(jax.random.fold_in(_gk, 3), (50000,)) ** 2.0).astype(jnp.int32), 99999)
        _o = jnp.argsort(dst, stable=True)
        src = src[_o]
        dst = dst[_o]
        edge_weight = jax.random.uniform(jax.random.fold_in(_gk, 13), (50000,), jnp.float32, 0.0, 0.999999)
        node_vec1 = jax.random.uniform(jax.random.fold_in(_gk, 14), (3125, 1), jnp.float32, 0.0, 0.999991)
        node_vec1_n2 = jax.random.uniform(jax.random.fold_in(_gk, 15), (3125, 1), jnp.float32, 0.0, 0.999991)
        return (x, src, dst, edge_weight, node_vec1, node_vec1_n2)
    x, src, dst, edge_weight, node_vec1, node_vec1_n2 = _rec_inputs()

    def _L0_gnn_setup():
        import jax, jax.numpy as jnp
        import numpy as np
        N_NODES = 3125
        N_EDGES = 100000
        IN_FEATS = 256
        OUT_FEATS = 256
        key = jax.random.key(seed)
        ks = jax.random.split(key, 8)
        feat = jax.random.normal(ks[0], (N_NODES, IN_FEATS), dtype=jnp.float32)
        norm0 = jax.random.uniform(ks[1], (N_NODES, 1), dtype=jnp.float32)
        norm1 = jax.random.uniform(ks[2], (N_NODES, 1), dtype=jnp.float32)
        limit = float(np.sqrt(6.0 / (IN_FEATS + OUT_FEATS)))
        weight = jax.random.uniform(ks[3], (IN_FEATS, OUT_FEATS), dtype=jnp.float32, minval=-limit, maxval=limit)
        bias = jnp.zeros((OUT_FEATS,), dtype=jnp.float32)
        edge_row = jax.random.randint(ks[4], (N_EDGES,), 0, N_NODES, dtype=jnp.int32)
        edge_col = jax.random.randint(ks[5], (N_EDGES,), 0, N_NODES, dtype=jnp.int32)
        edge_vals = jax.random.uniform(ks[6], (N_EDGES,), dtype=jnp.float32)
        return {'feat': feat, 'norm0': norm0, 'norm1': norm1, 'weight': weight, 'bias': bias, 'edge_row': edge_row, 'edge_col': edge_col, 'edge_vals': edge_vals}
    _L0_gnn_all = _L0_gnn_setup()
    _L0_gnn_in = {k: v for k, v in _L0_gnn_all.items() if k in ('weight', 'bias')}
    del _L0_gnn_all

    def _L1_gnn_setup():
        import jax, jax.numpy as jnp
        import numpy as np
        N = 50000
        E = 25000
        IN = 256
        HID = 64
        HEADS = 4
        OUT = 256
        NEG_SLOPE = 0.2

        def _gat_layer(x, src, dst, W, a_src, a_dst, b, heads, concat):
            n = x.shape[0]
            h = (x @ W).reshape(n, heads, -1)
            al_s = jnp.einsum('nhf,hf->nh', h, a_src)
            al_d = jnp.einsum('nhf,hf->nh', h, a_dst)
            e = jax.nn.leaky_relu(al_s[src] + al_d[dst], NEG_SLOPE)
            m = jax.lax.stop_gradient(jax.ops.segment_max(e, dst, num_segments=n))
            ex = jnp.exp(e - m[dst])
            denom = jax.ops.segment_sum(ex, dst, num_segments=n)
            alpha = ex / (denom[dst] + 1e-16)
            out = jax.ops.segment_sum(h[src] * alpha[:, :, None], dst, num_segments=n)
            out = out.reshape(n, -1) if concat else out.mean(axis=1)
            return out + b
        key = jax.random.key(seed)
        ks = jax.random.split(key, 12)
        s = 0.1
        return {'x': jax.random.normal(ks[0], (N, IN), jnp.float32), 'edge_index': jax.random.randint(ks[1], (2, E), 0, N, dtype=jnp.int32), 'W1': jax.random.normal(ks[2], (IN, HEADS * HID), jnp.float32) * s, 'att_src1': jax.random.normal(ks[3], (HEADS, HID), jnp.float32) * s, 'att_dst1': jax.random.normal(ks[4], (HEADS, HID), jnp.float32) * s, 'b1': jnp.zeros((HEADS * HID,), jnp.float32), 'W2': jax.random.normal(ks[5], (HEADS * HID, OUT), jnp.float32) * s, 'att_src2': jax.random.normal(ks[6], (1, OUT), jnp.float32) * s, 'att_dst2': jax.random.normal(ks[7], (1, OUT), jnp.float32) * s, 'b2': jnp.zeros((OUT,), jnp.float32)}
    _L1_gnn_all = _L1_gnn_setup()
    _L1_gnn_in = {k: v for k, v in _L1_gnn_all.items() if k in ('W1', 'att_src1', 'att_dst1', 'b1', 'W2', 'att_src2', 'att_dst2', 'b2')}
    del _L1_gnn_all

    def _L2_gnn_setup():
        import jax, jax.numpy as jnp
        import numpy as np
        N = 3125
        E = 50000
        IN_FEATS = 256
        OUT_FEATS = 256
        MAXK = 32

        def _maxk(x, k):
            _, idx = jax.lax.top_k(x, k)
            rows = jnp.arange(x.shape[0])[:, None]
            mask = jnp.zeros_like(x).at[rows, idx].set(1.0)
            return x * mask
        key = jax.random.key(seed)
        k1, k2, k3, k4, k5 = jax.random.split(key, 5)
        feat = jax.random.normal(k1, (N, IN_FEATS), dtype=jnp.float32)
        W_self = jax.random.normal(k2, (IN_FEATS, OUT_FEATS), dtype=jnp.float32) * (1.0 / np.sqrt(IN_FEATS))
        W_neigh = jax.random.normal(k3, (IN_FEATS, OUT_FEATS), dtype=jnp.float32) * (1.0 / np.sqrt(IN_FEATS))
        src = jax.random.randint(k4, (E,), 0, N, dtype=jnp.int64)
        dst = jax.random.randint(k5, (E,), 0, N, dtype=jnp.int64)
        return {'feat': feat, 'W_self': W_self, 'W_neigh': W_neigh, 'src': src, 'dst': dst}
    _L2_gnn_all = _L2_gnn_setup()
    _L2_gnn_in = {k: v for k, v in _L2_gnn_all.items() if k in ('W_self', 'W_neigh')}
    del _L2_gnn_all

    def _L3_gnn_setup():
        import jax, jax.numpy as jnp
        import numpy as np
        N = 50000
        E = 25000
        HEADS = 4
        C = 64
        IN = 256
        NEG_SLOPE = 0.2

        def _gat_forward(x, edge_index, W, att_src, att_dst, bias):
            n = x.shape[0]
            h = (x @ W).reshape(n, HEADS, C)
            loop = jnp.arange(n, dtype=edge_index.dtype)
            src = jnp.concatenate([edge_index[0], loop])
            dst = jnp.concatenate([edge_index[1], loop])
            a_src = jnp.einsum('nhc,hc->nh', h, att_src)
            a_dst = jnp.einsum('nhc,hc->nh', h, att_dst)
            logits = a_src[src] + a_dst[dst]
            logits = jnp.where(logits >= 0, logits, NEG_SLOPE * logits)
            seg_max = jax.ops.segment_max(logits, dst, num_segments=n)
            seg_max = jnp.where(jnp.isfinite(seg_max), seg_max, 0.0)
            ex = jnp.exp(logits - seg_max[dst])
            denom = jax.ops.segment_sum(ex, dst, num_segments=n)
            alpha = ex / (denom[dst] + 1e-16)
            msgs = alpha[:, :, None] * h[src]
            out = jax.ops.segment_sum(msgs, dst, num_segments=n)
            out = out.reshape(n, HEADS * C) + bias
            return jax.nn.relu(out)
        key = jax.random.key(seed)
        k = jax.random.split(key, 6)
        x = jax.random.normal(k[0], (N, IN), dtype=jnp.float32)
        edge_index = jax.random.randint(k[1], (2, E), 0, N, dtype=jnp.int64)
        W = jax.random.normal(k[2], (IN, HEADS * C), dtype=jnp.float32) * (1.0 / np.sqrt(IN))
        att_src = jax.random.normal(k[3], (HEADS, C), dtype=jnp.float32) * (1.0 / np.sqrt(C))
        att_dst = jax.random.normal(k[4], (HEADS, C), dtype=jnp.float32) * (1.0 / np.sqrt(C))
        bias = jax.random.normal(k[5], (HEADS * C,), dtype=jnp.float32) * 0.02
        return {'x': x, 'edge_index': edge_index, 'W': W, 'att_src': att_src, 'att_dst': att_dst, 'bias': bias}
    _L3_gnn_all = _L3_gnn_setup()
    _L3_gnn_in = {k: v for k, v in _L3_gnn_all.items() if k in ('W', 'att_src', 'att_dst', 'bias')}
    del _L3_gnn_all
    return {'x': x, 'src': src, 'dst': dst, 'edge_weight': edge_weight, 'node_vec1': node_vec1, 'node_vec1_n2': node_vec1_n2, 'L0_gnn_weight': _L0_gnn_in['weight'], 'L0_gnn_bias': _L0_gnn_in['bias'], 'L1_gnn_W1': _L1_gnn_in['W1'], 'L1_gnn_att_src1': _L1_gnn_in['att_src1'], 'L1_gnn_att_dst1': _L1_gnn_in['att_dst1'], 'L1_gnn_b1': _L1_gnn_in['b1'], 'L1_gnn_W2': _L1_gnn_in['W2'], 'L1_gnn_att_src2': _L1_gnn_in['att_src2'], 'L1_gnn_att_dst2': _L1_gnn_in['att_dst2'], 'L1_gnn_b2': _L1_gnn_in['b2'], 'L2_gnn_W_self': _L2_gnn_in['W_self'], 'L2_gnn_W_neigh': _L2_gnn_in['W_neigh'], 'L3_gnn_W': _L3_gnn_in['W'], 'L3_gnn_att_src': _L3_gnn_in['att_src'], 'L3_gnn_att_dst': _L3_gnn_in['att_dst'], 'L3_gnn_bias': _L3_gnn_in['bias']}

def reference(x, src, dst, edge_weight, node_vec1, node_vec1_n2, L0_gnn_weight, L0_gnn_bias, L1_gnn_W1, L1_gnn_att_src1, L1_gnn_att_dst1, L1_gnn_b1, L1_gnn_W2, L1_gnn_att_src2, L1_gnn_att_dst2, L1_gnn_b2, L2_gnn_W_self, L2_gnn_W_neigh, L3_gnn_W, L3_gnn_att_src, L3_gnn_att_dst, L3_gnn_bias):
    import jax
    import jax.numpy as jnp

    def _L0_gnn_ref(feat, norm0, norm1, weight, bias, edge_row, edge_col, edge_vals):
        import jax, jax.numpy as jnp
        import numpy as np
        N_NODES = 3125
        N_EDGES = 100000
        IN_FEATS = 256
        OUT_FEATS = 256
        h = feat * norm0
        h = jnp.matmul(h, weight)
        gathered = edge_vals[:, None] * h[edge_col]
        rst = jax.ops.segment_sum(gathered, edge_row, num_segments=N_NODES)
        rst = rst + bias
        return jax.nn.relu(rst)

    def _L1_gnn_ref(x, edge_index, W1, att_src1, att_dst1, b1, W2, att_src2, att_dst2, b2):
        import jax, jax.numpy as jnp
        import numpy as np
        N = 50000
        E = 25000
        IN = 256
        HID = 64
        HEADS = 4
        OUT = 256
        NEG_SLOPE = 0.2

        def _gat_layer(x, src, dst, W, a_src, a_dst, b, heads, concat):
            n = x.shape[0]
            h = (x @ W).reshape(n, heads, -1)
            al_s = jnp.einsum('nhf,hf->nh', h, a_src)
            al_d = jnp.einsum('nhf,hf->nh', h, a_dst)
            e = jax.nn.leaky_relu(al_s[src] + al_d[dst], NEG_SLOPE)
            m = jax.lax.stop_gradient(jax.ops.segment_max(e, dst, num_segments=n))
            ex = jnp.exp(e - m[dst])
            denom = jax.ops.segment_sum(ex, dst, num_segments=n)
            alpha = ex / (denom[dst] + 1e-16)
            out = jax.ops.segment_sum(h[src] * alpha[:, :, None], dst, num_segments=n)
            out = out.reshape(n, -1) if concat else out.mean(axis=1)
            return out + b
        n = x.shape[0]
        loop = jnp.arange(n, dtype=edge_index.dtype)
        ei = jnp.concatenate([edge_index, jnp.stack([loop, loop])], axis=1)
        src, dst = (ei[0], ei[1])
        h = _gat_layer(x, src, dst, W1, att_src1, att_dst1, b1, HEADS, True)
        h = jax.nn.elu(h)
        out = _gat_layer(h, src, dst, W2, att_src2, att_dst2, b2, 1, False)
        return out

    def _L2_gnn_ref(feat, W_self, W_neigh, src, dst):
        import jax, jax.numpy as jnp
        import numpy as np
        N = 3125
        E = 50000
        IN_FEATS = 256
        OUT_FEATS = 256
        MAXK = 32

        def _maxk(x, k):
            _, idx = jax.lax.top_k(x, k)
            rows = jnp.arange(x.shape[0])[:, None]
            mask = jnp.zeros_like(x).at[rows, idx].set(1.0)
            return x * mask
        n = feat.shape[0]
        h_self = feat @ W_self
        h_neigh = feat @ W_neigh
        h_sparse = _maxk(h_neigh, MAXK)
        msg = h_sparse[src]
        summed = jax.ops.segment_sum(msg, dst, num_segments=n)
        deg = jax.ops.segment_sum(jnp.ones((src.shape[0],), dtype=feat.dtype), dst, num_segments=n)
        neigh = summed / jnp.maximum(deg, 1.0)[:, None]
        return h_self + neigh

    def _L3_gnn_ref(x, edge_index, W, att_src, att_dst, bias):
        import jax, jax.numpy as jnp
        import numpy as np
        N = 50000
        E = 25000
        HEADS = 4
        C = 64
        IN = 256
        NEG_SLOPE = 0.2

        def _gat_forward(x, edge_index, W, att_src, att_dst, bias):
            n = x.shape[0]
            h = (x @ W).reshape(n, HEADS, C)
            loop = jnp.arange(n, dtype=edge_index.dtype)
            src = jnp.concatenate([edge_index[0], loop])
            dst = jnp.concatenate([edge_index[1], loop])
            a_src = jnp.einsum('nhc,hc->nh', h, att_src)
            a_dst = jnp.einsum('nhc,hc->nh', h, att_dst)
            logits = a_src[src] + a_dst[dst]
            logits = jnp.where(logits >= 0, logits, NEG_SLOPE * logits)
            seg_max = jax.ops.segment_max(logits, dst, num_segments=n)
            seg_max = jnp.where(jnp.isfinite(seg_max), seg_max, 0.0)
            ex = jnp.exp(logits - seg_max[dst])
            denom = jax.ops.segment_sum(ex, dst, num_segments=n)
            alpha = ex / (denom[dst] + 1e-16)
            msgs = alpha[:, :, None] * h[src]
            out = jax.ops.segment_sum(msgs, dst, num_segments=n)
            out = out.reshape(n, HEADS * C) + bias
            return jax.nn.relu(out)
        return _gat_forward(x, edge_index, W, att_src, att_dst, bias)
    edge_index = jnp.stack([src, dst])
    h = jnp.maximum(_layernorm(x, axis=-1), 0.0)
    x = x + _L0_gnn_ref(h, node_vec1, node_vec1_n2, L0_gnn_weight, L0_gnn_bias, src, dst, edge_weight)
    h = jnp.maximum(_layernorm(x, axis=-1), 0.0)
    x = x + _L1_gnn_ref(h, edge_index, L1_gnn_W1, L1_gnn_att_src1, L1_gnn_att_dst1, L1_gnn_b1, L1_gnn_W2, L1_gnn_att_src2, L1_gnn_att_dst2, L1_gnn_b2)
    h = jnp.maximum(_layernorm(x, axis=-1), 0.0)
    x = x + _L2_gnn_ref(h, L2_gnn_W_self, L2_gnn_W_neigh, src, dst)
    h = jnp.maximum(_layernorm(x, axis=-1), 0.0)
    x = x + _L3_gnn_ref(h, edge_index, L3_gnn_W, L3_gnn_att_src, L3_gnn_att_dst, L3_gnn_bias)
    return x

_drawn_inputs = setup_inputs


def setup_inputs(seed=0):
    import zlib

    import numpy as np

    out = dict(_drawn_inputs(seed))
    spreads = {'L0_gnn_bias': (0.0, 0.1), 'L1_gnn_b1': (0.0, 0.1), 'L1_gnn_b2': (0.0, 0.1)}
    factors = {'L1_gnn_att_dst1': 19.19,
     'L1_gnn_att_dst2': 38.487,
     'L3_gnn_att_src': 6.049,
     'L3_gnn_att_dst': 26.356,
     'L3_gnn_bias': 8.0,
     'L1_gnn_att_src2': 2.853}
    for name, (base, spread) in spreads.items():
        noise = np.random.default_rng([zlib.crc32(name.encode()), seed]).standard_normal(out[name].shape)
        drawn = base * np.exp(spread * noise) if base else spread * noise
        out[name] = jnp.asarray(drawn.astype(out[name].dtype))
    for name, factor in factors.items():
        out[name] = (out[name] * factor).astype(out[name].dtype)
    return out
```

```python
import numpy as np
import concourse.bass as bass
from concourse import mybir
from contextlib import ExitStack

fp32 = mybir.dt.float32
bf16 = mybir.dt.bfloat16
i32 = mybir.dt.int32
u8 = mybir.dt.uint8
ALU = mybir.AluOpType
ACT = mybir.ActivationFunctionType
X = mybir.AxisListType.X

P = 128
BIG = 1e30
NEG_SLOPE = 0.2
EPS_LN = 1e-5
EPS_DEN = 1e-16


class Chain:

    def __init__(self, engine, sem):
        self.engine, self.sem, self.n = engine, sem, 0

    def step(self, instruction):
        instruction.then_inc(self.sem, 1)
        self.n = self.n + 1

    def link(self, instruction):
        self.step(instruction)
        self.engine.wait_ge(self.sem, self.n)


def gnn_kernel(nc, a, out):
    N, F = a["x"].shape
    E = a["src"].shape[0]
    K2 = F // P
    NT = -(-N // P)
    LAST = N - (NT - 1) * P
    NP = NT * P
    QB = 4
    U = 8
    C = -(-(E + 1) // (P * U)) * U
    Q = C // QB
    EP = C * P
    CX = C + NT - 1
    CX = -(-CX // U) * U
    PAD = NP - 1
    H = a["L1_gnn_att_src1"].shape[0]
    CH = F // H
    AUX = 2 * H + 1
    WX = F + 2 * H
    WMAX = 2 * F
    POS_N = NT * C
    PIECES = 20
    PW = POS_N // PIECES
    assert Q * QB == C and POS_N % PIECES == 0 and PW <= 512 and PAD >= N and C % U == 0

    tables = [nc.dram_tensor(f"table_{n}", (NP, F), fp32, kind="Internal").ap() for n in range(5)]
    records = nc.dram_tensor("records", (EP, 4), fp32, kind="Internal").ap()
    dst_padded = nc.dram_tensor("dst_padded", (EP,), fp32, kind="Internal").ap()
    low_rows = nc.dram_tensor("low_rows", (2, EP), u8, kind="Internal").ap()

    top = ExitStack()
    names = [0]

    def sb(stack, name, shape, dt):
        names[0] += 1
        return stack.enter_context(nc.sbuf_tensor(f"{name}_{names[0]}", shape, dt))

    def banks(stack, name, n):
        names[0] += 1
        return [stack.enter_context(nc.psum_tensor(f"{name}_{names[0]}_{i}", [P, 512], fp32)) for i in range(n)]

    def sem(stack, name):
        names[0] += 1
        s = stack.enter_context(nc.semaphore(f"{name}_{names[0]}"))
        stack.callback(lambda: nc.sync.sem_clear(s))
        return s

    with top:
        ident = sb(top, "ident", [P, P], fp32)
        iota = sb(top, "iota", [P, P], fp32)
        part = sb(top, "part", [P, 1], fp32)
        ones = sb(top, "ones", [P, P], fp32)
        row0 = sb(top, "row0", [P, P], fp32)
        hot_hi = [sb(top, f"hot_hi{w}", [P, NT, C], u8) for w in range(2)]
        gidx_d = sb(top, "gidx_d", [P, CX], fp32)
        gidx_s = sb(top, "gidx_s", [P, CX], fp32)
        local_d = sb(top, "local_d", [P, CX], fp32)
        local_s = sb(top, "local_s", [P, CX], fp32)
        w_s = sb(top, "w_s", [P, CX], fp32)
        tile_d = sb(top, "tile_d", [1, CX], i32)
        tile_s = sb(top, "tile_s", [1, CX], i32)
        begin_d = sb(top, "begin_d", [1, NT], i32)
        begin_s = sb(top, "begin_s", [1, NT], i32)
        is_last = sb(top, "is_last", [P, C], fp32)
        reset_f = sb(top, "reset_f", [Q, H * QB * P], fp32)
        reset_b = sb(top, "reset_b", [Q, H * QB * P], fp32)
        join_f = sb(top, "join_f", [H, C], fp32)
        join_b = sb(top, "join_b", [H, C], fp32)
        gate_f = sb(top, "gate_f", [H, C], fp32)
        gate_b = sb(top, "gate_b", [H, C], fp32)
        edge_aux = sb(top, "edge_aux", [P, CX, AUX], fp32)

        def row_broadcast(vec, rows=P):
            return vec.partition_broadcast(rows)

        slot_done = [top.enter_context(nc.semaphore(f"slot_done{s}")) for s in range(U)]
        slots_used = [0]

        with ExitStack() as ph, nc.Block() as block:
            made = sem(ph, "made")

            @block.gpsimd
            def _(pool):
                pool.iota(iota[:, :], [[1, P]], 0, 0, allow_small_or_imprecise_dtypes=True).then_inc(made, 1)
                pool.iota(part[:, :], [[0, 1]], 0, 1, allow_small_or_imprecise_dtypes=True).then_inc(made, 1)
                pool.memset(ident[:, :], 0.0).then_inc(made, 1)
                pool.memset(row0[:, :], 0.0).then_inc(made, 1)
                pool.memset(ones[:, :], 1.0).then_inc(made, 1)
                pool.wait_ge(made, 5)
                pool.affine_select(out=ident[:, :], in_=ident[:, :], compare_op=ALU.not_equal, fill=1.0, base=0,
                                   pattern=[[-1, P]], channel_multiplier=1).then_inc(made, 1)
                pool.memset(row0[0:1, :], 1.0).then_inc(made, 1)
                pool.wait_ge(made, 7)

        with ExitStack() as ph:
            rows_i = sb(ph, "rows_i", [Q, 2, QB * P], i32)
            rows_lo = sb(ph, "rows_lo", [Q, 2, QB * P], i32)
            rows_lo8 = sb(ph, "rows_lo8", [Q, 2, QB * P], u8)
            rows_f = sb(ph, "rows_f", [Q, 2, QB * P], fp32)
            rows_w = sb(ph, "rows_w", [Q, QB * P], fp32)
            edge = sb(ph, "edge", [P, 2, C], fp32)
            edge_w = sb(ph, "edge_w", [P, C], fp32)
            edge_i = sb(ph, "edge_i", [P, 2, C], i32)
            hi_i = sb(ph, "hi_i", [P, 2, C], i32)
            hi_f = sb(ph, "hi_f", [P, 2, C], fp32)
            hi_rep = sb(ph, "hi_rep", [P, 2, C], fp32)
            next_first = sb(ph, "next_first", [Q, QB], fp32)
            chunk_first = sb(ph, "chunk_first", [H, C], fp32)
            chunk_last = sb(ph, "chunk_last", [H, C], fp32)
            last_rows = sb(ph, "last_rows", [Q, QB, P], fp32)
            counts = sb(ph, "counts", [P, 2, NT], fp32)
            begins = sb(ph, "begins", [1, 2, NT], fp32)
            begins_i = sb(ph, "begins_i", [1, 2, NT], i32)
            record = sb(ph, "record", [P, C, 4], fp32)
            rank = sb(ph, "rank", [P, C], fp32)
            rank_i = sb(ph, "rank_i", [P, C], i32)

            with ExitStack() as st, nc.Block() as block:
                ps = banks(st, "edges", 5)
                cleared = sem(st, "cleared")
                loaded = sem(st, "loaded")
                cast = sem(st, "cast")
                turned = sem(st, "turned")
                stored = sem(st, "stored")
                looked = sem(st, "looked")
                spread = sem(st, "spread")
                last_made = sem(st, "last_made")
                sv = sem(st, "dve_chain")
                counted = sem(st, "counted")

                @block.sync
                def _(sp):
                    sp.wait_ge(cleared, 3)
                    full = E // P
                    for what, tile in (("src", rows_i[:, 0, :]), ("dst", rows_i[:, 1, :]), ("edge_weight", rows_w[:, :])):
                        for b in range(QB):
                            n = min(Q, full - b * Q)
                            sp.dma_start(tile[0:n, b * P:(b + 1) * P],
                                         a[what][b * Q * P:(b * Q + n) * P].rearrange("(q p) -> q p", p=P)).then_inc(loaded, 16)
                        r = full - (QB - 1) * Q
                        sp.dma_start(tile[r:r + 1, (QB - 1) * P:(QB - 1) * P + E - full * P],
                                     a[what][full * P:E].rearrange("(o p) -> o p", o=1)).then_inc(loaded, 16)
                    sp.wait_ge(cast, 2)
                    sp.dma_start(dst_padded.rearrange("(b q p) -> q b p", b=QB, p=P),
                                 rows_f[:, 1, :].rearrange("q (b p) -> q b p", p=P)).then_inc(stored, 16)
                    for w in range(2):
                        sp.dma_start(low_rows[w, :].rearrange("(b q p) -> q b p", b=QB, p=P),
                                     rows_lo8[:, w, :].rearrange("q (b p) -> q b p", p=P)).then_inc(stored, 16)
                    sp.wait_ge(stored, 48)
                    with nc.allow_non_contiguous_dma(reason="one value per chunk"):
                        firsts = dst_padded.rearrange("(c p) -> p c", p=P)[0:1, :]
                        lasts = dst_padded.rearrange("(c p) -> p c", p=P)[P - 1:P, :]
                        for h in range(H):
                            sp.dma_start(chunk_first[h:h + 1, :], firsts).then_inc(looked, 16)
                            sp.dma_start(chunk_last[h:h + 1, :], lasts).then_inc(looked, 16)
                        for b in range(QB):
                            n = Q if b < QB - 1 else Q - 1
                            at = b * Q + 1
                            sp.dma_start(next_first[0:n, b:b + 1],
                                         dst_padded.rearrange("(c p) -> c p", p=P)[at:at + n, 0:1]).then_inc(looked, 16)

                @block.vector
                def _(dve):
                    v = Chain(dve, sv)
                    dve.memset(rows_i[:, :, :], PAD).then_inc(cleared, 1)
                    dve.memset(rows_w[:, :], 0.0).then_inc(cleared, 1)
                    dve.memset(next_first[:, :], -1.0).then_inc(cleared, 1)
                    v.step(dve.memset(reset_f[:, :], -BIG))
                    v.step(dve.memset(reset_b[:, :], -BIG))
                    v.step(dve.memset(join_f[:, :], -BIG))
                    v.step(dve.memset(join_b[:, :], -BIG))
                    v.step(dve.memset(record[:, :, 3], 0.0))
                    dve.wait_ge(loaded, 15 * 16)
                    v.link(dve.tensor_scalar(rows_lo[:, :, :], rows_i[:, :, :], P - 1, None, ALU.bitwise_and))
                    dve.tensor_copy(rows_lo8[:, :, :], rows_lo[:, :, :]).then_inc(cast, 1)
                    dve.tensor_copy(rows_f[:, :, :], rows_i[:, :, :]).then_inc(cast, 1)
                    dve.wait_ge(turned, 3)
                    v.step(dve.tensor_copy(edge[:, 0, :], ps[0][:, 0:C]))
                    v.step(dve.tensor_copy(edge[:, 1, :], ps[1][:, 0:C]))
                    v.link(dve.tensor_copy(edge_w[:, :], ps[2][:, 0:C]))
                    v.link(dve.tensor_copy(edge_i[:, :, :], edge[:, :, :]))
                    v.link(dve.tensor_scalar(hi_i[:, :, :], edge_i[:, :, :], 7, None, ALU.logical_shift_right))
                    v.link(dve.tensor_copy(hi_f[:, :, :], hi_i[:, :, :]))
                    for w in range(2):
                        for t in range(NT):
                            v.step(dve.tensor_scalar(hot_hi[w][:, t, :], hi_f[:, w, :], float(t), None, ALU.is_equal))
                    v.link(dve.tensor_copy(tile_d[:, 0:C], hi_i[0:1, 1, :]))
                    for w in range(2):
                        v.link(dve.tensor_reduce(counts[:, w, :], hot_hi[w][:, :, :], X, ALU.add))
                    dve.sem_inc(counted, 1)
                    v.step(dve.tensor_copy(gidx_d[:, 0:C], edge[:, 0, :]))
                    v.step(dve.tensor_copy(record[:, :, 0], edge[:, 1, :]))
                    v.step(dve.tensor_copy(record[:, :, 1], edge_w[:, :]))
                    v.step(dve.tensor_copy(record[:, :, 2], edge[:, 0, :]))
                    dve.wait_ge(spread, 1)
                    for w in range(2):
                        v.link(dve.tensor_tensor_scan(begins[:, w, :], ones[0:1, 0:NT], ps[3][0:1, w * NT:(w + 1) * NT], 0.0,
                                                      ALU.mult, ALU.add))
                    v.link(dve.tensor_copy(begins_i[:, :, :], begins[:, :, :]))
                    v.step(dve.tensor_scalar(begin_s[:, :], begins_i[:, 0, :], 7, None, ALU.logical_shift_right))
                    v.step(dve.tensor_scalar(begin_d[:, :], begins_i[:, 1, :], 7, None, ALU.logical_shift_right))
                    v.link(dve.tensor_copy(hi_rep[:, 1, :], ps[4][:, 0:C]))
                    v.step(dve.scalar_tensor_tensor(local_d[:, 0:C], hi_rep[:, 1, :], -float(P), edge[:, 1, :], ALU.mult, ALU.add))
                    rf = reset_f[:, :].rearrange("q (h r p) -> q h r p", h=H, p=P)
                    rb = reset_b[:, :].rearrange("q (h r p) -> q h r p", h=H, p=P)
                    d = rows_f[:, 1, :].rearrange("q (b p) -> q b p", p=P)
                    v.link(dve.tensor_tensor(rf[:, 0, :, 1:P], d[:, :, 1:P], d[:, :, 0:P - 1], ALU.is_equal))
                    v.step(dve.tensor_scalar(last_rows[:, :, 0:P - 1], rf[:, 0, :, 1:P], -1.0, 1.0, ALU.mult, ALU.add))
                    v.link(dve.tensor_scalar(rb[:, 0, :, 0:P - 1], rf[:, 0, :, 1:P], -1.0, BIG, ALU.add, ALU.mult))
                    v.link(dve.tensor_copy(rf[:, 0, :, 1:P], rb[:, 0, :, 0:P - 1]))
                    for h in range(1, H):
                        v.step(dve.tensor_copy(rf[:, h, :, :], rf[:, 0, :, :]))
                        v.step(dve.tensor_copy(rb[:, h, :, :], rb[:, 0, :, :]))
                    dve.wait_ge(looked, (2 * H + QB) * 16)
                    v.link(dve.tensor_tensor(last_rows[:, :, P - 1], d[:, :, P - 1], next_first[:, :], ALU.is_equal))
                    v.link(dve.tensor_scalar(last_rows[:, :, P - 1], last_rows[:, :, P - 1], -1.0, 1.0, ALU.mult, ALU.add))
                    dve.sem_inc(last_made, 1)
                    v.link(dve.tensor_tensor(join_f[:, 1:C], chunk_first[:, 1:C], chunk_last[:, 0:C - 1], ALU.is_equal))
                    v.link(dve.tensor_scalar(join_b[:, 0:C - 1], join_f[:, 1:C], -1.0, BIG, ALU.add, ALU.mult))
                    v.link(dve.tensor_copy(join_f[:, 1:C], join_b[:, 0:C - 1]))
                    v.link(dve.tensor_tensor(gate_f[:, :], chunk_first[:, :], chunk_last[:, :], ALU.is_equal))
                    v.link(dve.tensor_scalar(gate_b[:, :], gate_f[:, :], -1.0, BIG, ALU.add, ALU.mult))
                    v.link(dve.tensor_tensor(gate_f[:, :], gate_b[:, :], join_f[:, :], ALU.add))
                    v.link(dve.tensor_tensor(gate_b[:, :], gate_b[:, :], join_b[:, :], ALU.add))
                    dve.wait_ge(turned, 4)
                    v.link(dve.tensor_copy(is_last[:, :], ps[0][:, 0:C]))

                @block.tensor
                def _(pe):
                    pe.wait_ge(cast, 2)
                    for n, rows in enumerate((rows_f[:, 0, :], rows_f[:, 1, :], rows_w[:, :])):
                        for b in range(QB):
                            last = nc.tensor.transpose(ps[n][:, b * Q:(b + 1) * Q], rows[:, b * P:(b + 1) * P], ident[0:Q, 0:Q])
                        last.then_inc(turned, 1)
                    pe.wait_ge(counted, 1)
                    nc.tensor.matmul(ps[3][:, 0:2 * NT], ones[:, :], counts[:, :, :].rearrange("p w t -> p (w t)"), start=True, stop=True)
                    nc.tensor.matmul(ps[4][:, 0:C], row0[:, :], hi_f[:, 1, :], start=True, stop=True).then_inc(spread, 1)
                    pe.wait_ge(last_made, 1)
                    for b in range(QB):
                        last = nc.tensor.transpose(ps[0][:, b * Q:(b + 1) * Q], last_rows[:, b, :], ident[0:Q, 0:Q])
                    last.then_inc(turned, 1)

            with ExitStack() as st, nc.Block() as block:
                ps = banks(st, "place", 4)
                hot = sb(st, "hot", [P, NT, C], bf16)
                place = sb(st, "place", [P, NT, C], fp32)
                before = sb(st, "before", [P, P], bf16)
                ones_b = sb(st, "ones_b", [P, P], bf16)
                total = sb(st, "total", [P, 2, PW], fp32)
                hot_made = sem(st, "hot_made")
                const_made = sem(st, "const_made")
                summed = sem(st, "summed")
                sv = sem(st, "dve_chain")
                placed = sem(st, "placed")

                @block.gpsimd
                def _(pool):
                    pool.memset(ones_b[:, :], 1.0).then_inc(const_made, 1)
                    pool.memset(before[:, :], -1.0).then_inc(const_made, 1)
                    pool.wait_ge(const_made, 2)
                    pool.affine_select(out=before[:, :], in_=before[:, :], compare_op=ALU.is_ge, fill=0.0, base=0,
                                       pattern=[[-1, P]], channel_multiplier=1).then_inc(const_made, 1)

                @block.tensor
                def _(pe):
                    pe.wait_ge(const_made, 3)
                    pe.wait_ge(hot_made, 1)
                    flat = hot[:, :, :].rearrange("p t c -> p (t c)")
                    for n in range(PIECES):
                        if n >= 2:
                            pe.wait_ge(placed, n - 1)
                        piece = flat[:, n * PW:(n + 1) * PW]
                        nc.tensor.matmul(ps[n % 2][:, 0:PW], ones_b[:, :], piece, start=True, stop=True)
                        nc.tensor.matmul(ps[2 + n % 2][:, 0:PW], before[:, :], piece, start=True, stop=True).then_inc(summed, 1)

                @block.vector
                def _(dve):
                    v = Chain(dve, sv)
                    dve.tensor_copy(hot[:, :, :], hot_hi[0][:, :, :]).then_inc(hot_made, 1)
                    flat = place[:, :, :].rearrange("p t c -> p (t c)")
                    for n in range(PIECES):
                        dve.wait_ge(summed, n + 1)
                        start = 0.0 if n == 0 else total[:, (n - 1) % 2, PW - 1:PW]
                        v.link(dve.tensor_tensor_scan(total[:, n % 2, :], ones[:, 0:1].broadcast_to([P, PW]), ps[n % 2][:, 0:PW], start,
                                                      ALU.mult, ALU.add))
                        v.step(dve.tensor_tensor(flat[:, n * PW:(n + 1) * PW], total[:, n % 2, :], ps[2 + n % 2][:, 0:PW], ALU.add))
                        dve.wait_ge(sv, v.n)
                        dve.sem_inc(placed, 1)
                    v.link(dve.tensor_tensor(place[:, :, :], place[:, :, :], hot[:, :, :], ALU.mult))
                    v.link(dve.tensor_reduce(rank[:, :], place[:, :, :].rearrange("p t c -> p c t"), X, ALU.add))
                    v.link(dve.tensor_copy(rank_i[:, :], rank[:, :]))

            with ExitStack() as st, nc.Block() as block:
                r_slot = sb(st, "r_slot", [P, U, 4], fp32)
                i_slot = sb(st, "i_slot", [P, U], i32)
                staged = sem(st, "staged")

                @block.scalar
                def _(act):
                    def stage(s, c):
                        act.activation(i_slot[:, s:s + 1], rank_i[:, bass.ds(c, 1)], ACT.Copy).then_inc(staged, 1)
                        act.activation(r_slot[:, s:s + 1, :], record[:, bass.ds(c, 1), :], ACT.Copy).then_inc(staged, 1)

                    for s in range(U):
                        stage(s, s)
                    with act.Fori(1, C // U) as i:
                        for s in range(U):
                            act.wait_ge(slot_done[s], 16 * i)
                            stage(s, U * i + s)

                @block.gpsimd
                def _(pool):
                    with pool.Fori(0, C // U) as i:
                        for s in range(U):
                            pool.wait_ge(staged, 2 * U * i + 2 * s + 2)
                            pool.nop(nofuse=True)
                            pool.indirect_dma_start(out=records, out_offset=bass.IndirectOffsetOnAxis(ap=i_slot[:, s:s + 1], axis=0),
                                                    in_=r_slot[:, s, :], in_offset=None).then_inc(slot_done[s], 16)
                    for s in range(U):
                        pool.wait_ge(slot_done[s], 16 * (C // U))

            slots_used[0] += C // U
            with ExitStack() as st, nc.Block() as block:
                ps = banks(st, "back", 4)
                rec_rows = sb(st, "rec_rows", [Q, QB, P, 4], fp32)
                near = sb(st, "near", [P, 2, NT], fp32)
                back = sem(st, "back")
                turned = sem(st, "turned")
                hi_made = sem(st, "hi_made")
                spread = sem(st, "spread")
                sv = sem(st, "dve_chain")

                @block.sync
                def _(sp):
                    sp.dma_start(rec_rows[:, :, :, :].rearrange("q b p k -> q b (p k)"),
                                 records.rearrange("(b q p) k -> q b (p k)", b=QB, p=P)).then_inc(back, 16)

                @block.tensor
                def _(pe):
                    pe.wait_ge(back, 16)
                    for k in range(3):
                        for b in range(QB):
                            last = nc.tensor.transpose(ps[k][:, b * Q:(b + 1) * Q], rec_rows[:, b, :, k], ident[0:Q, 0:Q])
                    last.then_inc(turned, 1)
                    pe.wait_ge(hi_made, 1)
                    nc.tensor.matmul(ps[3][:, 0:C], row0[:, :], hi_f[:, 0, :], start=True, stop=True).then_inc(spread, 1)

                @block.vector
                def _(dve):
                    v = Chain(dve, sv)
                    dve.wait_ge(turned, 1)
                    v.step(dve.tensor_copy(gidx_s[:, 0:C], ps[0][:, 0:C]))
                    v.step(dve.tensor_copy(w_s[:, 0:C], ps[1][:, 0:C]))
                    v.step(dve.tensor_copy(edge[:, 0, :], ps[2][:, 0:C]))
                    v.link(dve.tensor_copy(edge_i[:, 0, :], ps[2][:, 0:C]))
                    v.link(dve.tensor_scalar(hi_i[:, 0, :], edge_i[:, 0, :], 7, None, ALU.logical_shift_right))
                    v.link(dve.tensor_copy(hi_f[:, 0, :], hi_i[:, 0, :]))
                    dve.sem_inc(hi_made, 1)
                    v.step(dve.tensor_copy(tile_s[:, 0:C], hi_i[0:1, 0, :]))
                    dve.wait_ge(spread, 1)
                    v.link(dve.tensor_copy(hi_rep[:, 0, :], ps[3][:, 0:C]))
                    v.link(dve.scalar_tensor_tensor(local_s[:, 0:C], hi_rep[:, 0, :], -float(P), edge[:, 0, :], ALU.mult, ALU.add))
                    for col in (gidx_d, gidx_s, w_s):
                        v.step(dve.memset(col[:, C:CX], 0.0))
                    for col in (local_d, local_s):
                        v.step(dve.memset(col[:, C:CX], -1.0))
                    for col in (tile_d, tile_s):
                        v.step(dve.memset(col[:, C:CX], 0))
                    dve.wait_ge(sv, v.n)
                    for t in range(NT - 1):
                        for begin, w, pairs in ((begin_d, 1, ((gidx_d, gidx_d), (local_d, edge[:, 1, :]))),
                                                (begin_s, 0, ((gidx_s, gidx_s), (w_s, w_s), (local_s, edge[:, 0, :])))):
                            c = dve.value_load(begin[0:1, t:t + 1], min_val=0, max_val=C - 1)
                            for to, of in pairs:
                                v.step(dve.tensor_copy(to[:, C + t:C + t + 1], of[:, bass.ds(c, 1)]))
                            v.step(dve.tensor_copy(near[:, w, t:t + 1], hi_rep[:, w, bass.ds(c, 1)]))
                        v.step(dve.memset(tile_d[:, C + t:C + t + 1], t + 1))
                        v.step(dve.memset(tile_s[:, C + t:C + t + 1], t + 1))
                    dve.wait_ge(sv, v.n)
                    own = sb(st, "own", [P, NT - 1], fp32)
                    off = sb(st, "off", [P, NT - 1], fp32)
                    for t in range(NT - 1):
                        v.step(dve.memset(off[:, t:t + 1], float(P * (t + 1))))
                    dve.wait_ge(sv, v.n)
                    for w, col in ((0, local_s), (1, local_d)):
                        v.link(dve.tensor_scalar(own[:, :], near[:, w, 0:NT - 1], float(P), None, ALU.mult))
                        v.link(dve.tensor_tensor(own[:, :], own[:, :], off[:, :], ALU.is_equal))
                        v.link(dve.scalar_tensor_tensor(own[:, :], own[:, :], -2.0 * NP, off[:, :], ALU.mult, ALU.subtract))
                        v.link(dve.tensor_tensor(col[:, C:C + NT - 1], col[:, C:C + NT - 1], own[:, :], ALU.add))

        x_sb = sb(top, "x_sb", [P, NT, F], fp32)
        h_sb = sb(top, "h_sb", [P, NT, F], fp32)
        alphas = sb(top, "alphas", [P, NT, 2 * H], fp32)
        W_sb = sb(top, "W_sb", [P, K2, WMAX], fp32)
        norm = sb(top, "norm", [P, NT], fp32)
        with ExitStack() as ph, nc.Block() as block:
            loaded = sem(ph, "loaded")
            zeroed = sem(ph, "zeroed")

            @block.vector
            def _(dve):
                dve.memset(x_sb[:, NT - 1, :], 0.0).then_inc(zeroed, 1)
                dve.memset(norm[:, :], 0.0).then_inc(zeroed, 1)

            @block.sync
            def _(sp):
                sp.wait_ge(zeroed, 2)
                sp.dma_start(x_sb[:, 0:NT - 1, :], a["x"][0:(NT - 1) * P, :].rearrange("(t p) f -> p t f", p=P)).then_inc(loaded, 16)
                sp.dma_start(x_sb[0:LAST, NT - 1, :], a["x"][(NT - 1) * P:N, :]).then_inc(loaded, 16)
                with nc.allow_non_contiguous_dma(reason="one value per node"):
                    sp.dma_start(norm[:, 0:NT - 1], a["node_vec1"][0:(NT - 1) * P, :].rearrange("(t p) o -> p (t o)", p=P)).then_inc(loaded, 16)
                    sp.dma_start(norm[0:LAST, NT - 1:NT], a["node_vec1"][(NT - 1) * P:N, :]).then_inc(loaded, 16)
                sp.wait_ge(loaded, 64)

        def layer_norm(f_all):
            with ExitStack() as st, nc.Block() as block:
                stats = sb(st, "stats", [P, NT, 6], fp32)
                mv = sb(st, "mv", [P, NT, 2], fp32)
                var = sb(st, "var", [P, NT], fp32)
                dev = sb(st, "dev", [P, NT], fp32)
                rstd = sb(st, "rstd", [P, NT], fp32)
                shift = sb(st, "shift", [P, NT], fp32)
                var_made = sem(st, "var_made")
                dev_made = sem(st, "dev_made")
                scale_made = sem(st, "scale_made")
                sv = sem(st, "dve_chain")

                @block.vector
                def _(dve):
                    v = Chain(dve, sv)
                    for t in range(NT):
                        v.step(dve.bn_stats(stats[:, t, :], x_sb[:, t, :]))
                    dve.wait_ge(sv, v.n)
                    for t in range(NT):
                        v.step(dve.bn_aggr(mv[:, t, :], stats[:, t, :]))
                    dve.wait_ge(sv, v.n)
                    dve.tensor_scalar(var[:, :], mv[:, :, 1], EPS_LN, None, ALU.add).then_inc(var_made, 1)
                    dve.wait_ge(dev_made, 1)
                    v.link(dve.reciprocal(rstd[:, :], dev[:, :]))
                    dve.scalar_tensor_tensor(shift[:, :], mv[:, :, 0], -1.0, rstd[:, :], ALU.mult, ALU.mult).then_inc(scale_made, 1)

                @block.scalar
                def _(act):
                    act.wait_ge(var_made, 1)
                    act.activation(dev[:, :], var[:, :], ACT.Sqrt).then_inc(dev_made, 1)
                    act.wait_ge(scale_made, 1)
                    for t in range(NT):
                        act.activation(f_all[:, t, :], x_sb[:, t, :], ACT.Relu, bias=shift[:, t:t + 1], scale=rstd[:, t:t + 1])

        def load_weights(parts, attention=None, nh=0):
            with ExitStack() as st, nc.Block() as block:
                vec = sb(st, "vec", [P, 2, F], fp32)
                prod = sb(st, "prod", [P, F], fp32)
                loaded = sem(st, "loaded")
                sv = sem(st, "dve_chain")

                @block.sync
                def _(sp):
                    for n, w in enumerate(parts):
                        sp.dma_start(W_sb[:, :, n * F:(n + 1) * F], w.rearrange("(k p) f -> p k f", p=P)).then_inc(loaded, 16)
                    for n, vector in enumerate(attention or ()):
                        sp.dma_start(vec[:, n, :], row_broadcast(vector.rearrange("h c -> (h c)"))).then_inc(loaded, 16)
                    sp.wait_ge(loaded, 16 * (len(parts) + len(attention or ())))

                @block.vector
                def _(dve):
                    v = Chain(dve, sv)
                    if attention:
                        dve.wait_ge(loaded, 48)
                        for k in range(K2):
                            for n in range(2):
                                v.link(dve.tensor_tensor(prod[:, :], W_sb[:, k, 0:F], vec[:, n, :], ALU.mult))
                                v.link(dve.tensor_reduce(W_sb[:, k, F + n * nh:F + (n + 1) * nh],
                                                         prod[:, :].rearrange("p (h c) -> p h c", h=nh), X, ALU.add))

        def project(f_all, cols, put, n_puts, table, table_src, scale=None):
            with ExitStack() as st, nc.Block() as block:
                ps_t = banks(st, "turn", 2)
                ps_h = banks(st, "prod", 2)
                f_t = sb(st, "f_t", [P, 2, F], fp32)
                turned = sem(st, "turned")
                f_ready = sem(st, "f_ready")
                product = sem(st, "product")
                taken = sem(st, "taken")
                stored = sem(st, "stored")

                @block.tensor
                def _(pe):
                    def turn(t):
                        if t >= 2:
                            pe.wait_ge(f_ready, t - 1)
                        for k in range(K2):
                            last = nc.tensor.transpose(ps_t[t % 2][:, k * P:(k + 1) * P], f_all[:, t, k * P:(k + 1) * P], ident[:, :])
                        last.then_inc(turned, 1)

                    turn(0)
                    for t in range(NT):
                        if t + 1 < NT:
                            turn(t + 1)
                        pe.wait_ge(f_ready, t + 1)
                        if t >= 2:
                            pe.wait_ge(taken, n_puts * (t - 1))
                        for k in range(K2):
                            last = nc.tensor.matmul(ps_h[t % 2][:, 0:cols], f_t[:, t % 2, k * P:(k + 1) * P], W_sb[:, k, 0:cols],
                                                    start=(k == 0), stop=(k == K2 - 1))
                        last.then_inc(product, 1)

                @block.vector
                def _(dve):
                    for t in range(NT):
                        dve.wait_ge(turned, t + 1)
                        if t >= 2:
                            dve.wait_ge(product, t - 1)
                        dve.tensor_copy(f_t[:, t % 2, :], ps_t[t % 2][:, 0:F]).then_inc(f_ready, 1)

                @block.scalar
                def _(act):
                    for t in range(NT):
                        act.wait_ge(product, t + 1)
                        put(act, t, ps_h[t % 2], taken)

                if table is not None:
                    @block.sync
                    def _(sp):
                        step = 5
                        for t in range(0, NT, step):
                            sp.wait_ge(taken, n_puts * (t + step))
                            sp.dma_start(table[t * P:(t + step) * P, :].rearrange("(t p) f -> p t f", p=P),
                                         table_src[:, t:t + step, :]).then_inc(stored, 16)
                        sp.wait_ge(stored, 16 * (NT // step))

        def look_up(which, nh, found):
            W = NT * nh
            G = 4
            with ExitStack() as st, nc.Block() as block:
                low = sb(st, "low", [P, EP], u8)
                parts = sb(st, "parts", [P, 3, NT, nh], bf16)
                rest = sb(st, "rest", [P, 2, NT, nh], fp32)
                hot = sb(st, "hot", [P, 2, G * P], bf16)
                picked = sb(st, "picked", [P, 2, G, nh, NT], fp32)
                ps = banks(st, "ps", 2)
                low_in = sem(st, "low_in")
                hot_made = sem(st, "hot_made")
                product = sem(st, "product")
                sv = sem(st, "dve_chain")

                @block.sync
                def _(sp):
                    sp.dma_start(low[:, :], row_broadcast(low_rows[which, :])).then_inc(low_in, 16)

                @block.vector
                def _(dve):
                    v = Chain(dve, sv)
                    tab = alphas[:, :, which * nh:(which + 1) * nh]
                    v.link(dve.tensor_copy(parts[:, 0, :, :], tab))
                    v.link(dve.tensor_tensor(rest[:, 0, :, :], tab, parts[:, 0, :, :], ALU.subtract))
                    v.link(dve.tensor_copy(parts[:, 1, :, :], rest[:, 0, :, :]))
                    v.link(dve.tensor_tensor(rest[:, 1, :, :], rest[:, 0, :, :], parts[:, 1, :, :], ALU.subtract))
                    v.link(dve.tensor_copy(parts[:, 2, :, :], rest[:, 1, :, :]))
                    dve.wait_ge(low_in, 16)
                    base = v.n
                    with dve.Fori(0, C // (2 * G)) as i:
                        v.n = base + 4 * i
                        for u in range(2):
                            dve.tensor_scalar(hot[:, u, :], low[:, bass.ds((2 * i + u) * G * P, G * P)], part[:, 0:1], None,
                                              ALU.is_equal).then_inc(hot_made, 1)
                        for u in range(2):
                            dve.wait_ge(product, 2 * i + u + 1)
                            v.step(dve.tensor_tensor(
                                picked[:, u, :, :, :].rearrange("p c h t -> p c t h"),
                                ps[u][:, 0:G * W].rearrange("p (c t h) -> p c t h", c=G, h=nh),
                                hot_hi[which][:, :, bass.ds((2 * i + u) * G, G)].rearrange("p t c -> p c t").unsqueeze(3).broadcast_to([P, G, NT, nh]),
                                ALU.mult))
                        dve.wait_ge(sv, v.n)
                        for u in range(2):
                            v.step(dve.tensor_reduce(found[:, bass.ds((2 * i + u) * G, G), 0:nh], picked[:, u, :, :, :], X, ALU.add))
                        dve.wait_ge(sv, v.n)

                @block.tensor
                def _(pe):
                    with pe.Fori(0, C // (2 * G)) as i:
                        for u in range(2):
                            pe.wait_ge(hot_made, 2 * i + u + 1)
                            for g in range(G):
                                for k in range(3):
                                    last = nc.tensor.matmul(ps[u][:, g * W:(g + 1) * W], hot[:, u, g * P:(g + 1) * P],
                                                            parts[:, k, :, :].rearrange("p t h -> p (t h)"), start=(k == 0), stop=(k == 2))
                            last.then_inc(product, 1)

        def edge_softmax(nh, at_src, at_dst):
            L = nh * QB * P
            with ExitStack() as st, nc.Block() as block:
                ps = banks(st, "ps", 8)
                rows = sb(st, "rows", [Q, H * QB * P], fp32)
                run_f = sb(st, "run_f", [Q, H * QB * P], fp32)
                run_b = sb(st, "run_b", [Q, H * QB * P], fp32)
                ends = sb(st, "ends", [H, 2, C], fp32)
                carry = sb(st, "carry", [H, 2, C], fp32)
                top_src = sb(st, "top_src", [P, C, H], fp32)
                turned = sem(st, "turned")
                ran = sem(st, "ran")
                carried = sem(st, "carried")
                ready = sem(st, "ready")
                exped = sem(st, "exped")
                sv = sem(st, "dve_chain")

                def rows_v(tile):
                    return tile[:, 0:L].rearrange("q (h b p) -> q h b p", h=nh, p=P)

                @block.tensor
                def _(pe):
                    for h in range(nh):
                        for b in range(QB):
                            last = nc.tensor.transpose(ps[h][0:Q, b * P:(b + 1) * P], at_src[:, b * Q:(b + 1) * Q, h], ident[:, :])
                    last.then_inc(turned, 1)
                    pe.wait_ge(ran, 1)
                    for n, (tile, p) in enumerate(((run_f, P - 1), (run_b, 0))):
                        for b in range(QB):
                            last = nc.tensor.transpose(ps[4 + n][0:nh, b * Q:(b + 1) * Q], rows_v(tile)[:, :, b, p], ident[0:Q, 0:Q])
                    last.then_inc(turned, 1)
                    pe.wait_ge(carried, 1)
                    for n in range(2):
                        for b in range(QB):
                            last = nc.tensor.transpose(ps[6 + n][0:Q, b * nh:(b + 1) * nh], carry[0:nh, n, b * Q:(b + 1) * Q],
                                                       ident[0:nh, 0:nh])
                    last.then_inc(turned, 1)
                    pe.wait_ge(ran, 2)
                    for h in range(nh):
                        for b in range(QB):
                            last = nc.tensor.transpose(ps[h][:, b * Q:(b + 1) * Q], rows_v(run_f)[:, h, b, :], ident[0:Q, 0:Q])
                    last.then_inc(turned, 1)

                @block.vector
                def _(dve):
                    v = Chain(dve, sv)

                    def runs():
                        v.step(dve.tensor_tensor_scan(run_f[:, 0:L], reset_f[:, 0:L], rows[:, 0:L], -BIG, ALU.add, ALU.max))
                        v.link(dve.tensor_tensor_scan(run_b[:, 0:L][:, ::-1], reset_b[:, 0:L][:, ::-1], rows[:, 0:L][:, ::-1], -BIG,
                                                      ALU.add, ALU.max))

                    dve.wait_ge(turned, 1)
                    for h in range(nh):
                        v.step(dve.tensor_copy(rows[:, h * QB * P:(h + 1) * QB * P], ps[h][0:Q, 0:QB * P]))
                    dve.wait_ge(sv, v.n)
                    runs()
                    dve.sem_inc(ran, 1)
                    dve.wait_ge(turned, 2)
                    v.link(dve.tensor_tensor_scan(ends[0:nh, 0, :], gate_f[0:nh, :], ps[4][0:nh, 0:C], -BIG, ALU.add, ALU.max))
                    v.link(dve.tensor_tensor_scan(ends[0:nh, 1, ::-1], gate_b[0:nh, ::-1], ps[5][0:nh, 0:C][:, ::-1], -BIG, ALU.add, ALU.max))
                    v.step(dve.tensor_tensor(carry[0:nh, 0, 1:C], ends[0:nh, 0, 0:C - 1], join_f[0:nh, 1:C], ALU.add))
                    v.step(dve.memset(carry[0:nh, 0, 0:1], -BIG))
                    v.step(dve.tensor_tensor(carry[0:nh, 1, 0:C - 1], ends[0:nh, 1, 1:C], join_b[0:nh, 0:C - 1], ALU.add))
                    v.link(dve.memset(carry[0:nh, 1, C - 1:C], -BIG))
                    dve.sem_inc(carried, 1)
                    dve.wait_ge(turned, 3)
                    for n, p in ((0, 0), (1, P - 1)):
                        v.link(dve.tensor_tensor(rows_v(rows)[:, :, :, p], rows_v(rows)[:, :, :, p],
                                                 ps[6 + n][0:Q, 0:QB * nh].rearrange("q (b h) -> q h b", h=nh), ALU.max))
                    runs()
                    v.link(dve.tensor_tensor(run_f[:, 0:L], run_f[:, 0:L], run_b[:, 0:L], ALU.max))
                    dve.sem_inc(ran, 1)
                    dve.wait_ge(turned, 4)
                    for h in range(nh):
                        v.step(dve.tensor_copy(top_src[:, :, h], ps[h][:, 0:C]))
                    dve.wait_ge(sv, v.n)
                    s, d, m = at_src[:, :, 0:nh], at_dst[:, :, 0:nh], top_src[:, :, 0:nh]
                    v.step(dve.tensor_tensor(edge_aux[:, 0:C, nh:2 * nh], m, is_last[:, :].unsqueeze(2).broadcast_to([P, C, nh]), ALU.mult))
                    v.step(dve.tensor_copy(edge_aux[:, 0:C, 2 * nh], is_last[:, :]))
                    v.step(dve.memset(edge_aux[:, C:CX, :], 0.0))
                    v.link(dve.tensor_tensor(s, s, d, ALU.add))
                    v.link(dve.scalar_tensor_tensor(s, s, NEG_SLOPE, s, ALU.mult, ALU.max))
                    v.link(dve.tensor_tensor(d, m, d, ALU.add))
                    v.link(dve.scalar_tensor_tensor(d, d, NEG_SLOPE, d, ALU.mult, ALU.max))
                    v.link(dve.tensor_tensor(s, s, d, ALU.subtract))
                    dve.sem_inc(ready, 1)
                    dve.wait_ge(exped, 1)
                    for t in range(NT - 1):
                        c = dve.value_load(begin_d[0:1, t:t + 1], min_val=0, max_val=C - 1)
                        v.step(dve.tensor_copy(edge_aux[:, C + t:C + t + 1, :], edge_aux[:, bass.ds(c, 1), :]))
                    dve.wait_ge(sv, v.n)

                @block.scalar
                def _(act):
                    act.wait_ge(ready, 1)
                    act.activation(edge_aux[:, 0:C, 0:nh], at_src[:, :, 0:nh], ACT.Exp).then_inc(exped, 1)

        def aggregate(acc, table, index, local, tiles, weight=None, nh=0, aux=None, n_aux=0):
            W = F + n_aux
            with ExitStack() as st, nc.Block() as block:
                ps = banks(st, "ps", U)
                rows = sb(st, "rows", [P, U, F], fp32)
                msg = sb(st, "msg", [P, U, F], fp32)
                hot = sb(st, "hot", [P, U, P], fp32)
                i_slot = sb(st, "i_slot", [P, U], i32)
                row_in, base = slot_done, 16 * slots_used[0]
                slots_used[0] += CX // U
                staged = sem(st, "staged")
                row_free = sem(st, "row_free")
                msg_made = sem(st, "msg_made")
                product = sem(st, "product")
                added = sem(st, "added")
                sv = sem(st, "dve_chain")
                weighted = weight is not None or nh > 0
                iters = CX // U

                @block.scalar
                def _(act):
                    with act.Fori(0, iters) as i:
                        for s in range(U):
                            act.wait_ge(row_free, U * i + s + 1)
                            act.activation(i_slot[:, s:s + 1], index[:, bass.ds(U * i + s, 1)], ACT.Copy).then_inc(staged, 1)

                @block.gpsimd
                def _(pool):
                    with pool.Fori(0, iters) as i:
                        for s in range(U):
                            pool.wait_ge(staged, U * i + s + 1)
                            pool.nop(nofuse=True)
                            pool.indirect_dma_start(out=rows[:, s, :], out_offset=None, in_=table,
                                                    in_offset=bass.IndirectOffsetOnAxis(ap=i_slot[:, s:s + 1], axis=0)).then_inc(row_in[s], 16)

                @block.vector
                def _(dve):
                    dve.memset(acc[:, :, :], 0.0).then_inc(added, U)
                    dve.wait_ge(added, U)
                    dve.sem_inc(row_free, U)
                    with dve.Fori(0, iters) as i:
                        for s in range(U):
                            c = U * i + s
                            dve.tensor_scalar(hot[:, s, :], iota[:, :], local[:, bass.ds(c, 1)], None, ALU.is_equal).then_inc(sv, 1)
                            if weighted:
                                dve.wait_ge(row_in[s], base + 16 * i + 16)
                                if nh > 1:
                                    m = dve.tensor_tensor(msg[:, s, :].rearrange("p (h c) -> p h c", h=nh),
                                                          rows[:, s, :].rearrange("p (h c) -> p h c", h=nh),
                                                          aux[:, bass.ds(c, 1), 0:nh].rearrange("p o h -> p h o").broadcast_to([P, nh, CH]), ALU.mult)
                                elif nh == 1:
                                    m = dve.tensor_scalar(msg[:, s, :], rows[:, s, :], aux[:, bass.ds(c, 1), 0:1].rearrange("p o h -> p (o h)"), None, ALU.mult)
                                else:
                                    m = dve.tensor_scalar(msg[:, s, :], rows[:, s, :], weight[:, bass.ds(c, 1)], None, ALU.mult)
                                m.then_inc(msg_made, 1)
                                dve.wait_ge(msg_made, c + 1)
                                dve.sem_inc(row_free, 1)
                        for s in range(U):
                            c = U * i + s
                            t = dve.value_load(tiles[0:1, bass.ds(c, 1)], min_val=0, max_val=NT - 1)
                            dve.wait_ge(product, c + 1)
                            dve.wait_ge(added, c + U)
                            dve.tensor_tensor(acc[:, bass.ds(t, 1), 0:W], acc[:, bass.ds(t, 1), 0:W], ps[s][:, 0:W].unsqueeze(1), ALU.add).then_inc(added, 1)
                            if not weighted:
                                dve.sem_inc(row_free, 1)
                        dve.wait_ge(added, U * i + 2 * U)

                @block.tensor
                def _(pe):
                    with pe.Fori(0, iters) as i:
                        for s in range(U):
                            c = U * i + s
                            pe.wait_ge(sv, c + 1)
                            if weighted:
                                pe.wait_ge(msg_made, c + 1)
                            else:
                                pe.wait_ge(row_in[s], base + 16 * i + 16)
                            pe.wait_ge(added, c + 1)
                            src = msg if weighted else rows
                            last = nc.tensor.matmul(ps[s][:, 0:F], hot[:, s, :], src[:, s, :], start=True, stop=True)
                            if n_aux:
                                rhs = ones[:, 0:1] if aux is None else aux[:, bass.ds(c, 1), 0:n_aux].rearrange("p o k -> p (o k)")
                                last = nc.tensor.matmul(ps[s][:, F:F + n_aux], hot[:, s, :], rhs, start=True, stop=True)
                            last.then_inc(product, 1)

        def gat_combine(acc, nh, bias, finish, temps):
            ch = F // nh
            with ExitStack() as st, nc.Block() as block:
                vec = sb(st, "vec", [P, F], fp32)
                small = sb(st, "small", [P, 6, NT, nh], fp32)
                loaded = sem(st, "loaded")
                ready = sem(st, "ready")
                exped = sem(st, "exped")
                sv = sem(st, "dve_chain")
                finish_sem = sem(st, "finish")

                @block.sync
                def _(sp):
                    sp.dma_start(vec[:, :], row_broadcast(bias)).then_inc(loaded, 16)

                @block.scalar
                def _(act):
                    act.wait_ge(ready, 1)
                    act.activation(small[:, 0:2, :, :], small[:, 0:2, :, :], ACT.Exp).then_inc(exped, 1)
                    finish(None, act, None, None, finish_sem)

                @block.vector
                def _(dve):
                    v = Chain(dve, sv)
                    edge_max, self_max, both, den, own, tmp = (small[:, k, :, :] for k in range(6))
                    a_s, a_d = alphas[:, :, 0:nh], alphas[:, :, nh:2 * nh]
                    any_edge = acc[:, :, F + 2 * nh:F + 2 * nh + 1].broadcast_to([P, NT, nh])
                    v.step(dve.tensor_tensor(self_max, a_s, a_d, ALU.add))
                    v.link(dve.tensor_tensor(edge_max, acc[:, :, F + nh:F + 2 * nh], a_d, ALU.add))
                    v.step(dve.scalar_tensor_tensor(self_max, self_max, NEG_SLOPE, self_max, ALU.mult, ALU.max))
                    v.step(dve.scalar_tensor_tensor(edge_max, edge_max, NEG_SLOPE, edge_max, ALU.mult, ALU.max))
                    v.link(dve.tensor_scalar(tmp, any_edge, -1.0, BIG, ALU.add, ALU.mult))
                    v.link(dve.tensor_tensor(edge_max, edge_max, tmp, ALU.add))
                    v.link(dve.tensor_tensor(both, edge_max, self_max, ALU.max))
                    v.step(dve.tensor_tensor(edge_max, edge_max, both, ALU.subtract))
                    v.link(dve.tensor_tensor(self_max, self_max, both, ALU.subtract))
                    dve.sem_inc(ready, 1)
                    dve.wait_ge(exped, 1)
                    v.link(dve.tensor_tensor(den, acc[:, :, F:F + nh], edge_max, ALU.mult))
                    v.link(dve.tensor_tensor(den, den, self_max, ALU.add))
                    v.link(dve.tensor_scalar(den, den, EPS_DEN, None, ALU.add))
                    v.link(dve.reciprocal(own, den))
                    v.step(dve.tensor_tensor(edge_max, edge_max, own, ALU.mult))
                    v.link(dve.tensor_tensor(self_max, self_max, own, ALU.mult))
                    dve.wait_ge(loaded, 16)
                    work = temps
                    for t in range(NT):
                        accv = acc[:, t, 0:F].rearrange("p (h c) -> p h c", h=nh)
                        hv = h_sb[:, t, :].rearrange("p (h c) -> p h c", h=nh)
                        wv = work[:, t, :].rearrange("p (h c) -> p h c", h=nh)
                        v.step(dve.tensor_tensor(accv, accv, edge_max[:, t, :].unsqueeze(2).broadcast_to([P, nh, ch]), ALU.mult))
                        v.step(dve.tensor_tensor(wv, hv, self_max[:, t, :].unsqueeze(2).broadcast_to([P, nh, ch]), ALU.mult))
                    dve.wait_ge(sv, v.n)
                    v.link(dve.tensor_tensor(work[:, :, :], work[:, :, :], acc[:, :, 0:F], ALU.add))
                    v.link(dve.tensor_tensor(work[:, :, :], work[:, :, :], vec[:, :].unsqueeze(1).broadcast_to([P, NT, F]), ALU.add))
                    finish(v, None, dve, work, finish_sem)

        def put_h(act, t, bank, taken, nh=0, scale=None):
            if scale is None:
                act.activation(h_sb[:, t, :], bank[:, 0:F], ACT.Copy).then_inc(taken, 1)
            else:
                act.activation(h_sb[:, t, :], bank[:, 0:F], ACT.Copy, scale=scale[:, t:t + 1]).then_inc(taken, 1)
            if nh:
                act.activation(alphas[:, t, 0:2 * nh], bank[:, F:F + 2 * nh], ACT.Copy).then_inc(taken, 1)

        def attention_layer(table, nh, temps_scope, bias, finish):
            with ExitStack() as st:
                at_src = sb(st, "at_src", [P, C, nh], fp32)
                at_dst = sb(st, "at_dst", [P, C, nh], fp32)
                look_up(0, nh, at_src)
                look_up(1, nh, at_dst)
                edge_softmax(nh, at_src, at_dst)
            acc = sb(temps_scope, "acc", [P, NT, F + 2 * nh + 1], fp32)
            aggregate(acc, table, gidx_d, local_d, tile_d, nh=nh, aux=edge_aux, n_aux=2 * nh + 1)
            work = sb(temps_scope, "work", [P, NT, F], fp32)
            gat_combine(acc, nh, bias, finish, work)

        with ExitStack() as ls:
            load_weights([a["L0_gnn_weight"]])
            with ExitStack() as fs:
                f_all = sb(fs, "f_all", [P, NT, F], fp32)
                layer_norm(f_all)
                project(f_all, F, lambda act, t, bank, taken: put_h(act, t, bank, taken, scale=norm), 1, tables[0], h_sb)
            acc = sb(ls, "acc", [P, NT, F], fp32)
            aggregate(acc, tables[0], gidx_s, local_s, tile_s, weight=w_s)
            with ExitStack() as st, nc.Block() as block:
                vec = sb(st, "vec", [P, F], fp32)
                loaded = sem(st, "loaded")
                sv = sem(st, "dve_chain")

                @block.sync
                def _(sp):
                    sp.dma_start(vec[:, :], row_broadcast(a["L0_gnn_bias"])).then_inc(loaded, 16)

                @block.vector
                def _(dve):
                    v = Chain(dve, sv)
                    dve.wait_ge(loaded, 16)
                    v.link(dve.tensor_tensor(acc[:, :, :], acc[:, :, :], vec[:, :].unsqueeze(1).broadcast_to([P, NT, F]), ALU.add))
                    v.link(dve.scalar_tensor_tensor(x_sb[:, :, :], acc[:, :, :], 0.0, x_sb[:, :, :], ALU.max, ALU.add))

        with ExitStack() as ls:
            load_weights([a["L1_gnn_W1"]], (a["L1_gnn_att_src1"], a["L1_gnn_att_dst1"]), H)
            with ExitStack() as fs:
                f_all = sb(fs, "f_all", [P, NT, F], fp32)
                layer_norm(f_all)
                project(f_all, F + 2 * H, lambda act, t, bank, taken: put_h(act, t, bank, taken, nh=H), 2, tables[1], h_sb)

            def finish_elu(v, act, dve, work, done):
                if act is not None:
                    act.wait_ge(done, 1)
                    act.activation(h_sb[:, :, :], h_sb[:, :, :], ACT.Exp).then_inc(done, 1)
                else:
                    v.link(dve.tensor_scalar(h_sb[:, :, :], work[:, :, :], 0.0, None, ALU.min))
                    dve.sem_inc(done, 1)
                    v.link(dve.tensor_scalar(work[:, :, :], work[:, :, :], 0.0, -1.0, ALU.max, ALU.add))
                    dve.wait_ge(done, 2)
                    v.link(dve.tensor_tensor(h_sb[:, :, :], work[:, :, :], h_sb[:, :, :], ALU.add))

            with ExitStack() as ts:
                attention_layer(tables[1], H, ts, a["L1_gnn_b1"], finish_elu)

        with ExitStack() as ls:
            load_weights([a["L1_gnn_W2"]], (a["L1_gnn_att_src2"], a["L1_gnn_att_dst2"]), 1)
            with ExitStack() as fs:
                project(h_sb, F + 2, lambda act, t, bank, taken: put_h(act, t, bank, taken, nh=1), 2, tables[2], h_sb)

            def finish_add(v, act, dve, work, done):
                if dve is not None:
                    v.link(dve.tensor_tensor(x_sb[:, :, :], x_sb[:, :, :], work[:, :, :], ALU.add))

            with ExitStack() as ts:
                attention_layer(tables[2], 1, ts, a["L1_gnn_b2"], finish_add)

        with ExitStack() as ls:
            load_weights([a["L2_gnn_W_self"], a["L2_gnn_W_neigh"]])
            with ExitStack() as fs:
                neigh = sb(fs, "neigh", [P, NT, F], fp32)
                with ExitStack() as gs:
                    f_all = sb(gs, "f_all", [P, NT, F], fp32)
                    layer_norm(f_all)

                    def put_both(act, t, bank, taken):
                        act.activation(h_sb[:, t, :], bank[:, 0:F], ACT.Copy).then_inc(taken, 1)
                        act.activation(neigh[:, t, :], bank[:, F:2 * F], ACT.Copy).then_inc(taken, 1)

                    project(f_all, 2 * F, put_both, 2, None, None)
                with ExitStack() as st, nc.Block() as block:
                    best = sb(st, "best", [P, 2, 8], fp32)
                    left = sb(st, "left", [P, 2, F], fp32)
                    kept = sem(st, "kept")
                    stored = sem(st, "stored")
                    sv = sem(st, "dve_chain")

                    @block.vector
                    def _(dve):
                        v = Chain(dve, sv)
                        for t in range(NT):
                            for r in range(4):
                                of = neigh[:, t, :] if r == 0 else left[:, (r - 1) % 2, :]
                                v.link(dve.max(best[:, t % 2, :], of))
                                v.link(dve.match_replace(left[:, r % 2, :], best[:, t % 2, :], of, -BIG))
                            dve.scalar_tensor_tensor(neigh[:, t, :], left[:, 1, :], -BIG, neigh[:, t, :], ALU.is_le, ALU.mult).then_inc(kept, 1)

                    @block.sync
                    def _(sp):
                        for t in range(0, NT, 5):
                            sp.wait_ge(kept, t + 5)
                            sp.dma_start(tables[3][t * P:(t + 5) * P, :].rearrange("(t p) f -> p t f", p=P), neigh[:, t:t + 5, :]).then_inc(stored, 16)
                        sp.wait_ge(stored, 16 * (NT // 5))
            acc = sb(ls, "acc", [P, NT, F + 1], fp32)
            aggregate(acc, tables[3], gidx_d, local_d, tile_d, n_aux=1)
            with ExitStack() as st, nc.Block() as block:
                deg = sb(st, "deg", [P, NT], fp32)
                sv = sem(st, "dve_chain")

                @block.vector
                def _(dve):
                    v = Chain(dve, sv)
                    v.step(dve.tensor_tensor(x_sb[:, :, :], x_sb[:, :, :], h_sb[:, :, :], ALU.add))
                    v.link(dve.tensor_scalar(deg[:, :], acc[:, :, F], 1.0, None, ALU.max))
                    v.link(dve.reciprocal(deg[:, :], deg[:, :]))
                    for t in range(NT):
                        v.step(dve.scalar_tensor_tensor(x_sb[:, t, :], acc[:, t, 0:F], deg[:, t:t + 1], x_sb[:, t, :], ALU.mult, ALU.add))
                    dve.wait_ge(sv, v.n)

        with ExitStack() as ls:
            load_weights([a["L3_gnn_W"]], (a["L3_gnn_att_src"], a["L3_gnn_att_dst"]), H)
            with ExitStack() as fs:
                f_all = sb(fs, "f_all", [P, NT, F], fp32)
                layer_norm(f_all)
                project(f_all, F + 2 * H, lambda act, t, bank, taken: put_h(act, t, bank, taken, nh=H), 2, tables[4], h_sb)

            def finish_relu(v, act, dve, work, done):
                if dve is not None:
                    v.link(dve.scalar_tensor_tensor(x_sb[:, :, :], work[:, :, :], 0.0, x_sb[:, :, :], ALU.max, ALU.add))

            with ExitStack() as ts:
                attention_layer(tables[4], H, ts, a["L3_gnn_bias"], finish_relu)

        with ExitStack() as st, nc.Block() as block:
            stored = sem(st, "stored")

            @block.sync
            def _(sp):
                sp.dma_start(out[0:(NT - 1) * P, :].rearrange("(t p) f -> p t f", p=P), x_sb[:, 0:NT - 1, :]).then_inc(stored, 16)
                sp.dma_start(out[(NT - 1) * P:N, :], x_sb[0:LAST, NT - 1, :]).then_inc(stored, 16)
                sp.wait_ge(stored, 32)


_INS = ["x", "src", "dst", "edge_weight", "node_vec1", "L0_gnn_weight", "L0_gnn_bias", "L1_gnn_W1", "L1_gnn_att_src1",
        "L1_gnn_att_dst1", "L1_gnn_b1", "L1_gnn_W2", "L1_gnn_att_src2", "L1_gnn_att_dst2", "L1_gnn_b2", "L2_gnn_W_self",
        "L2_gnn_W_neigh", "L3_gnn_W", "L3_gnn_att_src", "L3_gnn_att_dst", "L3_gnn_bias"]


def kernel(**inputs):
    import concourse.bacc as bacc
    from concourse.bass_utils import run_bass_kernel_spmd

    nc = bacc.Bacc("TRN2", target_bir_lowering=False, num_devices=1)
    arrays, args = {}, {}
    for name in _INS:
        array = np.ascontiguousarray(inputs[name])
        arrays[f"in_{name}"] = array
        args[name] = nc.dram_tensor(f"in_{name}", array.shape, mybir.dt.from_np(array.dtype), kind="ExternalInput").ap()
    out = nc.dram_tensor("out_x", arrays["in_x"].shape, fp32, kind="ExternalOutput").ap()
    gnn_kernel(nc, args, out)
    r = run_bass_kernel_spmd(nc, [arrays], core_ids=[0])
    return r.results[0]["out_x"]
```

```python
import numpy as np
import concourse.bass as bass
from concourse import mybir
from contextlib import ExitStack

fp32 = mybir.dt.float32
bf16 = mybir.dt.bfloat16
i32 = mybir.dt.int32
u8 = mybir.dt.uint8
ALU = mybir.AluOpType
ACT = mybir.ActivationFunctionType
X = mybir.AxisListType.X

P = 128
BIG = 1e30
NEG_SLOPE = 0.2
EPS_LN = 1e-5
EPS_DEN = 1e-16


class Chain:

    def __init__(self, engine, sem):
        self.engine, self.sem, self.n = engine, sem, 0

    def step(self, instruction):
        instruction.then_inc(self.sem, 1)
        self.n = self.n + 1

    def link(self, instruction):
        self.step(instruction)
        self.engine.wait_ge(self.sem, self.n)


def gnn_kernel(nc, a, out):
    N, F = a["x"].shape
    E = a["src"].shape[0]
    K2 = F // P
    NT = -(-N // P)
    LAST = N - (NT - 1) * P
    NP = NT * P
    QB = 4
    U = 8
    C = -(-(E + 1) // (P * U)) * U
    Q = C // QB
    EP = C * P
    CX = C + NT - 1
    CX = -(-CX // U) * U
    PAD = NP - 1
    H = a["L1_gnn_att_src1"].shape[0]
    CH = F // H
    AUX = 2 * H + 1
    WX = F + 2 * H
    WMAX = 2 * F
    POS_N = NT * C
    PIECES = 20
    PW = POS_N // PIECES
    assert E % P and Q * QB == C and POS_N % PIECES == 0 and PW <= 512 and PAD >= N and C % U == 0

    tables = [nc.dram_tensor(f"table_{n}", (NP, F), fp32, kind="Internal").ap() for n in range(5)]
    records = nc.dram_tensor("records", (EP, 4), fp32, kind="Internal").ap()
    dst_padded = nc.dram_tensor("dst_padded", (EP,), fp32, kind="Internal").ap()
    low_rows = nc.dram_tensor("low_rows", (2, EP), u8, kind="Internal").ap()

    top = ExitStack()
    names = [0]

    def sb(stack, name, shape, dt):
        names[0] += 1
        return stack.enter_context(nc.sbuf_tensor(f"{name}_{names[0]}", shape, dt))

    def banks(stack, name, n):
        names[0] += 1
        return [stack.enter_context(nc.psum_tensor(f"{name}_{names[0]}_{i}", [P, 512], fp32)) for i in range(n)]

    def sem(stack, name):
        names[0] += 1
        s = stack.enter_context(nc.semaphore(f"{name}_{names[0]}"))
        stack.callback(lambda: nc.sync.sem_clear(s))
        return s

    with top:
        ident = sb(top, "ident", [P, P], fp32)
        iota = sb(top, "iota", [P, P], fp32)
        part = sb(top, "part", [P, 1], fp32)
        ones = sb(top, "ones", [P, P], fp32)
        row0 = sb(top, "row0", [P, P], fp32)
        hot_hi = [sb(top, f"hot_hi{w}", [P, NT, C], u8) for w in range(2)]
        gidx_d = sb(top, "gidx_d", [P, CX], fp32)
        gidx_s = sb(top, "gidx_s", [P, CX], fp32)
        local_d = sb(top, "local_d", [P, CX], fp32)
        local_s = sb(top, "local_s", [P, CX], fp32)
        w_s = sb(top, "w_s", [P, CX], fp32)
        tile_d = sb(top, "tile_d", [1, CX], i32)
        tile_s = sb(top, "tile_s", [1, CX], i32)
        begin_d = sb(top, "begin_d", [1, NT], i32)
        begin_s = sb(top, "begin_s", [1, NT], i32)
        is_last = sb(top, "is_last", [P, C], fp32)
        reset_f = sb(top, "reset_f", [Q, H * QB * P], fp32)
        reset_b = sb(top, "reset_b", [Q, H * QB * P], fp32)
        join_f = sb(top, "join_f", [H, C], fp32)
        join_b = sb(top, "join_b", [H, C], fp32)
        gate_f = sb(top, "gate_f", [H, C], fp32)
        gate_b = sb(top, "gate_b", [H, C], fp32)
        edge_aux = sb(top, "edge_aux", [P, CX, AUX], fp32)

        def row_broadcast(vec, rows=P):
            return vec.partition_broadcast(rows)

        slot_done = [top.enter_context(nc.semaphore(f"slot_done{s}")) for s in range(U)]
        slots_used = [0]
        sort_done = top.enter_context(nc.semaphore("sort_done"))

        with ExitStack() as ph, nc.Block() as block:
            made = sem(ph, "made")

            @block.gpsimd
            def _(pool):
                pool.iota(iota[:, :], [[1, P]], 0, 0, allow_small_or_imprecise_dtypes=True).then_inc(made, 1)
                pool.iota(part[:, :], [[0, 1]], 0, 1, allow_small_or_imprecise_dtypes=True).then_inc(made, 1)
                pool.memset(ident[:, :], 0.0).then_inc(made, 1)
                pool.memset(row0[:, :], 0.0).then_inc(made, 1)
                pool.memset(ones[:, :], 1.0).then_inc(made, 1)
                pool.wait_ge(made, 5)
                pool.affine_select(out=ident[:, :], in_=ident[:, :], compare_op=ALU.not_equal, fill=1.0, base=0,
                                   pattern=[[-1, P]], channel_multiplier=1).then_inc(made, 1)
                pool.memset(row0[0:1, :], 1.0).then_inc(made, 1)
                pool.wait_ge(made, 7)

        with ExitStack() as ph:
            rows_i = sb(ph, "rows_i", [Q, 2, QB * P], i32)
            rows_lo = sb(ph, "rows_lo", [Q, 2, QB * P], i32)
            rows_lo8 = sb(ph, "rows_lo8", [Q, 2, QB * P], u8)
            rows_f = sb(ph, "rows_f", [Q, 2, QB * P], fp32)
            rows_w = sb(ph, "rows_w", [Q, QB * P], fp32)
            edge = sb(ph, "edge", [P, 2, C], fp32)
            edge_w = sb(ph, "edge_w", [P, C], fp32)
            edge_i = sb(ph, "edge_i", [P, 2, C], i32)
            hi_i = sb(ph, "hi_i", [P, 2, C], i32)
            hi_f = sb(ph, "hi_f", [P, 2, C], fp32)
            hi_rep = sb(ph, "hi_rep", [P, 2, C], fp32)
            next_first = sb(ph, "next_first", [Q, QB], fp32)
            chunk_first = sb(ph, "chunk_first", [H, C], fp32)
            chunk_last = sb(ph, "chunk_last", [H, C], fp32)
            last_rows = sb(ph, "last_rows", [Q, QB, P], fp32)
            counts = sb(ph, "counts", [P, 2, NT], fp32)
            begins = sb(ph, "begins", [1, 2, NT], fp32)
            begins_i = sb(ph, "begins_i", [1, 2, NT], i32)
            record = sb(ph, "record", [P, C, 4], fp32)
            rank = sb(ph, "rank", [P, C], fp32)
            rank_i = sb(ph, "rank_i", [P, C], i32)

            unsorted = sb(ph, "unsorted", [1, 1], i32)
            with ExitStack() as st, nc.Block() as block:
                ps = banks(st, "load", 1)
                order = sb(st, "order", [Q, QB, P + 1], i32)
                falls = sb(st, "falls", [Q, QB, P], fp32)
                falls_row = sb(st, "falls_row", [Q, 1], fp32)
                cleared = sem(st, "cleared")
                loaded = sem(st, "loaded")
                counted = sem(st, "counted")
                summed = sem(st, "summed")
                sv = sem(st, "dve_chain")

                @block.sync
                def _(sp):
                    sp.wait_ge(cleared, 3)
                    full = E // P
                    for what, tile in (("src", rows_i[:, 0, :]), ("dst", rows_i[:, 1, :]), ("edge_weight", rows_w[:, :])):
                        for b in range(QB):
                            n = min(Q, full - b * Q)
                            sp.dma_start(tile[0:n, b * P:(b + 1) * P],
                                         a[what][b * Q * P:(b * Q + n) * P].rearrange("(q p) -> q p", p=P)).then_inc(loaded, 16)
                        r = full - (QB - 1) * Q
                        sp.dma_start(tile[r:r + 1, (QB - 1) * P:(QB - 1) * P + E - full * P],
                                     a[what][full * P:E].rearrange("(o p) -> o p", o=1)).then_inc(loaded, 16)
                    for b in range(QB):
                        n = min(Q, full - b * Q)
                        src = a["dst"]
                        sp.dma_start(order[0:n, b, :], bass.AP(src.tensor, src.offset + b * Q * P, [[P, n], [1, P + 1]])).then_inc(loaded, 16)
                    sp.dma_start(order[r:r + 1, QB - 1, 0:E - full * P],
                                 a["dst"][full * P:E].rearrange("(o p) -> o p", o=1)).then_inc(loaded, 16)

                @block.vector
                def _(dve):
                    v = Chain(dve, sv)
                    dve.memset(rows_i[:, :, :], PAD).then_inc(cleared, 1)
                    dve.memset(rows_w[:, :], 0.0).then_inc(cleared, 1)
                    dve.memset(order[:, :, :], PAD).then_inc(cleared, 1)
                    dve.wait_ge(loaded, 20 * 16)
                    v.link(dve.tensor_tensor(falls[:, :, :], order[:, :, 1:P + 1], order[:, :, 0:P], ALU.is_lt))
                    dve.tensor_reduce(falls_row[:, :], falls[:, :, :], mybir.AxisListType.XY, ALU.add).then_inc(counted, 1)
                    dve.wait_ge(summed, 1)
                    v.link(dve.tensor_scalar(unsorted[:, :], ps[0][0:1, 0:1], 1.0, None, ALU.min))

                @block.tensor
                def _(pe):
                    pe.wait_ge(counted, 1)
                    nc.tensor.matmul(ps[0][0:1, 0:1], falls_row[:, :], ones[0:Q, 0:1], start=True, stop=True).then_inc(summed, 1)

            with ExitStack() as st, nc.Block() as block:
                KN = 14
                KP = EP // KN
                COLS = QB * P
                keys = sb(st, "keys", [Q, KP], fp32)
                place_in = sb(st, "place_in", [Q, KP], fp32)
                same = sb(st, "same", [Q, KP], fp32)
                own = sb(st, "own", [Q, COLS], fp32)
                own_in = sb(st, "own_in", [Q, COLS], fp32)
                below = sb(st, "below", [Q, 2, COLS], fp32)
                rank_d = sb(st, "rank", [Q, COLS], fp32)
                rank_di = sb(st, "rank_di", [Q, COLS], i32)
                rec = sb(st, "rec", [Q, COLS, 4], fp32)
                i_slot = sb(st, "i_slot", [Q, 1], i32)
                r_slot = sb(st, "r_slot", [Q, 4], fp32)
                cast = sem(st, "cast")
                stored = sem(st, "stored")
                keys_in = sem(st, "keys_in")
                keys_used = sem(st, "keys_used")
                places = sem(st, "places")
                ranked = sem(st, "ranked")
                staged = sem(st, "staged")
                scattered = sem(st, "scattered")
                back = sem(st, "back")
                sv = sem(st, "dve_chain")

                @block.sync
                def _(sp):
                    with sp.If(sp.value_load(unsorted[0:1, 0:1], min_val=0, max_val=1)):
                        sp.wait_ge(cast, 1)
                        sp.dma_start(dst_padded.rearrange("(b q p) -> q b p", b=QB, p=P),
                                     rows_f[:, 1, :].rearrange("q (b p) -> q b p", p=P)).then_inc(stored, 16)
                        sp.wait_ge(stored, 16)
                        for n in range(KN):
                            if n:
                                sp.wait_ge(keys_used, n)
                            sp.dma_start(keys[:, :], dst_padded[n * KP:(n + 1) * KP].partition_broadcast(Q)).then_inc(keys_in, 16)
                        sp.wait_ge(scattered, 1)
                        sp.dma_start(rec[:, :, :].rearrange("q (b p) k -> q b (p k)", p=P),
                                     records.rearrange("(b q p) k -> q b (p k)", b=QB, p=P)).then_inc(back, 16)

                @block.gpsimd
                def _(pool):
                    with pool.If(pool.value_load(unsorted[0:1, 0:1], min_val=0, max_val=1)):
                        pool.iota(place_in[:, :], [[1, KP]], 0, 0, allow_small_or_imprecise_dtypes=True).then_inc(places, 1)
                        pool.iota(own[:, :], [[Q * P, QB], [1, P]], 0, P, allow_small_or_imprecise_dtypes=True).then_inc(places, 1)
                        pool.wait_ge(ranked, 1)
                        with pool.Fori(0, COLS) as j:
                            pool.tensor_copy(i_slot[:, :], rank_di[:, bass.ds(j, 1)]).then_inc(staged, 1)
                            pool.tensor_copy(r_slot[:, :].unsqueeze(1), rec[:, bass.ds(j, 1), :]).then_inc(staged, 1)
                            pool.wait_ge(staged, 2 * j + 2)
                            pool.nop(nofuse=True)
                            pool.indirect_dma_start(out=records, out_offset=bass.IndirectOffsetOnAxis(ap=i_slot[:, :], axis=0),
                                                    in_=r_slot[:, :], in_offset=None).then_inc(sort_done, 16)
                            pool.wait_ge(sort_done, 16 * j + 16)
                        pool.sem_inc(scattered, 1)

                @block.vector
                def _(dve):
                    with dve.If(dve.value_load(unsorted[0:1, 0:1], min_val=0, max_val=1)):
                        v = Chain(dve, sv)
                        dve.tensor_copy(rows_f[:, :, :], rows_i[:, :, :]).then_inc(cast, 1)
                        dve.wait_ge(cast, 1)
                        v.step(dve.tensor_copy(rec[:, :, 0], rows_f[:, 1, :]))
                        v.step(dve.tensor_copy(rec[:, :, 1], rows_w[:, :]))
                        v.step(dve.tensor_copy(rec[:, :, 2], rows_f[:, 0, :]))
                        v.step(dve.memset(rec[:, :, 3], 0.0))
                        v.link(dve.memset(rank_d[:, :], 0.0))
                        dve.wait_ge(places, 2)
                        for n in range(KN):
                            dve.wait_ge(keys_in, 16 * (n + 1))
                            v.link(dve.tensor_scalar(own_in[:, :], own[:, :], -float(n * KP), None, ALU.add))
                            base = v.n
                            with dve.Fori(0, COLS) as j:
                                v.n = base + 3 * j
                                key = rows_f[:, 1, bass.ds(j, 1)]
                                v.link(dve.tensor_scalar(same[:, :], keys[:, :], key, None, ALU.is_lt, ALU.add,
                                                         accum_out=below[:, 0, bass.ds(j, 1)]))
                                v.link(dve.tensor_scalar(same[:, :], keys[:, :], key, None, ALU.is_equal))
                                v.link(dve.scalar_tensor_tensor(same[:, :], place_in[:, :], own_in[:, bass.ds(j, 1)], same[:, :],
                                                                ALU.is_lt, ALU.mult, accum_out=below[:, 1, bass.ds(j, 1)]))
                            v.n = base + 3 * COLS
                            dve.sem_inc(keys_used, 1)
                            for k in range(2):
                                v.link(dve.tensor_tensor(rank_d[:, :], rank_d[:, :], below[:, k, :], ALU.add))
                        v.link(dve.tensor_copy(rank_di[:, :], rank_d[:, :]))
                        dve.sem_inc(ranked, 1)
                        dve.wait_ge(back, 16)
                        v.step(dve.tensor_copy(rows_i[:, 0, :], rec[:, :, 2]))
                        v.step(dve.tensor_copy(rows_i[:, 1, :], rec[:, :, 0]))
                        v.link(dve.tensor_copy(rows_w[:, :], rec[:, :, 1]))

            with ExitStack() as st, nc.Block() as block:
                ps = banks(st, "edges", 5)
                cleared = sem(st, "cleared")
                loaded = sem(st, "loaded")
                cast = sem(st, "cast")
                turned = sem(st, "turned")
                stored = sem(st, "stored")
                looked = sem(st, "looked")
                spread = sem(st, "spread")
                last_made = sem(st, "last_made")
                sv = sem(st, "dve_chain")
                counted = sem(st, "counted")

                @block.sync
                def _(sp):
                    sp.wait_ge(cast, 2)
                    sp.dma_start(dst_padded.rearrange("(b q p) -> q b p", b=QB, p=P),
                                 rows_f[:, 1, :].rearrange("q (b p) -> q b p", p=P)).then_inc(stored, 16)
                    for w in range(2):
                        sp.dma_start(low_rows[w, :].rearrange("(b q p) -> q b p", b=QB, p=P),
                                     rows_lo8[:, w, :].rearrange("q (b p) -> q b p", p=P)).then_inc(stored, 16)
                    sp.wait_ge(stored, 48)
                    sp.wait_ge(cleared, 1)
                    with nc.allow_non_contiguous_dma(reason="one value per chunk"):
                        firsts = dst_padded.rearrange("(c p) -> p c", p=P)[0:1, :]
                        lasts = dst_padded.rearrange("(c p) -> p c", p=P)[P - 1:P, :]
                        for h in range(H):
                            sp.dma_start(chunk_first[h:h + 1, :], firsts).then_inc(looked, 16)
                            sp.dma_start(chunk_last[h:h + 1, :], lasts).then_inc(looked, 16)
                        for b in range(QB):
                            n = Q if b < QB - 1 else Q - 1
                            at = b * Q + 1
                            sp.dma_start(next_first[0:n, b:b + 1],
                                         dst_padded.rearrange("(c p) -> c p", p=P)[at:at + n, 0:1]).then_inc(looked, 16)

                @block.vector
                def _(dve):
                    v = Chain(dve, sv)
                    dve.memset(next_first[:, :], -1.0).then_inc(cleared, 1)
                    v.step(dve.memset(reset_f[:, :], -BIG))
                    v.step(dve.memset(reset_b[:, :], -BIG))
                    v.step(dve.memset(join_f[:, :], -BIG))
                    v.step(dve.memset(join_b[:, :], -BIG))
                    v.step(dve.memset(record[:, :, 3], 0.0))
                    v.link(dve.tensor_scalar(rows_lo[:, :, :], rows_i[:, :, :], P - 1, None, ALU.bitwise_and))
                    dve.tensor_copy(rows_lo8[:, :, :], rows_lo[:, :, :]).then_inc(cast, 1)
                    dve.tensor_copy(rows_f[:, :, :], rows_i[:, :, :]).then_inc(cast, 1)
                    dve.wait_ge(turned, 3)
                    v.step(dve.tensor_copy(edge[:, 0, :], ps[0][:, 0:C]))
                    v.step(dve.tensor_copy(edge[:, 1, :], ps[1][:, 0:C]))
                    v.link(dve.tensor_copy(edge_w[:, :], ps[2][:, 0:C]))
                    v.link(dve.tensor_copy(edge_i[:, :, :], edge[:, :, :]))
                    v.link(dve.tensor_scalar(hi_i[:, :, :], edge_i[:, :, :], 7, None, ALU.logical_shift_right))
                    v.link(dve.tensor_copy(hi_f[:, :, :], hi_i[:, :, :]))
                    for w in range(2):
                        for t in range(NT):
                            v.step(dve.tensor_scalar(hot_hi[w][:, t, :], hi_f[:, w, :], float(t), None, ALU.is_equal))
                    v.link(dve.tensor_copy(tile_d[:, 0:C], hi_i[0:1, 1, :]))
                    for w in range(2):
                        v.link(dve.tensor_reduce(counts[:, w, :], hot_hi[w][:, :, :], X, ALU.add))
                    dve.sem_inc(counted, 1)
                    v.step(dve.tensor_copy(gidx_d[:, 0:C], edge[:, 0, :]))
                    v.step(dve.tensor_copy(record[:, :, 0], edge[:, 1, :]))
                    v.step(dve.tensor_copy(record[:, :, 1], edge_w[:, :]))
                    v.step(dve.tensor_copy(record[:, :, 2], edge[:, 0, :]))
                    dve.wait_ge(spread, 1)
                    for w in range(2):
                        v.link(dve.tensor_tensor_scan(begins[:, w, :], ones[0:1, 0:NT], ps[3][0:1, w * NT:(w + 1) * NT], 0.0,
                                                      ALU.mult, ALU.add))
                    v.link(dve.tensor_copy(begins_i[:, :, :], begins[:, :, :]))
                    v.step(dve.tensor_scalar(begin_s[:, :], begins_i[:, 0, :], 7, None, ALU.logical_shift_right))
                    v.step(dve.tensor_scalar(begin_d[:, :], begins_i[:, 1, :], 7, None, ALU.logical_shift_right))
                    v.link(dve.tensor_copy(hi_rep[:, 1, :], ps[4][:, 0:C]))
                    v.step(dve.scalar_tensor_tensor(local_d[:, 0:C], hi_rep[:, 1, :], -float(P), edge[:, 1, :], ALU.mult, ALU.add))
                    rf = reset_f[:, :].rearrange("q (h r p) -> q h r p", h=H, p=P)
                    rb = reset_b[:, :].rearrange("q (h r p) -> q h r p", h=H, p=P)
                    d = rows_f[:, 1, :].rearrange("q (b p) -> q b p", p=P)
                    v.link(dve.tensor_tensor(rf[:, 0, :, 1:P], d[:, :, 1:P], d[:, :, 0:P - 1], ALU.is_equal))
                    v.step(dve.tensor_scalar(last_rows[:, :, 0:P - 1], rf[:, 0, :, 1:P], -1.0, 1.0, ALU.mult, ALU.add))
                    v.link(dve.tensor_scalar(rb[:, 0, :, 0:P - 1], rf[:, 0, :, 1:P], -1.0, BIG, ALU.add, ALU.mult))
                    v.link(dve.tensor_copy(rf[:, 0, :, 1:P], rb[:, 0, :, 0:P - 1]))
                    for h in range(1, H):
                        v.step(dve.tensor_copy(rf[:, h, :, :], rf[:, 0, :, :]))
                        v.step(dve.tensor_copy(rb[:, h, :, :], rb[:, 0, :, :]))
                    dve.wait_ge(looked, (2 * H + QB) * 16)
                    v.link(dve.tensor_tensor(last_rows[:, :, P - 1], d[:, :, P - 1], next_first[:, :], ALU.is_equal))
                    v.link(dve.tensor_scalar(last_rows[:, :, P - 1], last_rows[:, :, P - 1], -1.0, 1.0, ALU.mult, ALU.add))
                    dve.sem_inc(last_made, 1)
                    v.link(dve.tensor_tensor(join_f[:, 1:C], chunk_first[:, 1:C], chunk_last[:, 0:C - 1], ALU.is_equal))
                    v.link(dve.tensor_scalar(join_b[:, 0:C - 1], join_f[:, 1:C], -1.0, BIG, ALU.add, ALU.mult))
                    v.link(dve.tensor_copy(join_f[:, 1:C], join_b[:, 0:C - 1]))
                    v.link(dve.tensor_tensor(gate_f[:, :], chunk_first[:, :], chunk_last[:, :], ALU.is_equal))
                    v.link(dve.tensor_scalar(gate_b[:, :], gate_f[:, :], -1.0, BIG, ALU.add, ALU.mult))
                    v.link(dve.tensor_tensor(gate_f[:, :], gate_b[:, :], join_f[:, :], ALU.add))
                    v.link(dve.tensor_tensor(gate_b[:, :], gate_b[:, :], join_b[:, :], ALU.add))
                    dve.wait_ge(turned, 4)
                    v.link(dve.tensor_copy(is_last[:, :], ps[0][:, 0:C]))

                @block.tensor
                def _(pe):
                    pe.wait_ge(cast, 2)
                    for n, rows in enumerate((rows_f[:, 0, :], rows_f[:, 1, :], rows_w[:, :])):
                        for b in range(QB):
                            last = nc.tensor.transpose(ps[n][:, b * Q:(b + 1) * Q], rows[:, b * P:(b + 1) * P], ident[0:Q, 0:Q])
                        last.then_inc(turned, 1)
                    pe.wait_ge(counted, 1)
                    nc.tensor.matmul(ps[3][:, 0:2 * NT], ones[:, :], counts[:, :, :].rearrange("p w t -> p (w t)"), start=True, stop=True)
                    nc.tensor.matmul(ps[4][:, 0:C], row0[:, :], hi_f[:, 1, :], start=True, stop=True).then_inc(spread, 1)
                    pe.wait_ge(last_made, 1)
                    for b in range(QB):
                        last = nc.tensor.transpose(ps[0][:, b * Q:(b + 1) * Q], last_rows[:, b, :], ident[0:Q, 0:Q])
                    last.then_inc(turned, 1)

            with ExitStack() as st, nc.Block() as block:
                ps = banks(st, "place", 4)
                hot = sb(st, "hot", [P, NT, C], bf16)
                place = sb(st, "place", [P, NT, C], fp32)
                before = sb(st, "before", [P, P], bf16)
                ones_b = sb(st, "ones_b", [P, P], bf16)
                total = sb(st, "total", [P, 2, PW], fp32)
                hot_made = sem(st, "hot_made")
                const_made = sem(st, "const_made")
                summed = sem(st, "summed")
                sv = sem(st, "dve_chain")
                placed = sem(st, "placed")

                @block.gpsimd
                def _(pool):
                    pool.memset(ones_b[:, :], 1.0).then_inc(const_made, 1)
                    pool.memset(before[:, :], -1.0).then_inc(const_made, 1)
                    pool.wait_ge(const_made, 2)
                    pool.affine_select(out=before[:, :], in_=before[:, :], compare_op=ALU.is_ge, fill=0.0, base=0,
                                       pattern=[[-1, P]], channel_multiplier=1).then_inc(const_made, 1)

                @block.tensor
                def _(pe):
                    pe.wait_ge(const_made, 3)
                    pe.wait_ge(hot_made, 1)
                    flat = hot[:, :, :].rearrange("p t c -> p (t c)")
                    for n in range(PIECES):
                        if n >= 2:
                            pe.wait_ge(placed, n - 1)
                        piece = flat[:, n * PW:(n + 1) * PW]
                        nc.tensor.matmul(ps[n % 2][:, 0:PW], ones_b[:, :], piece, start=True, stop=True)
                        nc.tensor.matmul(ps[2 + n % 2][:, 0:PW], before[:, :], piece, start=True, stop=True).then_inc(summed, 1)

                @block.vector
                def _(dve):
                    v = Chain(dve, sv)
                    dve.tensor_copy(hot[:, :, :], hot_hi[0][:, :, :]).then_inc(hot_made, 1)
                    flat = place[:, :, :].rearrange("p t c -> p (t c)")
                    for n in range(PIECES):
                        dve.wait_ge(summed, n + 1)
                        start = 0.0 if n == 0 else total[:, (n - 1) % 2, PW - 1:PW]
                        v.link(dve.tensor_tensor_scan(total[:, n % 2, :], ones[:, 0:1].broadcast_to([P, PW]), ps[n % 2][:, 0:PW], start,
                                                      ALU.mult, ALU.add))
                        v.step(dve.tensor_tensor(flat[:, n * PW:(n + 1) * PW], total[:, n % 2, :], ps[2 + n % 2][:, 0:PW], ALU.add))
                        dve.wait_ge(sv, v.n)
                        dve.sem_inc(placed, 1)
                    v.link(dve.tensor_tensor(place[:, :, :], place[:, :, :], hot[:, :, :], ALU.mult))
                    v.link(dve.tensor_reduce(rank[:, :], place[:, :, :].rearrange("p t c -> p c t"), X, ALU.add))
                    v.link(dve.tensor_copy(rank_i[:, :], rank[:, :]))

            with ExitStack() as st, nc.Block() as block:
                r_slot = sb(st, "r_slot", [P, U, 4], fp32)
                i_slot = sb(st, "i_slot", [P, U], i32)
                staged = sem(st, "staged")

                @block.scalar
                def _(act):
                    def stage(s, c):
                        act.activation(i_slot[:, s:s + 1], rank_i[:, bass.ds(c, 1)], ACT.Copy).then_inc(staged, 1)
                        act.activation(r_slot[:, s:s + 1, :], record[:, bass.ds(c, 1), :], ACT.Copy).then_inc(staged, 1)

                    for s in range(U):
                        stage(s, s)
                    with act.Fori(1, C // U) as i:
                        for s in range(U):
                            act.wait_ge(slot_done[s], 16 * i)
                            stage(s, U * i + s)

                @block.gpsimd
                def _(pool):
                    with pool.Fori(0, C // U) as i:
                        for s in range(U):
                            pool.wait_ge(staged, 2 * U * i + 2 * s + 2)
                            pool.nop(nofuse=True)
                            pool.indirect_dma_start(out=records, out_offset=bass.IndirectOffsetOnAxis(ap=i_slot[:, s:s + 1], axis=0),
                                                    in_=r_slot[:, s, :], in_offset=None).then_inc(slot_done[s], 16)
                    for s in range(U):
                        pool.wait_ge(slot_done[s], 16 * (C // U))

            slots_used[0] += C // U
            with ExitStack() as st, nc.Block() as block:
                ps = banks(st, "back", 4)
                rec_rows = sb(st, "rec_rows", [Q, QB, P, 4], fp32)
                near = sb(st, "near", [P, 2, NT], fp32)
                back = sem(st, "back")
                turned = sem(st, "turned")
                hi_made = sem(st, "hi_made")
                spread = sem(st, "spread")
                sv = sem(st, "dve_chain")

                @block.sync
                def _(sp):
                    sp.dma_start(rec_rows[:, :, :, :].rearrange("q b p k -> q b (p k)"),
                                 records.rearrange("(b q p) k -> q b (p k)", b=QB, p=P)).then_inc(back, 16)

                @block.tensor
                def _(pe):
                    pe.wait_ge(back, 16)
                    for k in range(3):
                        for b in range(QB):
                            last = nc.tensor.transpose(ps[k][:, b * Q:(b + 1) * Q], rec_rows[:, b, :, k], ident[0:Q, 0:Q])
                    last.then_inc(turned, 1)
                    pe.wait_ge(hi_made, 1)
                    nc.tensor.matmul(ps[3][:, 0:C], row0[:, :], hi_f[:, 0, :], start=True, stop=True).then_inc(spread, 1)

                @block.vector
                def _(dve):
                    v = Chain(dve, sv)
                    dve.wait_ge(turned, 1)
                    v.step(dve.tensor_copy(gidx_s[:, 0:C], ps[0][:, 0:C]))
                    v.step(dve.tensor_copy(w_s[:, 0:C], ps[1][:, 0:C]))
                    v.step(dve.tensor_copy(edge[:, 0, :], ps[2][:, 0:C]))
                    v.link(dve.tensor_copy(edge_i[:, 0, :], ps[2][:, 0:C]))
                    v.link(dve.tensor_scalar(hi_i[:, 0, :], edge_i[:, 0, :], 7, None, ALU.logical_shift_right))
                    v.link(dve.tensor_copy(hi_f[:, 0, :], hi_i[:, 0, :]))
                    dve.sem_inc(hi_made, 1)
                    v.step(dve.tensor_copy(tile_s[:, 0:C], hi_i[0:1, 0, :]))
                    dve.wait_ge(spread, 1)
                    v.link(dve.tensor_copy(hi_rep[:, 0, :], ps[3][:, 0:C]))
                    v.link(dve.scalar_tensor_tensor(local_s[:, 0:C], hi_rep[:, 0, :], -float(P), edge[:, 0, :], ALU.mult, ALU.add))
                    for col in (gidx_d, gidx_s, w_s):
                        v.step(dve.memset(col[:, C:CX], 0.0))
                    for col in (local_d, local_s):
                        v.step(dve.memset(col[:, C:CX], -1.0))
                    for col in (tile_d, tile_s):
                        v.step(dve.memset(col[:, C:CX], 0))
                    dve.wait_ge(sv, v.n)
                    for t in range(NT - 1):
                        for begin, w, pairs in ((begin_d, 1, ((gidx_d, gidx_d), (local_d, edge[:, 1, :]))),
                                                (begin_s, 0, ((gidx_s, gidx_s), (w_s, w_s), (local_s, edge[:, 0, :])))):
                            c = dve.value_load(begin[0:1, t:t + 1], min_val=0, max_val=C - 1)
                            for to, of in pairs:
                                v.step(dve.tensor_copy(to[:, C + t:C + t + 1], of[:, bass.ds(c, 1)]))
                            v.step(dve.tensor_copy(near[:, w, t:t + 1], hi_rep[:, w, bass.ds(c, 1)]))
                        v.step(dve.memset(tile_d[:, C + t:C + t + 1], t + 1))
                        v.step(dve.memset(tile_s[:, C + t:C + t + 1], t + 1))
                    dve.wait_ge(sv, v.n)
                    own = sb(st, "own", [P, NT - 1], fp32)
                    off = sb(st, "off", [P, NT - 1], fp32)
                    for t in range(NT - 1):
                        v.step(dve.memset(off[:, t:t + 1], float(P * (t + 1))))
                    dve.wait_ge(sv, v.n)
                    for w, col in ((0, local_s), (1, local_d)):
                        v.link(dve.tensor_scalar(own[:, :], near[:, w, 0:NT - 1], float(P), None, ALU.mult))
                        v.link(dve.tensor_tensor(own[:, :], own[:, :], off[:, :], ALU.is_equal))
                        v.link(dve.scalar_tensor_tensor(own[:, :], own[:, :], -2.0 * NP, off[:, :], ALU.mult, ALU.subtract))
                        v.link(dve.tensor_tensor(col[:, C:C + NT - 1], col[:, C:C + NT - 1], own[:, :], ALU.add))

        x_sb = sb(top, "x_sb", [P, NT, F], fp32)
        h_sb = sb(top, "h_sb", [P, NT, F], fp32)
        alphas = sb(top, "alphas", [P, NT, 2 * H], fp32)
        W_sb = sb(top, "W_sb", [P, K2, WMAX], fp32)
        norm = sb(top, "norm", [P, NT], fp32)
        with ExitStack() as ph, nc.Block() as block:
            loaded = sem(ph, "loaded")
            zeroed = sem(ph, "zeroed")

            @block.vector
            def _(dve):
                dve.memset(x_sb[:, NT - 1, :], 0.0).then_inc(zeroed, 1)
                dve.memset(norm[:, :], 0.0).then_inc(zeroed, 1)

            @block.sync
            def _(sp):
                sp.wait_ge(zeroed, 2)
                sp.dma_start(x_sb[:, 0:NT - 1, :], a["x"][0:(NT - 1) * P, :].rearrange("(t p) f -> p t f", p=P)).then_inc(loaded, 16)
                sp.dma_start(x_sb[0:LAST, NT - 1, :], a["x"][(NT - 1) * P:N, :]).then_inc(loaded, 16)
                with nc.allow_non_contiguous_dma(reason="one value per node"):
                    sp.dma_start(norm[:, 0:NT - 1], a["node_vec1"][0:(NT - 1) * P, :].rearrange("(t p) o -> p (t o)", p=P)).then_inc(loaded, 16)
                    sp.dma_start(norm[0:LAST, NT - 1:NT], a["node_vec1"][(NT - 1) * P:N, :]).then_inc(loaded, 16)
                sp.wait_ge(loaded, 64)

        def layer_norm(f_all):
            with ExitStack() as st, nc.Block() as block:
                stats = sb(st, "stats", [P, NT, 6], fp32)
                mv = sb(st, "mv", [P, NT, 2], fp32)
                var = sb(st, "var", [P, NT], fp32)
                dev = sb(st, "dev", [P, NT], fp32)
                rstd = sb(st, "rstd", [P, NT], fp32)
                shift = sb(st, "shift", [P, NT], fp32)
                var_made = sem(st, "var_made")
                dev_made = sem(st, "dev_made")
                scale_made = sem(st, "scale_made")
                sv = sem(st, "dve_chain")

                @block.vector
                def _(dve):
                    v = Chain(dve, sv)
                    for t in range(NT):
                        v.step(dve.bn_stats(stats[:, t, :], x_sb[:, t, :]))
                    dve.wait_ge(sv, v.n)
                    for t in range(NT):
                        v.step(dve.bn_aggr(mv[:, t, :], stats[:, t, :]))
                    dve.wait_ge(sv, v.n)
                    dve.tensor_scalar(var[:, :], mv[:, :, 1], EPS_LN, None, ALU.add).then_inc(var_made, 1)
                    dve.wait_ge(dev_made, 1)
                    v.link(dve.reciprocal(rstd[:, :], dev[:, :]))
                    dve.scalar_tensor_tensor(shift[:, :], mv[:, :, 0], -1.0, rstd[:, :], ALU.mult, ALU.mult).then_inc(scale_made, 1)

                @block.scalar
                def _(act):
                    act.wait_ge(var_made, 1)
                    act.activation(dev[:, :], var[:, :], ACT.Sqrt).then_inc(dev_made, 1)
                    act.wait_ge(scale_made, 1)
                    for t in range(NT):
                        act.activation(f_all[:, t, :], x_sb[:, t, :], ACT.Relu, bias=shift[:, t:t + 1], scale=rstd[:, t:t + 1])

        def load_weights(parts, attention=None, nh=0):
            with ExitStack() as st, nc.Block() as block:
                vec = sb(st, "vec", [P, 2, F], fp32)
                prod = sb(st, "prod", [P, F], fp32)
                loaded = sem(st, "loaded")
                sv = sem(st, "dve_chain")

                @block.sync
                def _(sp):
                    for n, w in enumerate(parts):
                        sp.dma_start(W_sb[:, :, n * F:(n + 1) * F], w.rearrange("(k p) f -> p k f", p=P)).then_inc(loaded, 16)
                    for n, vector in enumerate(attention or ()):
                        sp.dma_start(vec[:, n, :], row_broadcast(vector.rearrange("h c -> (h c)"))).then_inc(loaded, 16)
                    sp.wait_ge(loaded, 16 * (len(parts) + len(attention or ())))

                @block.vector
                def _(dve):
                    v = Chain(dve, sv)
                    if attention:
                        dve.wait_ge(loaded, 48)
                        for k in range(K2):
                            for n in range(2):
                                v.link(dve.tensor_tensor(prod[:, :], W_sb[:, k, 0:F], vec[:, n, :], ALU.mult))
                                v.link(dve.tensor_reduce(W_sb[:, k, F + n * nh:F + (n + 1) * nh],
                                                         prod[:, :].rearrange("p (h c) -> p h c", h=nh), X, ALU.add))

        def project(f_all, cols, put, n_puts, table, table_src, scale=None):
            with ExitStack() as st, nc.Block() as block:
                ps_t = banks(st, "turn", 2)
                ps_h = banks(st, "prod", 2)
                f_t = sb(st, "f_t", [P, 2, F], fp32)
                turned = sem(st, "turned")
                f_ready = sem(st, "f_ready")
                product = sem(st, "product")
                taken = sem(st, "taken")
                stored = sem(st, "stored")

                @block.tensor
                def _(pe):
                    def turn(t):
                        if t >= 2:
                            pe.wait_ge(f_ready, t - 1)
                        for k in range(K2):
                            last = nc.tensor.transpose(ps_t[t % 2][:, k * P:(k + 1) * P], f_all[:, t, k * P:(k + 1) * P], ident[:, :])
                        last.then_inc(turned, 1)

                    turn(0)
                    for t in range(NT):
                        if t + 1 < NT:
                            turn(t + 1)
                        pe.wait_ge(f_ready, t + 1)
                        if t >= 2:
                            pe.wait_ge(taken, n_puts * (t - 1))
                        for k in range(K2):
                            last = nc.tensor.matmul(ps_h[t % 2][:, 0:cols], f_t[:, t % 2, k * P:(k + 1) * P], W_sb[:, k, 0:cols],
                                                    start=(k == 0), stop=(k == K2 - 1))
                        last.then_inc(product, 1)

                @block.vector
                def _(dve):
                    for t in range(NT):
                        dve.wait_ge(turned, t + 1)
                        if t >= 2:
                            dve.wait_ge(product, t - 1)
                        dve.tensor_copy(f_t[:, t % 2, :], ps_t[t % 2][:, 0:F]).then_inc(f_ready, 1)

                @block.scalar
                def _(act):
                    for t in range(NT):
                        act.wait_ge(product, t + 1)
                        put(act, t, ps_h[t % 2], taken)

                if table is not None:
                    @block.sync
                    def _(sp):
                        step = 5
                        for t in range(0, NT, step):
                            sp.wait_ge(taken, n_puts * (t + step))
                            sp.dma_start(table[t * P:(t + step) * P, :].rearrange("(t p) f -> p t f", p=P),
                                         table_src[:, t:t + step, :]).then_inc(stored, 16)
                        sp.wait_ge(stored, 16 * (NT // step))

        def look_up(which, nh, found):
            W = NT * nh
            G = 4 if nh > 1 else 14
            with ExitStack() as st, nc.Block() as block:
                low = sb(st, "low", [P, EP], u8)
                parts = sb(st, "parts", [P, 3, NT, nh], bf16)
                rest = sb(st, "rest", [P, 2, NT, nh], fp32)
                hot = sb(st, "hot", [P, 2, G * P], bf16)
                picked = sb(st, "picked", [P, 2, G, nh, NT], fp32)
                ps = banks(st, "ps", 2)
                low_in = sem(st, "low_in")
                hot_made = sem(st, "hot_made")
                product = sem(st, "product")
                masked = sem(st, "masked")
                summed = sem(st, "summed")
                sv = sem(st, "dve_chain")

                @block.sync
                def _(sp):
                    sp.dma_start(low[:, :], row_broadcast(low_rows[which, :])).then_inc(low_in, 16)

                @block.vector
                def _(dve):
                    v = Chain(dve, sv)
                    tab = alphas[:, :, which * nh:(which + 1) * nh]
                    v.link(dve.tensor_copy(parts[:, 0, :, :], tab))
                    v.link(dve.tensor_tensor(rest[:, 0, :, :], tab, parts[:, 0, :, :], ALU.subtract))
                    v.link(dve.tensor_copy(parts[:, 1, :, :], rest[:, 0, :, :]))
                    v.link(dve.tensor_tensor(rest[:, 1, :, :], rest[:, 0, :, :], parts[:, 1, :, :], ALU.subtract))
                    dve.tensor_copy(parts[:, 2, :, :], rest[:, 1, :, :]).then_inc(masked, 2)
                    dve.wait_ge(masked, 2)
                    dve.sem_inc(summed, 2)
                    dve.wait_ge(low_in, 16)

                    def one_hot(g, u):
                        dve.tensor_scalar(hot[:, u, :], low[:, bass.ds(g * G * P, G * P)], part[:, 0:1], None,
                                          ALU.is_equal).then_inc(hot_made, 1)

                    def pick(g, u, more):
                        dve.wait_ge(product, g + 1)
                        dve.wait_ge(summed, g + 1)
                        dve.tensor_tensor(
                            picked[:, u, :, :, :].rearrange("p c h t -> p c t h"),
                            ps[u][:, 0:G * W].rearrange("p (c t h) -> p c t h", c=G, h=nh),
                            hot_hi[which][:, :, bass.ds(g * G, G)].rearrange("p t c -> p c t").unsqueeze(3).broadcast_to([P, G, NT, nh]),
                            ALU.mult).then_inc(masked, 1)
                        if more:
                            one_hot(g + 2, u)
                        dve.wait_ge(masked, g + 3)
                        dve.tensor_reduce(found[:, bass.ds(g * G, G), 0:nh], picked[:, u, :, :, :], X, ALU.add).then_inc(summed, 1)

                    for u in range(2):
                        one_hot(u, u)
                    with dve.Fori(0, C // (2 * G) - 1) as i:
                        for u in range(2):
                            pick(2 * i + u, u, True)
                    for u in range(2):
                        pick(C // G - 2 + u, u, False)

                @block.tensor
                def _(pe):
                    with pe.Fori(0, C // (2 * G)) as i:
                        for u in range(2):
                            pe.wait_ge(hot_made, 2 * i + u + 1)
                            pe.wait_ge(masked, 2 * i + u + 1)
                            for g in range(G):
                                for k in range(3):
                                    last = nc.tensor.matmul(ps[u][:, g * W:(g + 1) * W], hot[:, u, g * P:(g + 1) * P],
                                                            parts[:, k, :, :].rearrange("p t h -> p (t h)"), start=(k == 0), stop=(k == 2))
                            last.then_inc(product, 1)

        def edge_softmax(nh, at_src, at_dst):
            L = nh * QB * P
            with ExitStack() as st, nc.Block() as block:
                ps = banks(st, "ps", 8)
                rows = sb(st, "rows", [Q, H * QB * P], fp32)
                run_f = sb(st, "run_f", [Q, H * QB * P], fp32)
                run_b = sb(st, "run_b", [Q, H * QB * P], fp32)
                ends = sb(st, "ends", [H, 2, C], fp32)
                carry = sb(st, "carry", [H, 2, C], fp32)
                top_src = sb(st, "top_src", [P, C, H], fp32)
                turned = sem(st, "turned")
                ran = sem(st, "ran")
                carried = sem(st, "carried")
                ready = sem(st, "ready")
                exped = sem(st, "exped")
                sv = sem(st, "dve_chain")

                def rows_v(tile):
                    return tile[:, 0:L].rearrange("q (h b p) -> q h b p", h=nh, p=P)

                @block.tensor
                def _(pe):
                    for h in range(nh):
                        for b in range(QB):
                            last = nc.tensor.transpose(ps[h][0:Q, b * P:(b + 1) * P], at_src[:, b * Q:(b + 1) * Q, h], ident[:, :])
                    last.then_inc(turned, 1)
                    pe.wait_ge(ran, 1)
                    for n, (tile, p) in enumerate(((run_f, P - 1), (run_b, 0))):
                        for b in range(QB):
                            last = nc.tensor.transpose(ps[4 + n][0:nh, b * Q:(b + 1) * Q], rows_v(tile)[:, :, b, p], ident[0:Q, 0:Q])
                    last.then_inc(turned, 1)
                    pe.wait_ge(carried, 1)
                    for n in range(2):
                        for b in range(QB):
                            last = nc.tensor.transpose(ps[6 + n][0:Q, b * nh:(b + 1) * nh], carry[0:nh, n, b * Q:(b + 1) * Q],
                                                       ident[0:nh, 0:nh])
                    last.then_inc(turned, 1)
                    pe.wait_ge(ran, 2)
                    for h in range(nh):
                        for b in range(QB):
                            last = nc.tensor.transpose(ps[h][:, b * Q:(b + 1) * Q], rows_v(run_f)[:, h, b, :], ident[0:Q, 0:Q])
                    last.then_inc(turned, 1)

                @block.vector
                def _(dve):
                    v = Chain(dve, sv)

                    def runs():
                        v.step(dve.tensor_tensor_scan(run_f[:, 0:L], reset_f[:, 0:L], rows[:, 0:L], -BIG, ALU.add, ALU.max))
                        v.link(dve.tensor_tensor_scan(run_b[:, 0:L][:, ::-1], reset_b[:, 0:L][:, ::-1], rows[:, 0:L][:, ::-1], -BIG,
                                                      ALU.add, ALU.max))

                    dve.wait_ge(turned, 1)
                    for h in range(nh):
                        v.step(dve.tensor_copy(rows[:, h * QB * P:(h + 1) * QB * P], ps[h][0:Q, 0:QB * P]))
                    dve.wait_ge(sv, v.n)
                    runs()
                    dve.sem_inc(ran, 1)
                    dve.wait_ge(turned, 2)
                    v.link(dve.tensor_tensor_scan(ends[0:nh, 0, :], gate_f[0:nh, :], ps[4][0:nh, 0:C], -BIG, ALU.add, ALU.max))
                    v.link(dve.tensor_tensor_scan(ends[0:nh, 1, ::-1], gate_b[0:nh, ::-1], ps[5][0:nh, 0:C][:, ::-1], -BIG, ALU.add, ALU.max))
                    v.step(dve.tensor_tensor(carry[0:nh, 0, 1:C], ends[0:nh, 0, 0:C - 1], join_f[0:nh, 1:C], ALU.add))
                    v.step(dve.memset(carry[0:nh, 0, 0:1], -BIG))
                    v.step(dve.tensor_tensor(carry[0:nh, 1, 0:C - 1], ends[0:nh, 1, 1:C], join_b[0:nh, 0:C - 1], ALU.add))
                    v.link(dve.memset(carry[0:nh, 1, C - 1:C], -BIG))
                    dve.sem_inc(carried, 1)
                    dve.wait_ge(turned, 3)
                    for n, p in ((0, 0), (1, P - 1)):
                        v.link(dve.tensor_tensor(rows_v(rows)[:, :, :, p], rows_v(rows)[:, :, :, p],
                                                 ps[6 + n][0:Q, 0:QB * nh].rearrange("q (b h) -> q h b", h=nh), ALU.max))
                    runs()
                    v.link(dve.tensor_tensor(run_f[:, 0:L], run_f[:, 0:L], run_b[:, 0:L], ALU.max))
                    dve.sem_inc(ran, 1)
                    dve.wait_ge(turned, 4)
                    for h in range(nh):
                        v.step(dve.tensor_copy(top_src[:, :, h], ps[h][:, 0:C]))
                    dve.wait_ge(sv, v.n)
                    s, d, m = at_src[:, :, 0:nh], at_dst[:, :, 0:nh], top_src[:, :, 0:nh]
                    v.step(dve.tensor_tensor(edge_aux[:, 0:C, nh:2 * nh], m, is_last[:, :].unsqueeze(2).broadcast_to([P, C, nh]), ALU.mult))
                    v.step(dve.tensor_copy(edge_aux[:, 0:C, 2 * nh], is_last[:, :]))
                    v.step(dve.memset(edge_aux[:, C:CX, :], 0.0))
                    v.link(dve.tensor_tensor(s, s, d, ALU.add))
                    v.link(dve.scalar_tensor_tensor(s, s, NEG_SLOPE, s, ALU.mult, ALU.max))
                    v.link(dve.tensor_tensor(d, m, d, ALU.add))
                    v.link(dve.scalar_tensor_tensor(d, d, NEG_SLOPE, d, ALU.mult, ALU.max))
                    v.link(dve.tensor_tensor(s, s, d, ALU.subtract))
                    dve.sem_inc(ready, 1)
                    dve.wait_ge(exped, 1)
                    for t in range(NT - 1):
                        c = dve.value_load(begin_d[0:1, t:t + 1], min_val=0, max_val=C - 1)
                        v.step(dve.tensor_copy(edge_aux[:, C + t:C + t + 1, :], edge_aux[:, bass.ds(c, 1), :]))
                    dve.wait_ge(sv, v.n)

                @block.scalar
                def _(act):
                    act.wait_ge(ready, 1)
                    act.activation(edge_aux[:, 0:C, 0:nh], at_src[:, :, 0:nh], ACT.Exp).then_inc(exped, 1)

        def aggregate(acc, table, index, local, tiles, weight=None, nh=0, aux=None, n_aux=0):
            W = F + n_aux
            with ExitStack() as st, nc.Block() as block:
                ps = banks(st, "ps", U)
                weighted = weight is not None or nh > 0
                rows = sb(st, "rows", [P, U, F if weighted else W], fp32)
                msg = sb(st, "msg", [P, U, W], fp32) if weighted else rows
                hot = sb(st, "hot", [P, U, P], fp32)
                i_slot = sb(st, "i_slot", [P, U], i32)
                row_in, base = slot_done, 16 * slots_used[0]
                slots_used[0] += CX // U
                staged = sem(st, "staged")
                hot_made = sem(st, "hot_made")
                msg_made = sem(st, "msg_made")
                product = sem(st, "product")
                added = sem(st, "added")
                aux_put = sem(st, "aux_put")
                row_used = msg_made if weighted else product
                iters = CX // U
                AHEAD = U // 2

                @block.scalar
                def _(act):
                    with act.Fori(0, iters) as i:
                        for s in range(U):
                            act.wait_ge(row_used, U * i + s + 1)
                            act.activation(i_slot[:, s:s + 1], index[:, bass.ds(U * i + s, 1)], ACT.Copy).then_inc(staged, 1)
                            if nh:
                                act.wait_ge(product, U * i + s + 1)
                                act.activation(msg[:, s:s + 1, F:W], aux[:, bass.ds(U * i + s, 1), 0:n_aux], ACT.Copy).then_inc(aux_put, 1)

                @block.gpsimd
                def _(pool):
                    with pool.Fori(0, iters) as i:
                        for s in range(U):
                            pool.wait_ge(staged, U * i + s + 1)
                            pool.nop(nofuse=True)
                            pool.indirect_dma_start(out=rows[:, s, 0:F], out_offset=None, in_=table,
                                                    in_offset=bass.IndirectOffsetOnAxis(ap=i_slot[:, s:s + 1], axis=0)).then_inc(row_in[s], 16)

                @block.vector
                def _(dve):
                    def prepare(c, s, turn):
                        dve.tensor_scalar(hot[:, s, :], iota[:, :], local[:, bass.ds(c, 1)], None, ALU.is_equal).then_inc(hot_made, 1)
                        if not weighted:
                            return
                        dve.wait_ge(row_in[s], base + 16 * turn + 16)
                        if nh > 1:
                            m = dve.tensor_tensor(msg[:, s, 0:F].rearrange("p (h c) -> p h c", h=nh),
                                                  rows[:, s, :].rearrange("p (h c) -> p h c", h=nh),
                                                  aux[:, bass.ds(c, 1), 0:nh].rearrange("p o h -> p h o").broadcast_to([P, nh, CH]), ALU.mult)
                        elif nh == 1:
                            m = dve.tensor_scalar(msg[:, s, 0:F], rows[:, s, :], aux[:, bass.ds(c, 1), 0:1].rearrange("p o h -> p (o h)"), None, ALU.mult)
                        else:
                            m = dve.tensor_scalar(msg[:, s, 0:F], rows[:, s, :], weight[:, bass.ds(c, 1)], None, ALU.mult)
                        m.then_inc(msg_made, 1)

                    def tiles_of(c):
                        _, values = nc.values_load_multi_w_load_instructions(
                            tiles[0:1, bass.ds(c, U)], engines=(mybir.EngineType.DVE,), min_val=0, max_val=NT - 1,
                            skip_runtime_bounds_check_because="a tile is a node's number shifted, or below NT by its place")
                        return values

                    def add(c, s, t):
                        dve.wait_ge(product, c + 1 + U)
                        dve.wait_ge(added, c + U)
                        dve.tensor_tensor(acc[:, bass.ds(t, 1), 0:W], acc[:, bass.ds(t, 1), 0:W], ps[s][:, 0:W].unsqueeze(1),
                                          ALU.add).then_inc(added, 1)

                    if n_aux and not nh:
                        dve.memset(rows[:, :, F:W], 1.0).then_inc(aux_put, 1)
                    dve.memset(hot[:, 0, 0:1], 0.0).then_inc(msg_made, U)
                    dve.memset(hot[:, 0, 1:2], 0.0).then_inc(product, U)
                    dve.memset(acc[:, :, :], 0.0).then_inc(added, U)
                    dve.wait_ge(added, U)
                    for s in range(AHEAD):
                        prepare(s, s, 0)
                    with dve.Fori(0, iters - 1) as i:
                        at = tiles_of(U * i)
                        for s in range(U):
                            n = s + AHEAD
                            prepare(U * i + n, n % U, i + n // U)
                            add(U * i + s, s, at[s])
                    at = tiles_of(U * (iters - 1))
                    for s in range(U):
                        c = U * (iters - 1) + s
                        if s < AHEAD:
                            prepare(c + AHEAD, s + AHEAD, iters - 1)
                        add(c, s, at[s])

                @block.tensor
                def _(pe):
                    if n_aux and not nh:
                        pe.wait_ge(aux_put, 1)
                    with pe.Fori(0, iters) as i:
                        for s in range(U):
                            c = U * i + s
                            pe.wait_ge(hot_made, c + 1)
                            if weighted:
                                pe.wait_ge(msg_made, c + 1 + U)
                            else:
                                pe.wait_ge(row_in[s], base + 16 * i + 16)
                            pe.wait_ge(added, c + 1)
                            if nh:
                                pe.wait_ge(aux_put, c + 1)
                            nc.tensor.matmul(ps[s][:, 0:W], hot[:, s, :], msg[:, s, :], start=True, stop=True).then_inc(product, 1)

        def gat_combine(acc, nh, bias, finish, temps):
            ch = F // nh
            with ExitStack() as st, nc.Block() as block:
                vec = sb(st, "vec", [P, F], fp32)
                small = sb(st, "small", [P, 6, NT, nh], fp32)
                loaded = sem(st, "loaded")
                ready = sem(st, "ready")
                exped = sem(st, "exped")
                sv = sem(st, "dve_chain")
                finish_sem = sem(st, "finish")

                @block.sync
                def _(sp):
                    sp.dma_start(vec[:, :], row_broadcast(bias)).then_inc(loaded, 16)

                @block.scalar
                def _(act):
                    act.wait_ge(ready, 1)
                    act.activation(small[:, 0:2, :, :], small[:, 0:2, :, :], ACT.Exp).then_inc(exped, 1)
                    finish(None, act, None, None, finish_sem)

                @block.vector
                def _(dve):
                    v = Chain(dve, sv)
                    edge_max, self_max, both, den, own, tmp = (small[:, k, :, :] for k in range(6))
                    a_s, a_d = alphas[:, :, 0:nh], alphas[:, :, nh:2 * nh]
                    any_edge = acc[:, :, F + 2 * nh:F + 2 * nh + 1].broadcast_to([P, NT, nh])
                    v.step(dve.tensor_tensor(self_max, a_s, a_d, ALU.add))
                    v.link(dve.tensor_tensor(edge_max, acc[:, :, F + nh:F + 2 * nh], a_d, ALU.add))
                    v.step(dve.scalar_tensor_tensor(self_max, self_max, NEG_SLOPE, self_max, ALU.mult, ALU.max))
                    v.step(dve.scalar_tensor_tensor(edge_max, edge_max, NEG_SLOPE, edge_max, ALU.mult, ALU.max))
                    v.link(dve.tensor_scalar(tmp, any_edge, -1.0, BIG, ALU.add, ALU.mult))
                    v.link(dve.tensor_tensor(edge_max, edge_max, tmp, ALU.add))
                    v.link(dve.tensor_tensor(both, edge_max, self_max, ALU.max))
                    v.step(dve.tensor_tensor(edge_max, edge_max, both, ALU.subtract))
                    v.link(dve.tensor_tensor(self_max, self_max, both, ALU.subtract))
                    dve.sem_inc(ready, 1)
                    dve.wait_ge(exped, 1)
                    v.link(dve.tensor_tensor(den, acc[:, :, F:F + nh], edge_max, ALU.mult))
                    v.link(dve.tensor_tensor(den, den, self_max, ALU.add))
                    v.link(dve.tensor_scalar(den, den, EPS_DEN, None, ALU.add))
                    v.link(dve.reciprocal(own, den))
                    v.step(dve.tensor_tensor(edge_max, edge_max, own, ALU.mult))
                    v.link(dve.tensor_tensor(self_max, self_max, own, ALU.mult))
                    dve.wait_ge(loaded, 16)
                    work = temps
                    for t in range(NT):
                        accv = acc[:, t, 0:F].rearrange("p (h c) -> p h c", h=nh)
                        hv = h_sb[:, t, :].rearrange("p (h c) -> p h c", h=nh)
                        wv = work[:, t, :].rearrange("p (h c) -> p h c", h=nh)
                        v.step(dve.tensor_tensor(accv, accv, edge_max[:, t, :].unsqueeze(2).broadcast_to([P, nh, ch]), ALU.mult))
                        v.step(dve.tensor_tensor(wv, hv, self_max[:, t, :].unsqueeze(2).broadcast_to([P, nh, ch]), ALU.mult))
                    dve.wait_ge(sv, v.n)
                    v.link(dve.tensor_tensor(work[:, :, :], work[:, :, :], acc[:, :, 0:F], ALU.add))
                    v.link(dve.tensor_tensor(work[:, :, :], work[:, :, :], vec[:, :].unsqueeze(1).broadcast_to([P, NT, F]), ALU.add))
                    finish(v, None, dve, work, finish_sem)

        def put_h(act, t, bank, taken, nh=0, scale=None):
            if scale is None:
                act.activation(h_sb[:, t, :], bank[:, 0:F], ACT.Copy).then_inc(taken, 1)
            else:
                act.activation(h_sb[:, t, :], bank[:, 0:F], ACT.Copy, scale=scale[:, t:t + 1]).then_inc(taken, 1)
            if nh:
                act.activation(alphas[:, t, 0:2 * nh], bank[:, F:F + 2 * nh], ACT.Copy).then_inc(taken, 1)

        def attention_layer(table, nh, temps_scope, bias, finish):
            with ExitStack() as st:
                at_src = sb(st, "at_src", [P, C, nh], fp32)
                at_dst = sb(st, "at_dst", [P, C, nh], fp32)
                look_up(0, nh, at_src)
                look_up(1, nh, at_dst)
                edge_softmax(nh, at_src, at_dst)
            acc = sb(temps_scope, "acc", [P, NT, F + 2 * nh + 1], fp32)
            aggregate(acc, table, gidx_d, local_d, tile_d, nh=nh, aux=edge_aux, n_aux=2 * nh + 1)
            work = sb(temps_scope, "work", [P, NT, F], fp32)
            gat_combine(acc, nh, bias, finish, work)

        with ExitStack() as ls:
            load_weights([a["L0_gnn_weight"]])
            with ExitStack() as fs:
                f_all = sb(fs, "f_all", [P, NT, F], fp32)
                layer_norm(f_all)
                project(f_all, F, lambda act, t, bank, taken: put_h(act, t, bank, taken, scale=norm), 1, tables[0], h_sb)
            acc = sb(ls, "acc", [P, NT, F], fp32)
            aggregate(acc, tables[0], gidx_s, local_s, tile_s, weight=w_s)
            with ExitStack() as st, nc.Block() as block:
                vec = sb(st, "vec", [P, F], fp32)
                loaded = sem(st, "loaded")
                sv = sem(st, "dve_chain")

                @block.sync
                def _(sp):
                    sp.dma_start(vec[:, :], row_broadcast(a["L0_gnn_bias"])).then_inc(loaded, 16)

                @block.vector
                def _(dve):
                    v = Chain(dve, sv)
                    dve.wait_ge(loaded, 16)
                    v.link(dve.tensor_tensor(acc[:, :, :], acc[:, :, :], vec[:, :].unsqueeze(1).broadcast_to([P, NT, F]), ALU.add))
                    v.link(dve.scalar_tensor_tensor(x_sb[:, :, :], acc[:, :, :], 0.0, x_sb[:, :, :], ALU.max, ALU.add))

        with ExitStack() as ls:
            load_weights([a["L1_gnn_W1"]], (a["L1_gnn_att_src1"], a["L1_gnn_att_dst1"]), H)
            with ExitStack() as fs:
                f_all = sb(fs, "f_all", [P, NT, F], fp32)
                layer_norm(f_all)
                project(f_all, F + 2 * H, lambda act, t, bank, taken: put_h(act, t, bank, taken, nh=H), 2, tables[1], h_sb)

            def finish_elu(v, act, dve, work, done):
                if act is not None:
                    act.wait_ge(done, 1)
                    act.activation(h_sb[:, :, :], h_sb[:, :, :], ACT.Exp).then_inc(done, 1)
                else:
                    v.link(dve.tensor_scalar(h_sb[:, :, :], work[:, :, :], 0.0, None, ALU.min))
                    dve.sem_inc(done, 1)
                    v.link(dve.tensor_scalar(work[:, :, :], work[:, :, :], 0.0, -1.0, ALU.max, ALU.add))
                    dve.wait_ge(done, 2)
                    v.link(dve.tensor_tensor(h_sb[:, :, :], work[:, :, :], h_sb[:, :, :], ALU.add))

            with ExitStack() as ts:
                attention_layer(tables[1], H, ts, a["L1_gnn_b1"], finish_elu)

        with ExitStack() as ls:
            load_weights([a["L1_gnn_W2"]], (a["L1_gnn_att_src2"], a["L1_gnn_att_dst2"]), 1)
            with ExitStack() as fs:
                project(h_sb, F + 2, lambda act, t, bank, taken: put_h(act, t, bank, taken, nh=1), 2, tables[2], h_sb)

            def finish_add(v, act, dve, work, done):
                if dve is not None:
                    v.link(dve.tensor_tensor(x_sb[:, :, :], x_sb[:, :, :], work[:, :, :], ALU.add))

            with ExitStack() as ts:
                attention_layer(tables[2], 1, ts, a["L1_gnn_b2"], finish_add)

        with ExitStack() as ls:
            load_weights([a["L2_gnn_W_self"], a["L2_gnn_W_neigh"]])
            with ExitStack() as fs:
                neigh = sb(fs, "neigh", [P, NT, F], fp32)
                with ExitStack() as gs:
                    f_all = sb(gs, "f_all", [P, NT, F], fp32)
                    layer_norm(f_all)

                    def put_both(act, t, bank, taken):
                        act.activation(h_sb[:, t, :], bank[:, 0:F], ACT.Copy).then_inc(taken, 1)
                        act.activation(neigh[:, t, :], bank[:, F:2 * F], ACT.Copy).then_inc(taken, 1)

                    project(f_all, 2 * F, put_both, 2, None, None)
                with ExitStack() as st, nc.Block() as block:
                    best = sb(st, "best", [P, 2, 8], fp32)
                    left = sb(st, "left", [P, 2, F], fp32)
                    kept = sem(st, "kept")
                    stored = sem(st, "stored")
                    sv = sem(st, "dve_chain")

                    @block.vector
                    def _(dve):
                        v = Chain(dve, sv)
                        for t in range(NT):
                            for r in range(4):
                                of = neigh[:, t, :] if r == 0 else left[:, (r - 1) % 2, :]
                                v.link(dve.max(best[:, t % 2, :], of))
                                v.link(dve.match_replace(left[:, r % 2, :], best[:, t % 2, :], of, -BIG))
                            dve.scalar_tensor_tensor(neigh[:, t, :], left[:, 1, :], -BIG, neigh[:, t, :], ALU.is_le, ALU.mult).then_inc(kept, 1)

                    @block.sync
                    def _(sp):
                        for t in range(0, NT, 5):
                            sp.wait_ge(kept, t + 5)
                            sp.dma_start(tables[3][t * P:(t + 5) * P, :].rearrange("(t p) f -> p t f", p=P), neigh[:, t:t + 5, :]).then_inc(stored, 16)
                        sp.wait_ge(stored, 16 * (NT // 5))
            acc = sb(ls, "acc", [P, NT, F + 1], fp32)
            aggregate(acc, tables[3], gidx_d, local_d, tile_d, n_aux=1)
            with ExitStack() as st, nc.Block() as block:
                deg = sb(st, "deg", [P, NT], fp32)
                sv = sem(st, "dve_chain")

                @block.vector
                def _(dve):
                    v = Chain(dve, sv)
                    v.step(dve.tensor_tensor(x_sb[:, :, :], x_sb[:, :, :], h_sb[:, :, :], ALU.add))
                    v.link(dve.tensor_scalar(deg[:, :], acc[:, :, F], 1.0, None, ALU.max))
                    v.link(dve.reciprocal(deg[:, :], deg[:, :]))
                    for t in range(NT):
                        v.step(dve.scalar_tensor_tensor(x_sb[:, t, :], acc[:, t, 0:F], deg[:, t:t + 1], x_sb[:, t, :], ALU.mult, ALU.add))
                    dve.wait_ge(sv, v.n)

        with ExitStack() as ls:
            load_weights([a["L3_gnn_W"]], (a["L3_gnn_att_src"], a["L3_gnn_att_dst"]), H)
            with ExitStack() as fs:
                f_all = sb(fs, "f_all", [P, NT, F], fp32)
                layer_norm(f_all)
                project(f_all, F + 2 * H, lambda act, t, bank, taken: put_h(act, t, bank, taken, nh=H), 2, tables[4], h_sb)

            def finish_relu(v, act, dve, work, done):
                if dve is not None:
                    v.link(dve.scalar_tensor_tensor(x_sb[:, :, :], work[:, :, :], 0.0, x_sb[:, :, :], ALU.max, ALU.add))

            with ExitStack() as ts:
                attention_layer(tables[4], H, ts, a["L3_gnn_bias"], finish_relu)

        with ExitStack() as st, nc.Block() as block:
            stored = sem(st, "stored")

            @block.sync
            def _(sp):
                sp.dma_start(out[0:(NT - 1) * P, :].rearrange("(t p) f -> p t f", p=P), x_sb[:, 0:NT - 1, :]).then_inc(stored, 16)
                sp.dma_start(out[(NT - 1) * P:N, :], x_sb[0:LAST, NT - 1, :]).then_inc(stored, 16)
                sp.wait_ge(stored, 32)


_INS = ["x", "src", "dst", "edge_weight", "node_vec1", "L0_gnn_weight", "L0_gnn_bias", "L1_gnn_W1", "L1_gnn_att_src1",
        "L1_gnn_att_dst1", "L1_gnn_b1", "L1_gnn_W2", "L1_gnn_att_src2", "L1_gnn_att_dst2", "L1_gnn_b2", "L2_gnn_W_self",
        "L2_gnn_W_neigh", "L3_gnn_W", "L3_gnn_att_src", "L3_gnn_att_dst", "L3_gnn_bias"]


def kernel(**inputs):
    import concourse.bacc as bacc
    from concourse.bass_utils import run_bass_kernel_spmd

    nc = bacc.Bacc("TRN2", target_bir_lowering=False, num_devices=1)
    arrays, args = {}, {}
    for name in _INS:
        array = np.ascontiguousarray(inputs[name])
        arrays[f"in_{name}"] = array
        args[name] = nc.dram_tensor(f"in_{name}", array.shape, mybir.dt.from_np(array.dtype), kind="ExternalInput").ap()
    out = nc.dram_tensor("out_x", arrays["in_x"].shape, fp32, kind="ExternalOutput").ap()
    gnn_kernel(nc, args, out)
    r = run_bass_kernel_spmd(nc, [arrays], core_ids=[0])
    return r.results[0]["out_x"]
```

```python
import numpy as np
import concourse.bass as bass
from concourse import mybir
from contextlib import ExitStack

fp32 = mybir.dt.float32
bf16 = mybir.dt.bfloat16
i32 = mybir.dt.int32
u8 = mybir.dt.uint8
ALU = mybir.AluOpType
ACT = mybir.ActivationFunctionType
X = mybir.AxisListType.X

P = 128
BIG = 1e30
NEG_SLOPE = 0.2
EPS_LN = 1e-5
EPS_DEN = 1e-16


class Chain:

    def __init__(self, engine, sem):
        self.engine, self.sem, self.n = engine, sem, 0

    def step(self, instruction):
        instruction.then_inc(self.sem, 1)
        self.n = self.n + 1

    def link(self, instruction):
        self.step(instruction)
        self.engine.wait_ge(self.sem, self.n)


def gnn_kernel(nc, a, out):
    N, F = a["x"].shape
    E = a["src"].shape[0]
    K2 = F // P
    NT = -(-N // P)
    LAST = N - (NT - 1) * P
    NP = NT * P
    QB = 4
    U = 8
    C = -(-(E + 1) // (P * U)) * U
    Q = C // QB
    EP = C * P
    CX = C + NT - 1
    CX = -(-CX // U) * U
    PAD = NP - 1
    H = a["L1_gnn_att_src1"].shape[0]
    CH = F // H
    AUX = 2 * H + 1
    WX = F + 2 * H
    WMAX = 2 * F
    POS_N = NT * C
    PIECES = 20
    PW = POS_N // PIECES
    GROUP = 8
    RING = 7
    PIECE = GROUP * P
    PN = C // GROUP
    assert PN % RING == 0 and E % P and Q * QB == C and POS_N % PIECES == 0 and PW <= 512 and PAD >= N and C % U == 0

    tables = [nc.dram_tensor(f"table_{n}", (NP, F), fp32, kind="Internal").ap() for n in range(5)]
    records = nc.dram_tensor("records", (EP, 4), fp32, kind="Internal").ap()
    dst_padded = nc.dram_tensor("dst_padded", (EP,), fp32, kind="Internal").ap()
    one_hots = nc.dram_tensor("one_hots", (2, PN, P, PIECE), bf16, kind="Internal").ap()
    low_rows = nc.dram_tensor("low_rows", (2, EP), u8, kind="Internal").ap()

    top = ExitStack()
    names = [0]

    def sb(stack, name, shape, dt):
        names[0] += 1
        return stack.enter_context(nc.sbuf_tensor(f"{name}_{names[0]}", shape, dt))

    def banks(stack, name, n):
        names[0] += 1
        return [stack.enter_context(nc.psum_tensor(f"{name}_{names[0]}_{i}", [P, 512], fp32)) for i in range(n)]

    def sem(stack, name):
        names[0] += 1
        s = stack.enter_context(nc.semaphore(f"{name}_{names[0]}"))
        stack.callback(lambda: nc.sync.sem_clear(s))
        return s

    with top:
        ident = sb(top, "ident", [P, P], fp32)
        iota = sb(top, "iota", [P, P], fp32)
        part = sb(top, "part", [P, 1], fp32)
        ones = sb(top, "ones", [P, P], fp32)
        row0 = sb(top, "row0", [P, P], fp32)
        hot_hi = [sb(top, "hot_hi", [P, NT, C], u8)]
        gidx_d = sb(top, "gidx_d", [P, CX], fp32)
        gidx_s = sb(top, "gidx_s", [P, CX], fp32)
        local_d = sb(top, "local_d", [P, CX], fp32)
        local_s = sb(top, "local_s", [P, CX], fp32)
        w_s = sb(top, "w_s", [P, CX], fp32)
        tile_d = sb(top, "tile_d", [1, CX], i32)
        tile_s = sb(top, "tile_s", [1, CX], i32)
        begin_d = sb(top, "begin_d", [1, NT], i32)
        hot_tile = sb(top, "hot_tile", [NT, CX], bf16)
        is_last = sb(top, "is_last", [P, C], fp32)
        reset_f = sb(top, "reset_f", [Q, H * QB * P], fp32)
        reset_b = sb(top, "reset_b", [Q, H * QB * P], fp32)
        join_f = sb(top, "join_f", [H, C], fp32)
        join_b = sb(top, "join_b", [H, C], fp32)
        gate_f = sb(top, "gate_f", [H, C], fp32)
        gate_b = sb(top, "gate_b", [H, C], fp32)
        hot_begin = sb(top, "hot_begin", [P, NT - 1, P], bf16)

        x_sb = sb(top, "x_sb", [P, NT, F], fp32)
        norm = sb(top, "norm", [P, NT], fp32)
        W_sb = sb(top, "W_sb", [P, K2, WMAX], fp32)

        def row_broadcast(vec, rows=P):
            return vec.partition_broadcast(rows)

        def norm_statistics(v, stats, mv, var, rstd, shift, var_made, dev, dev_made):
            dve = v.engine
            for t in range(NT):
                v.step(dve.bn_stats(stats[:, t, :], x_sb[:, t, :]))
            dve.wait_ge(v.sem, v.n)
            for t in range(NT):
                v.step(dve.bn_aggr(mv[:, t, :], stats[:, t, :]))
            dve.wait_ge(v.sem, v.n)
            dve.tensor_scalar(var[:, :], mv[:, :, 1], EPS_LN, None, ALU.add).then_inc(var_made, 1)
            dve.wait_ge(dev_made, 1)
            v.link(dve.reciprocal(rstd[:, :], dev[:, :]))
            v.link(dve.scalar_tensor_tensor(shift[:, :], mv[:, :, 0], -1.0, rstd[:, :], ALU.mult, ALU.mult))

        slot_done = [top.enter_context(nc.semaphore(f"slot_done{s}")) for s in range(U)]
        slots_used = [0]
        sort_done = top.enter_context(nc.semaphore("sort_done"))

        with ExitStack() as ph, nc.Block() as block:
            made = sem(ph, "made")

            @block.gpsimd
            def _(pool):
                pool.iota(iota[:, :], [[1, P]], 0, 0, allow_small_or_imprecise_dtypes=True).then_inc(made, 1)
                pool.iota(part[:, :], [[0, 1]], 0, 1, allow_small_or_imprecise_dtypes=True).then_inc(made, 1)
                pool.memset(ident[:, :], 0.0).then_inc(made, 1)
                pool.memset(row0[:, :], 0.0).then_inc(made, 1)
                pool.memset(ones[:, :], 1.0).then_inc(made, 1)
                pool.wait_ge(made, 5)
                pool.affine_select(out=ident[:, :], in_=ident[:, :], compare_op=ALU.not_equal, fill=1.0, base=0,
                                   pattern=[[-1, P]], channel_multiplier=1).then_inc(made, 1)
                pool.memset(row0[0:1, :], 1.0).then_inc(made, 1)
                pool.wait_ge(made, 7)

        with ExitStack() as ph:
            rows_i = sb(ph, "rows_i", [Q, 2, QB * P], i32)
            rows_lo = sb(ph, "rows_lo", [Q, 2, QB * P], i32)
            rows_lo8 = sb(ph, "rows_lo8", [Q, 2, QB * P], u8)
            rows_f = sb(ph, "rows_f", [Q, 2, QB * P], fp32)
            rows_w = sb(ph, "rows_w", [Q, QB * P], fp32)
            edge = sb(ph, "edge", [P, 2, C], fp32)
            edge_w = sb(ph, "edge_w", [P, C], fp32)
            edge_i = sb(ph, "edge_i", [P, 2, C], i32)
            hi_i = sb(ph, "hi_i", [P, 2, C], i32)
            hi_f = sb(ph, "hi_f", [P, 2, C], fp32)
            hi_rep = sb(ph, "hi_rep", [P, 2, C], fp32)
            next_first = sb(ph, "next_first", [Q, QB], fp32)
            chunk_first = sb(ph, "chunk_first", [H, C], fp32)
            chunk_last = sb(ph, "chunk_last", [H, C], fp32)
            tile_first = sb(ph, "tile_first", [Q, QB], fp32)
            last_rows = sb(ph, "last_rows", [Q, QB, P], fp32)
            counts = sb(ph, "counts", [P, 2, NT], fp32)
            begins = sb(ph, "begins", [P, 2, NT], fp32)
            begins_i = sb(ph, "begins_i", [P, 2, NT], i32)
            begin_i = sb(ph, "begin_i", [P, 2, NT], i32)
            begin_f = sb(ph, "begin_f", [P, 2, NT], fp32)
            within = sb(ph, "within", [P, 2, NT], fp32)
            to_local = sb(ph, "to_local", [P, 2, NT - 1], fp32)
            chunk_of_row = sb(ph, "chunk_of_row", [Q, QB], fp32)
            begin_pick = sb(ph, "begin_pick", [Q, 2, QB, NT], fp32)
            record = sb(ph, "record", [P, C, 4], fp32)
            rank = sb(ph, "rank", [P, C], fp32)
            rank_i = sb(ph, "rank_i", [P, C], i32)

            hot_hi.append(sb(ph, "hot_hi_d", [P, NT, C], u8))
            unsorted = sb(ph, "unsorted", [1, 1], i32)
            with ExitStack() as st, nc.Block() as block:
                ps = banks(st, "load", 1)
                order = sb(st, "order", [Q, QB, P + 1], i32)
                falls = sb(st, "falls", [Q, QB, P], fp32)
                falls_row = sb(st, "falls_row", [Q, 1], fp32)
                cleared = sem(st, "cleared")
                loaded = sem(st, "loaded")
                counted = sem(st, "counted")
                summed = sem(st, "summed")
                sv = sem(st, "dve_chain")

                @block.sync
                def _(sp):
                    sp.wait_ge(cleared, 3)
                    full = E // P
                    for what, tile in (("src", rows_i[:, 0, :]), ("dst", rows_i[:, 1, :]), ("edge_weight", rows_w[:, :])):
                        for b in range(QB):
                            n = min(Q, full - b * Q)
                            sp.dma_start(tile[0:n, b * P:(b + 1) * P],
                                         a[what][b * Q * P:(b * Q + n) * P].rearrange("(q p) -> q p", p=P)).then_inc(loaded, 16)
                        r = full - (QB - 1) * Q
                        sp.dma_start(tile[r:r + 1, (QB - 1) * P:(QB - 1) * P + E - full * P],
                                     a[what][full * P:E].rearrange("(o p) -> o p", o=1)).then_inc(loaded, 16)
                    for b in range(QB):
                        n = min(Q, full - b * Q)
                        src = a["dst"]
                        sp.dma_start(order[0:n, b, :], bass.AP(src.tensor, src.offset + b * Q * P, [[P, n], [1, P + 1]])).then_inc(loaded, 16)
                    sp.dma_start(order[r:r + 1, QB - 1, 0:E - full * P],
                                 a["dst"][full * P:E].rearrange("(o p) -> o p", o=1)).then_inc(loaded, 16)

                @block.vector
                def _(dve):
                    v = Chain(dve, sv)
                    dve.memset(rows_i[:, :, :], PAD).then_inc(cleared, 1)
                    dve.memset(rows_w[:, :], 0.0).then_inc(cleared, 1)
                    dve.memset(order[:, :, :], PAD).then_inc(cleared, 1)
                    dve.wait_ge(loaded, 20 * 16)
                    v.link(dve.tensor_tensor(falls[:, :, :], order[:, :, 1:P + 1], order[:, :, 0:P], ALU.is_lt))
                    dve.tensor_reduce(falls_row[:, :], falls[:, :, :], mybir.AxisListType.XY, ALU.add).then_inc(counted, 1)
                    dve.wait_ge(summed, 1)
                    v.link(dve.tensor_scalar(unsorted[:, :], ps[0][0:1, 0:1], 1.0, None, ALU.min))

                @block.tensor
                def _(pe):
                    pe.wait_ge(counted, 1)
                    nc.tensor.matmul(ps[0][0:1, 0:1], falls_row[:, :], ones[0:Q, 0:1], start=True, stop=True).then_inc(summed, 1)

            with ExitStack() as st, nc.Block() as block:
                KN = 14
                KP = EP // KN
                COLS = QB * P
                keys = sb(st, "keys", [Q, KP], fp32)
                place_in = sb(st, "place_in", [Q, KP], fp32)
                same = sb(st, "same", [Q, KP], fp32)
                own = sb(st, "own", [Q, COLS], fp32)
                own_in = sb(st, "own_in", [Q, COLS], fp32)
                below = sb(st, "below", [Q, 2, COLS], fp32)
                rank_d = sb(st, "rank", [Q, COLS], fp32)
                rank_di = sb(st, "rank_di", [Q, COLS], i32)
                rec = sb(st, "rec", [Q, COLS, 4], fp32)
                i_slot = sb(st, "i_slot", [Q, 1], i32)
                r_slot = sb(st, "r_slot", [Q, 4], fp32)
                cast = sem(st, "cast")
                stored = sem(st, "stored")
                keys_in = sem(st, "keys_in")
                keys_used = sem(st, "keys_used")
                places = sem(st, "places")
                ranked = sem(st, "ranked")
                staged = sem(st, "staged")
                scattered = sem(st, "scattered")
                back = sem(st, "back")
                sv = sem(st, "dve_chain")

                @block.sync
                def _(sp):
                    with sp.If(sp.value_load(unsorted[0:1, 0:1], min_val=0, max_val=1)):
                        sp.wait_ge(cast, 1)
                        sp.dma_start(dst_padded.rearrange("(b q p) -> q b p", b=QB, p=P),
                                     rows_f[:, 1, :].rearrange("q (b p) -> q b p", p=P)).then_inc(stored, 16)
                        sp.wait_ge(stored, 16)
                        for n in range(KN):
                            if n:
                                sp.wait_ge(keys_used, n)
                            sp.dma_start(keys[:, :], dst_padded[n * KP:(n + 1) * KP].partition_broadcast(Q)).then_inc(keys_in, 16)
                        sp.wait_ge(scattered, 1)
                        sp.dma_start(rec[:, :, :].rearrange("q (b p) k -> q b (p k)", p=P),
                                     records.rearrange("(b q p) k -> q b (p k)", b=QB, p=P)).then_inc(back, 16)

                @block.gpsimd
                def _(pool):
                    with pool.If(pool.value_load(unsorted[0:1, 0:1], min_val=0, max_val=1)):
                        pool.iota(place_in[:, :], [[1, KP]], 0, 0, allow_small_or_imprecise_dtypes=True).then_inc(places, 1)
                        pool.iota(own[:, :], [[Q * P, QB], [1, P]], 0, P, allow_small_or_imprecise_dtypes=True).then_inc(places, 1)
                        pool.wait_ge(ranked, 1)
                        with pool.Fori(0, COLS) as j:
                            pool.tensor_copy(i_slot[:, :], rank_di[:, bass.ds(j, 1)]).then_inc(staged, 1)
                            pool.tensor_copy(r_slot[:, :].unsqueeze(1), rec[:, bass.ds(j, 1), :]).then_inc(staged, 1)
                            pool.wait_ge(staged, 2 * j + 2)
                            pool.nop(nofuse=True)
                            pool.indirect_dma_start(out=records, out_offset=bass.IndirectOffsetOnAxis(ap=i_slot[:, :], axis=0),
                                                    in_=r_slot[:, :], in_offset=None).then_inc(sort_done, 16)
                            pool.wait_ge(sort_done, 16 * j + 16)
                        pool.sem_inc(scattered, 1)

                @block.vector
                def _(dve):
                    with dve.If(dve.value_load(unsorted[0:1, 0:1], min_val=0, max_val=1)):
                        v = Chain(dve, sv)
                        dve.tensor_copy(rows_f[:, :, :], rows_i[:, :, :]).then_inc(cast, 1)
                        dve.wait_ge(cast, 1)
                        v.step(dve.tensor_copy(rec[:, :, 0], rows_f[:, 1, :]))
                        v.step(dve.tensor_copy(rec[:, :, 1], rows_w[:, :]))
                        v.step(dve.tensor_copy(rec[:, :, 2], rows_f[:, 0, :]))
                        v.step(dve.memset(rec[:, :, 3], 0.0))
                        v.link(dve.memset(rank_d[:, :], 0.0))
                        dve.wait_ge(places, 2)
                        for n in range(KN):
                            dve.wait_ge(keys_in, 16 * (n + 1))
                            v.link(dve.tensor_scalar(own_in[:, :], own[:, :], -float(n * KP), None, ALU.add))
                            base = v.n
                            with dve.Fori(0, COLS) as j:
                                v.n = base + 3 * j
                                key = rows_f[:, 1, bass.ds(j, 1)]
                                v.link(dve.tensor_scalar(same[:, :], keys[:, :], key, None, ALU.is_lt, ALU.add,
                                                         accum_out=below[:, 0, bass.ds(j, 1)]))
                                v.link(dve.tensor_scalar(same[:, :], keys[:, :], key, None, ALU.is_equal))
                                v.link(dve.scalar_tensor_tensor(same[:, :], place_in[:, :], own_in[:, bass.ds(j, 1)], same[:, :],
                                                                ALU.is_lt, ALU.mult, accum_out=below[:, 1, bass.ds(j, 1)]))
                            v.n = base + 3 * COLS
                            dve.sem_inc(keys_used, 1)
                            for k in range(2):
                                v.link(dve.tensor_tensor(rank_d[:, :], rank_d[:, :], below[:, k, :], ALU.add))
                        v.link(dve.tensor_copy(rank_di[:, :], rank_d[:, :]))
                        dve.sem_inc(ranked, 1)
                        dve.wait_ge(back, 16)
                        v.step(dve.tensor_copy(rows_i[:, 0, :], rec[:, :, 2]))
                        v.step(dve.tensor_copy(rows_i[:, 1, :], rec[:, :, 0]))
                        v.link(dve.tensor_copy(rows_w[:, :], rec[:, :, 1]))

            with ExitStack() as st, nc.Block() as block:
                ps = banks(st, "edges", 6)
                cleared = sem(st, "cleared")
                loaded = sem(st, "loaded")
                cast = sem(st, "cast")
                turned = sem(st, "turned")
                stored = sem(st, "stored")
                looked = sem(st, "looked")
                spread = sem(st, "spread")
                last_made = sem(st, "last_made")
                picks_made = sem(st, "picks_made")
                picked = sem(st, "picked")
                rows_known = sem(st, "rows_known")
                runs_cleared = sem(st, "runs_cleared")
                sv = sem(st, "dve_chain")
                counted = sem(st, "counted")

                @block.gpsimd
                def _(pool):
                    pool.iota(chunk_of_row[:, :], [[Q, QB]], 0, 1, allow_small_or_imprecise_dtypes=True).then_inc(rows_known, 1)
                    for runs in (reset_f, reset_b, join_f, join_b):
                        pool.memset(runs[:, :], -BIG).then_inc(runs_cleared, 1)
                    pool.memset(record[:, :, 3], 0.0)

                @block.sync
                def _(sp):
                    sp.wait_ge(cast, 2)
                    sp.dma_start(dst_padded.rearrange("(b q p) -> q b p", b=QB, p=P),
                                 rows_f[:, 1, :].rearrange("q (b p) -> q b p", p=P)).then_inc(stored, 16)
                    for w in range(2):
                        sp.dma_start(low_rows[w, :].rearrange("(b q p) -> q b p", b=QB, p=P),
                                     rows_lo8[:, w, :].rearrange("q (b p) -> q b p", p=P)).then_inc(stored, 16)
                    sp.wait_ge(stored, 48)
                    sp.wait_ge(cleared, 1)
                    with nc.allow_non_contiguous_dma(reason="one value per chunk"):
                        firsts = dst_padded.rearrange("(c p) -> p c", p=P)[0:1, :]
                        lasts = dst_padded.rearrange("(c p) -> p c", p=P)[P - 1:P, :]
                        for h in range(H):
                            sp.dma_start(chunk_first[h:h + 1, :], firsts).then_inc(looked, 16)
                            sp.dma_start(chunk_last[h:h + 1, :], lasts).then_inc(looked, 16)
                        for b in range(QB):
                            n = Q if b < QB - 1 else Q - 1
                            at = b * Q + 1
                            sp.dma_start(next_first[0:n, b:b + 1],
                                         dst_padded.rearrange("(c p) -> c p", p=P)[at:at + n, 0:1]).then_inc(looked, 16)

                @block.vector
                def _(dve):
                    v = Chain(dve, sv)
                    dve.memset(next_first[:, :], -1.0).then_inc(cleared, 1)
                    v.link(dve.tensor_scalar(rows_lo[:, :, :], rows_i[:, :, :], P - 1, None, ALU.bitwise_and))
                    v.step(dve.tensor_copy(rows_lo8[:, 0, :], rows_lo[:, 0, :]))
                    v.step(dve.tensor_copy(tile_first[:, :], rows_lo[:, 1, :].rearrange("q (b p) -> q b p", p=P)[:, :, 0]))
                    dve.tensor_copy(rows_f[:, :, :], rows_i[:, :, :]).then_inc(cast, 1)
                    dve.wait_ge(cast, 1)
                    dve.wait_ge(sv, v.n)
                    to = rows_f[:, 1, :].rearrange("q (b p) -> q b p", p=P)
                    v.link(dve.tensor_tensor(tile_first[:, :], to[:, :, 0], tile_first[:, :], ALU.subtract))
                    v.link(dve.tensor_tensor(last_rows[:, :, :], to, tile_first[:, :].unsqueeze(2).broadcast_to([Q, QB, P]), ALU.subtract))
                    dve.tensor_scalar(rows_lo8[:, 1, :].rearrange("q (b p) -> q b p", p=P), last_rows[:, :, :], 255.0, None,
                                      ALU.min).then_inc(cast, 1)
                    dve.wait_ge(cast, 2)
                    dve.wait_ge(turned, 3)
                    v.step(dve.tensor_copy(edge[:, 0, :], ps[0][:, 0:C]))
                    v.step(dve.tensor_copy(edge[:, 1, :], ps[1][:, 0:C]))
                    v.link(dve.tensor_copy(edge_w[:, :], ps[2][:, 0:C]))
                    v.link(dve.tensor_copy(edge_i[:, :, :], edge[:, :, :]))
                    v.link(dve.tensor_scalar(hi_i[:, :, :], edge_i[:, :, :], 7, None, ALU.logical_shift_right))
                    v.link(dve.tensor_copy(hi_f[:, :, :], hi_i[:, :, :]))
                    for w in range(2):
                        for t in range(NT):
                            v.step(dve.tensor_scalar(hot_hi[w][:, t, :], hi_f[:, w, :], float(t), None, ALU.is_equal, ALU.add,
                                                     accum_out=counts[:, w, t:t + 1]))
                    v.link(dve.tensor_copy(tile_d[:, 0:C], hi_i[0:1, 1, :]))
                    dve.sem_inc(counted, 1)
                    v.step(dve.tensor_copy(gidx_d[:, 0:C], edge[:, 0, :]))
                    v.step(dve.tensor_copy(record[:, :, 0], edge[:, 1, :]))
                    v.step(dve.tensor_copy(record[:, :, 1], edge_w[:, :]))
                    v.step(dve.tensor_copy(record[:, :, 2], edge[:, 0, :]))
                    dve.wait_ge(spread, 1)
                    for w in range(2):
                        v.link(dve.tensor_tensor_scan(begins[:, w, :], ones[:, 0:NT], ps[3][:, w * NT:(w + 1) * NT], 0.0,
                                                      ALU.mult, ALU.add))
                    v.link(dve.tensor_copy(begins_i[:, :, :], begins[:, :, :]))
                    v.step(dve.tensor_scalar(begin_d[:, :], begins_i[0:1, 1, :], 7, None, ALU.logical_shift_right))
                    v.link(dve.tensor_scalar(begin_i[:, :, :], begins_i[:, :, :], 7, None, ALU.logical_shift_right))
                    v.step(dve.tensor_copy(begin_f[:, :, :], begin_i[:, :, :]))
                    v.link(dve.tensor_scalar(begins_i[:, :, :], begins_i[:, :, :], P - 1, None, ALU.bitwise_and))
                    v.link(dve.tensor_copy(within[:, :, :], begins_i[:, :, :]))
                    v.link(dve.tensor_scalar(within[:, :, :], within[:, :, :], 0.0, -2.0 * NP, ALU.is_equal, ALU.mult))
                    for w in range(2):
                        v.step(dve.scalar_tensor_tensor(to_local[:, w, :], iota[:, 1:NT], -float(P), within[:, w, 0:NT - 1], ALU.mult, ALU.add))
                    dve.wait_ge(rows_known, 1)
                    for w in range(2):
                        for b in range(QB):
                            v.step(dve.tensor_scalar(begin_pick[:, w, b, :], begin_f[0:Q, w, :], chunk_of_row[:, b:b + 1], None, ALU.is_equal))
                    dve.wait_ge(sv, v.n)
                    dve.sem_inc(picks_made, 1)
                    for col, empty in ((gidx_d, 0.0), (local_d, -1.0), (gidx_s, 0.0), (local_s, -1.0), (w_s, 0.0), (tile_d, 0), (tile_s, 0)):
                        v.step(dve.memset(col[:, C:CX], empty))
                    v.link(dve.memset(hot_tile[:, C:CX], 0.0))
                    v.step(dve.tensor_copy(tile_d[:, C:C + NT - 1], iota[0:1, 1:NT]))
                    v.step(dve.tensor_copy(tile_s[:, C:C + NT - 1], iota[0:1, 1:NT]))
                    v.step(dve.tensor_scalar(hot_tile[:, C:C + NT - 1], iota[0:NT, 1:NT], part[0:NT, 0:1], None, ALU.is_equal))
                    v.link(dve.tensor_copy(hi_rep[:, 1, :], ps[4][:, 0:C]))
                    v.step(dve.tensor_scalar(hot_tile[:, 0:C], hi_rep[0:NT, 1, :], part[0:NT, 0:1], None, ALU.is_equal))
                    v.step(dve.scalar_tensor_tensor(local_d[:, 0:C], hi_rep[:, 1, :], -float(P), edge[:, 1, :], ALU.mult, ALU.add))
                    dve.wait_ge(runs_cleared, 4)
                    rf = reset_f[:, :].rearrange("q (h r p) -> q h r p", h=H, p=P)
                    rb = reset_b[:, :].rearrange("q (h r p) -> q h r p", h=H, p=P)
                    d = rows_f[:, 1, :].rearrange("q (b p) -> q b p", p=P)
                    v.link(dve.tensor_tensor(rf[:, 0, :, 1:P], d[:, :, 1:P], d[:, :, 0:P - 1], ALU.is_equal))
                    v.step(dve.tensor_scalar(last_rows[:, :, 0:P - 1], rf[:, 0, :, 1:P], -1.0, 1.0, ALU.mult, ALU.add))
                    v.link(dve.tensor_scalar(rb[:, 0, :, 0:P - 1], rf[:, 0, :, 1:P], -1.0, BIG, ALU.add, ALU.mult))
                    v.link(dve.tensor_copy(rf[:, 0, :, 1:P], rb[:, 0, :, 0:P - 1]))
                    for h in range(1, H):
                        v.step(dve.tensor_copy(rf[:, h, :, :], rf[:, 0, :, :]))
                        v.step(dve.tensor_copy(rb[:, h, :, :], rb[:, 0, :, :]))
                    dve.wait_ge(looked, (2 * H + QB) * 16)
                    v.link(dve.tensor_tensor(last_rows[:, :, P - 1], d[:, :, P - 1], next_first[:, :], ALU.is_equal))
                    v.link(dve.tensor_scalar(last_rows[:, :, P - 1], last_rows[:, :, P - 1], -1.0, 1.0, ALU.mult, ALU.add))
                    dve.sem_inc(last_made, 1)
                    v.link(dve.tensor_tensor(join_f[:, 1:C], chunk_first[:, 1:C], chunk_last[:, 0:C - 1], ALU.is_equal))
                    v.link(dve.tensor_scalar(join_b[:, 0:C - 1], join_f[:, 1:C], -1.0, BIG, ALU.add, ALU.mult))
                    v.link(dve.tensor_copy(join_f[:, 1:C], join_b[:, 0:C - 1]))
                    v.link(dve.tensor_tensor(gate_f[:, :], chunk_first[:, :], chunk_last[:, :], ALU.is_equal))
                    v.link(dve.tensor_scalar(gate_b[:, :], gate_f[:, :], -1.0, BIG, ALU.add, ALU.mult))
                    v.link(dve.tensor_tensor(gate_f[:, :], gate_b[:, :], join_f[:, :], ALU.add))
                    v.link(dve.tensor_tensor(gate_b[:, :], gate_b[:, :], join_b[:, :], ALU.add))
                    dve.wait_ge(picked, 1)
                    v.step(dve.tensor_copy(gidx_d[:, C:C + NT - 1], ps[5][:, 0:NT - 1]))
                    v.step(dve.tensor_tensor(local_d[:, C:C + NT - 1], ps[5][:, NT:2 * NT - 1], to_local[:, 1, :], ALU.add))
                    dve.wait_ge(turned, 4)
                    v.link(dve.tensor_copy(is_last[:, :], ps[0][:, 0:C]))

                @block.tensor
                def _(pe):
                    pe.wait_ge(cast, 2)
                    for n, rows in enumerate((rows_f[:, 0, :], rows_f[:, 1, :], rows_w[:, :])):
                        for b in range(QB):
                            last = nc.tensor.transpose(ps[n][:, b * Q:(b + 1) * Q], rows[:, b * P:(b + 1) * P], ident[0:Q, 0:Q])
                        last.then_inc(turned, 1)
                    pe.wait_ge(counted, 1)
                    nc.tensor.matmul(ps[3][:, 0:2 * NT], ones[:, :], counts[:, :, :].rearrange("p w t -> p (w t)"), start=True, stop=True)
                    nc.tensor.matmul(ps[4][:, 0:C], row0[:, :], hi_f[:, 1, :], start=True, stop=True).then_inc(spread, 1)
                    pe.wait_ge(picks_made, 1)
                    for k in range(2):
                        for b in range(QB):
                            last = nc.tensor.matmul(ps[5][:, k * NT:(k + 1) * NT], rows_f[:, k, b * P:(b + 1) * P], begin_pick[:, 1, b, :],
                                                    start=(b == 0), stop=(b == QB - 1))
                    last.then_inc(picked, 1)
                    pe.wait_ge(last_made, 1)
                    for b in range(QB):
                        last = nc.tensor.transpose(ps[0][:, b * Q:(b + 1) * Q], last_rows[:, b, :], ident[0:Q, 0:Q])
                    last.then_inc(turned, 1)

            with ExitStack() as st, nc.Block() as block:
                ps = banks(st, "place", 4)
                hot = sb(st, "hot", [P, NT, C], bf16)
                place = sb(st, "place", [P, NT, C], fp32)
                before = sb(st, "before", [P, P], bf16)
                ones_b = sb(st, "ones_b", [P, P], bf16)
                total = sb(st, "total", [P, 2, PW], fp32)
                hot_made = sem(st, "hot_made")
                const_made = sem(st, "const_made")
                summed = sem(st, "summed")
                sv = sem(st, "dve_chain")
                placed = sem(st, "placed")
                place_masked = sem(st, "place_masked")
                zeroed = sem(st, "zeroed")
                loaded = sem(st, "loaded")

                @block.scalar
                def _(act):
                    act.activation(hot[:, NT // 2:NT, :], hot_hi[0][:, NT // 2:NT, :], ACT.Copy).then_inc(hot_made, 1)

                @block.sync
                def _(sp):
                    sp.dma_start(W_sb[:, :, 0:F], a["L0_gnn_weight"].rearrange("(k p) f -> p k f", p=P)).then_inc(loaded, 16)
                    sp.wait_ge(zeroed, 2)
                    sp.dma_start(x_sb[:, 0:NT - 1, :], a["x"][0:(NT - 1) * P, :].rearrange("(t p) f -> p t f", p=P)).then_inc(loaded, 16)
                    sp.dma_start(x_sb[0:LAST, NT - 1, :], a["x"][(NT - 1) * P:N, :]).then_inc(loaded, 16)
                    with nc.allow_non_contiguous_dma(reason="one value per node"):
                        sp.dma_start(norm[:, 0:NT - 1], a["node_vec1"][0:(NT - 1) * P, :].rearrange("(t p) o -> p (t o)", p=P)).then_inc(loaded, 16)
                        sp.dma_start(norm[0:LAST, NT - 1:NT], a["node_vec1"][(NT - 1) * P:N, :]).then_inc(loaded, 16)
                    sp.wait_ge(loaded, 80)

                @block.gpsimd
                def _(pool):
                    pool.memset(x_sb[:, NT - 1, :], 0.0).then_inc(zeroed, 1)
                    pool.memset(norm[:, :], 0.0).then_inc(zeroed, 1)
                    pool.memset(ones_b[:, :], 1.0).then_inc(const_made, 1)
                    pool.memset(before[:, :], -1.0).then_inc(const_made, 1)
                    pool.wait_ge(const_made, 2)
                    pool.affine_select(out=before[:, :], in_=before[:, :], compare_op=ALU.is_ge, fill=0.0, base=0,
                                       pattern=[[-1, P]], channel_multiplier=1).then_inc(const_made, 1)
                    flat, own = (tile[:, :, :].rearrange("p t c -> p (t c)") for tile in (place, hot))
                    pool.wait_ge(hot_made, 2)
                    for n in range(PIECES):
                        pool.wait_ge(placed, n + 1)
                        piece = flat[:, n * PW:(n + 1) * PW]
                        pool.tensor_tensor(piece, piece, own[:, n * PW:(n + 1) * PW], ALU.mult).then_inc(place_masked, 1)

                @block.tensor
                def _(pe):
                    pe.wait_ge(const_made, 3)
                    pe.wait_ge(hot_made, 2)
                    flat = hot[:, :, :].rearrange("p t c -> p (t c)")
                    for n in range(PIECES):
                        if n >= 2:
                            pe.wait_ge(placed, n - 1)
                        piece = flat[:, n * PW:(n + 1) * PW]
                        nc.tensor.matmul(ps[n % 2][:, 0:PW], ones_b[:, :], piece, start=True, stop=True)
                        nc.tensor.matmul(ps[2 + n % 2][:, 0:PW], before[:, :], piece, start=True, stop=True).then_inc(summed, 1)

                @block.vector
                def _(dve):
                    v = Chain(dve, sv)
                    dve.tensor_copy(hot[:, 0:NT // 2, :], hot_hi[0][:, 0:NT // 2, :]).then_inc(hot_made, 1)
                    flat = place[:, :, :].rearrange("p t c -> p (t c)")
                    for n in range(PIECES):
                        dve.wait_ge(summed, n + 1)
                        start = 0.0 if n == 0 else total[:, (n - 1) % 2, PW - 1:PW]
                        v.link(dve.tensor_tensor_scan(total[:, n % 2, :], ones[:, 0:1].broadcast_to([P, PW]), ps[n % 2][:, 0:PW], start,
                                                      ALU.mult, ALU.add))
                        v.step(dve.tensor_tensor(flat[:, n * PW:(n + 1) * PW], total[:, n % 2, :], ps[2 + n % 2][:, 0:PW], ALU.add))
                        dve.wait_ge(sv, v.n)
                        dve.sem_inc(placed, 1)
                    dve.wait_ge(place_masked, PIECES)
                    v.link(dve.tensor_reduce(rank[:, :], place[:, :, :].rearrange("p t c -> p c t"), X, ALU.add))
                    v.link(dve.tensor_copy(rank_i[:, :], rank[:, :]))

            with ExitStack() as st, nc.Block() as block:
                r_slot = sb(st, "r_slot", [P, U, 4], fp32)
                i_slot = sb(st, "i_slot", [P, U], i32)
                staged = sem(st, "staged")
                low = sb(st, "low", [P, RING, PIECE], u8)
                hot = sb(st, "hot", [P, RING, PIECE], bf16)
                low_in = [sem(st, f"low_in{r}") for r in range(RING)]
                hot_made = sem(st, "hot_made")
                hot_out = [sem(st, f"hot_out{r}") for r in range(RING)]
                stats = sb(st, "stats", [P, NT, 6], fp32)
                mv = sb(st, "mv", [P, NT, 2], fp32)
                var = sb(st, "var", [P, NT], fp32)
                dev = sb(st, "dev", [P, NT], fp32)
                rstd = sb(st, "rstd", [P, NT], fp32)
                shift = sb(st, "shift", [P, NT], fp32)
                normed = sb(st, "normed", [P, 3, F], fp32)
                f_t = sb(st, "f_t", [P, 2, F], fp32)
                STEP = 5
                rows_out = sb(st, "rows_out", [P, 2 * STEP, F], fp32)
                ps_t = banks(st, "turn", 2)
                ps_h = banks(st, "prod", 2)
                var_made = sem(st, "var_made")
                dev_made = sem(st, "dev_made")
                norm_made = sem(st, "norm_made")
                turned = sem(st, "turned")
                f_ready = sem(st, "f_ready")
                product = sem(st, "product")
                taken = sem(st, "taken")
                stored = [sem(st, f"stored{k}") for k in range(2)]
                sv = sem(st, "dve_chain")
                TURNS = 2 * PN // RING

                @block.vector
                def _(dve):
                    v = Chain(dve, sv)
                    norm_statistics(v, stats, mv, var, rstd, shift, var_made, dev, dev_made)
                    for t in range(NT + 3):
                        if t < NT:
                            if t >= 3:
                                dve.wait_ge(turned, t - 2)
                            dve.tensor_scalar(normed[:, t % 3, :], x_sb[:, t, :], rstd[:, t:t + 1], shift[:, t:t + 1],
                                              ALU.mult, ALU.add).then_inc(norm_made, 1)
                        if 1 <= t <= NT:
                            u = t - 1
                            dve.wait_ge(turned, u + 1)
                            if u >= 2:
                                dve.wait_ge(product, u - 1)
                            dve.tensor_scalar(f_t[:, u % 2, :], ps_t[u % 2][:, 0:F], 0.0, None, ALU.max).then_inc(f_ready, 1)
                        if t >= 3:
                            u = t - 3
                            dve.wait_ge(product, u + 1)
                            if u >= 2 * STEP and u % STEP == 0:
                                dve.wait_ge(stored[u // STEP % 2], 16 * (u // STEP // 2))
                            dve.tensor_scalar(rows_out[:, u % (2 * STEP), :], ps_h[u % 2][:, 0:F], norm[:, u:u + 1], None,
                                              ALU.mult).then_inc(taken, 1)

                    def one_hot(r):
                        dve.tensor_scalar(hot[:, r, :], low[:, r, :], part[:, 0:1], None, ALU.is_equal).then_inc(hot_made, 1)

                    for r in range(RING):
                        dve.wait_ge(low_in[r], 16)
                        one_hot(r)
                    with dve.Fori(1, TURNS) as i:
                        for r in range(RING):
                            dve.wait_ge(low_in[r], 16 * i + 16)
                            dve.wait_ge(hot_out[r], 16 * i)
                            one_hot(r)

                @block.tensor
                def _(pe):
                    def turn(t):
                        if t >= 2:
                            pe.wait_ge(f_ready, t - 1)
                        pe.wait_ge(norm_made, t + 1)
                        for k in range(K2):
                            last = nc.tensor.transpose(ps_t[t % 2][:, k * P:(k + 1) * P], normed[:, t % 3, k * P:(k + 1) * P], ident[:, :])
                        last.then_inc(turned, 1)

                    turn(0)
                    for t in range(NT):
                        if t + 1 < NT:
                            turn(t + 1)
                        pe.wait_ge(f_ready, t + 1)
                        if t >= 2:
                            pe.wait_ge(taken, t - 1)
                        for k in range(K2):
                            last = nc.tensor.matmul(ps_h[t % 2][:, 0:F], f_t[:, t % 2, k * P:(k + 1) * P], W_sb[:, k, 0:F],
                                                    start=(k == 0), stop=(k == K2 - 1))
                        last.then_inc(product, 1)

                @block.sync
                def _(sp):
                    low_pieces = low_rows.rearrange("w (n e) -> (w n) e", e=PIECE)
                    hot_pieces = one_hots.rearrange("w n p e -> (w n) p e")

                    def load(n, r):
                        sp.dma_start(low[:, r, :], row_broadcast(low_pieces[bass.ds(n, 1), :].rearrange("o e -> (o e)"))).then_inc(low_in[r], 16)

                    def store(n, r):
                        sp.wait_ge(hot_made, n + 1)
                        sp.dma_start(hot_pieces[bass.ds(n, 1), :, :].rearrange("o p e -> p (o e)"), hot[:, r, :]).then_inc(hot_out[r], 16)

                    for r in range(RING):
                        load(r, r)
                    for t in range(0, NT, STEP):
                        sp.wait_ge(taken, t + STEP)
                        sp.dma_start(tables[0][t * P:(t + STEP) * P, :].rearrange("(t p) f -> p t f", p=P),
                                     rows_out[:, t % (2 * STEP):t % (2 * STEP) + STEP, :]).then_inc(stored[t // STEP % 2], 16)
                    with sp.Fori(0, TURNS - 1) as i:
                        for r in range(RING):
                            store(RING * i + r, r)
                            load(RING * i + r + RING, r)
                    for r in range(RING):
                        store(RING * (TURNS - 1) + r, r)
                    for r in range(RING):
                        sp.wait_ge(hot_out[r], 16 * TURNS)
                    for k in range(2):
                        sp.wait_ge(stored[k], 16 * ((NT // STEP + 1 - k) // 2))

                @block.scalar
                def _(act):
                    def stage(s, c):
                        act.activation(i_slot[:, s:s + 1], rank_i[:, bass.ds(c, 1)], ACT.Copy).then_inc(staged, 1)
                        act.activation(r_slot[:, s:s + 1, :], record[:, bass.ds(c, 1), :], ACT.Copy).then_inc(staged, 1)

                    for s in range(U):
                        stage(s, s)
                    act.wait_ge(var_made, 1)
                    act.activation(dev[:, :], var[:, :], ACT.Sqrt).then_inc(dev_made, 1)
                    with act.Fori(1, C // U) as i:
                        for s in range(U):
                            act.wait_ge(slot_done[s], 16 * i)
                            stage(s, U * i + s)

                @block.gpsimd
                def _(pool):
                    with pool.Fori(0, C // U) as i:
                        for s in range(U):
                            pool.wait_ge(staged, 2 * U * i + 2 * s + 2)
                            pool.nop(nofuse=True)
                            pool.indirect_dma_start(out=records, out_offset=bass.IndirectOffsetOnAxis(ap=i_slot[:, s:s + 1], axis=0),
                                                    in_=r_slot[:, s, :], in_offset=None).then_inc(slot_done[s], 16)
                    for s in range(U):
                        pool.wait_ge(slot_done[s], 16 * (C // U))

            slots_used[0] += C // U
            with ExitStack() as st, nc.Block() as block:
                ps = banks(st, "back", 5)
                rec_rows = sb(st, "rec_rows", [Q, QB, P, 4], fp32)
                back = sem(st, "back")
                turned = sem(st, "turned")
                hi_made = sem(st, "hi_made")
                spread = sem(st, "spread")
                picked = sem(st, "picked")
                sv = sem(st, "dve_chain")

                @block.sync
                def _(sp):
                    sp.dma_start(rec_rows[:, :, :, :].rearrange("q b p k -> q b (p k)"),
                                 records.rearrange("(b q p) k -> q b (p k)", b=QB, p=P)).then_inc(back, 16)

                @block.tensor
                def _(pe):
                    pe.wait_ge(back, 16)
                    for k in range(3):
                        for b in range(QB):
                            last = nc.tensor.transpose(ps[k][:, b * Q:(b + 1) * Q], rec_rows[:, b, :, k], ident[0:Q, 0:Q])
                    last.then_inc(turned, 1)
                    for k in range(3):
                        for b in range(QB):
                            last = nc.tensor.matmul(ps[4][:, k * NT:(k + 1) * NT], rec_rows[:, b, :, k], begin_pick[:, 0, b, :],
                                                    start=(b == 0), stop=(b == QB - 1))
                    last.then_inc(picked, 1)
                    pe.wait_ge(hi_made, 1)
                    nc.tensor.matmul(ps[3][:, 0:C], row0[:, :], hi_f[:, 0, :], start=True, stop=True).then_inc(spread, 1)

                @block.vector
                def _(dve):
                    v = Chain(dve, sv)
                    dve.wait_ge(turned, 1)
                    v.step(dve.tensor_copy(gidx_s[:, 0:C], ps[0][:, 0:C]))
                    v.step(dve.tensor_copy(w_s[:, 0:C], ps[1][:, 0:C]))
                    v.step(dve.tensor_copy(edge[:, 0, :], ps[2][:, 0:C]))
                    v.link(dve.tensor_copy(edge_i[:, 0, :], ps[2][:, 0:C]))
                    v.link(dve.tensor_scalar(hi_i[:, 0, :], edge_i[:, 0, :], 7, None, ALU.logical_shift_right))
                    v.link(dve.tensor_copy(hi_f[:, 0, :], hi_i[:, 0, :]))
                    dve.sem_inc(hi_made, 1)
                    v.step(dve.tensor_copy(tile_s[:, 0:C], hi_i[0:1, 0, :]))
                    dve.wait_ge(spread, 1)
                    v.link(dve.tensor_copy(hi_rep[:, 0, :], ps[3][:, 0:C]))
                    v.link(dve.scalar_tensor_tensor(local_s[:, 0:C], hi_rep[:, 0, :], -float(P), edge[:, 0, :], ALU.mult, ALU.add))
                    dve.wait_ge(picked, 1)
                    v.step(dve.tensor_copy(gidx_s[:, C:C + NT - 1], ps[4][:, 0:NT - 1]))
                    v.step(dve.tensor_copy(w_s[:, C:C + NT - 1], ps[4][:, NT:2 * NT - 1]))
                    v.link(dve.tensor_tensor(local_s[:, C:C + NT - 1], ps[4][:, 2 * NT:3 * NT - 1], to_local[:, 0, :], ALU.add))

        with ExitStack() as st, nc.Block() as block:
            ps = banks(st, "turn", 2)
            hot = sb(st, "hot", [P, 2, 4, P], fp32)
            hot_made = sem(st, "hot_made")
            turned = sem(st, "turned")
            taken = sem(st, "taken")

            @block.vector
            def _(dve):
                for n in range(0, NT - 1, 4):
                    u = n // 4 % 2
                    dve.tensor_tensor(hot[:, u, :, :], iota[:, :].unsqueeze(1).broadcast_to([P, 4, P]),
                                      local_d[:, C + n:C + n + 4].unsqueeze(2).broadcast_to([P, 4, P]), ALU.is_equal).then_inc(hot_made, 1)
                    if n >= 4:
                        dve.wait_ge(turned, n // 4)
                        dve.tensor_copy(hot_begin[:, n - 4:n, :].rearrange("p t e -> p (t e)"), ps[1 - u][:, :]).then_inc(taken, 1)
                dve.wait_ge(turned, (NT - 1) // 4)
                dve.tensor_copy(hot_begin[:, NT - 5:NT - 1, :].rearrange("p t e -> p (t e)"), ps[((NT - 1) // 4 - 1) % 2][:, :]).then_inc(taken, 1)

            @block.tensor
            def _(pe):
                for n in range(0, NT - 1, 4):
                    u = n // 4 % 2
                    pe.wait_ge(hot_made, n // 4 + 1)
                    if n >= 8:
                        pe.wait_ge(taken, n // 4 - 1)
                    for k in range(4):
                        last = nc.tensor.transpose(ps[u][:, k * P:(k + 1) * P], hot[:, u, k, :], ident[:, :])
                    last.then_inc(turned, 1)

        h_sb = sb(top, "h_sb", [P, NT, F], fp32)
        alphas = sb(top, "alphas", [P, NT, 2 * H], fp32)
        edge_aux = sb(top, "edge_aux", [P, CX, AUX], fp32)

        def project(f_of, weights, attention, nh, put, n_puts, table, table_src, after=None):
            cols = len(weights) * F + 2 * nh
            with ExitStack() as st, nc.Block() as block:
                RT = 4
                vec = sb(st, "vec", [P, 2, F], fp32)
                prod = sb(st, "prod", [P, 2, F], fp32)
                stats = sb(st, "stats", [P, NT, 6], fp32)
                mv = sb(st, "mv", [P, NT, 2], fp32)
                var = sb(st, "var", [P, NT], fp32)
                dev = sb(st, "dev", [P, NT], fp32)
                rstd = sb(st, "rstd", [P, NT], fp32)
                shift = sb(st, "shift", [P, NT], fp32)
                normed = sb(st, "normed", [P, RT, F], fp32)
                best = sb(st, "best", [P, 2, 8], fp32)
                left = sb(st, "left", [P, 2, 2, F], fp32)
                ps_t = banks(st, "turn", 2)
                ps_h = banks(st, "prod", 2)
                f_t = sb(st, "f_t", [P, 2, F], fp32)
                loaded = sem(st, "loaded")
                var_made = sem(st, "var_made")
                dev_made = sem(st, "dev_made")
                scale_made = sem(st, "scale_made")
                norm_made = sem(st, "norm_made")
                columns_made = sem(st, "columns_made")
                turned = sem(st, "turned")
                f_ready = sem(st, "f_ready")
                product = sem(st, "product")
                taken = sem(st, "taken")
                finished = sem(st, "finished")
                stored = sem(st, "stored")
                sv = sem(st, "dve_chain")

                @block.sync
                def _(sp):
                    for n, w in enumerate(weights):
                        sp.dma_start(W_sb[:, :, n * F:(n + 1) * F], w.rearrange("(k p) f -> p k f", p=P)).then_inc(loaded, 16)
                    for n, vector in enumerate(attention):
                        sp.dma_start(vec[:, n, :], row_broadcast(vector.rearrange("h c -> (h c)"))).then_inc(loaded, 16)
                    step = 5
                    for t in range(0, NT, step):
                        if after:
                            sp.wait_ge(finished, t + step)
                        else:
                            sp.wait_ge(taken, n_puts * (t + step))
                        sp.dma_start(table[t * P:(t + step) * P, :].rearrange("(t p) f -> p t f", p=P),
                                     table_src[:, t:t + step, :]).then_inc(stored, 16)
                    sp.wait_ge(stored, 16 * (NT // step))

                @block.tensor
                def _(pe):
                    def turn(t):
                        if t >= 2:
                            pe.wait_ge(f_ready, t - 1)
                        if f_of is None:
                            pe.wait_ge(norm_made, t + 1)
                        of = normed[:, t % RT, :] if f_of is None else f_of[:, t, :]
                        for k in range(K2):
                            last = nc.tensor.transpose(ps_t[t % 2][:, k * P:(k + 1) * P], of[:, k * P:(k + 1) * P], ident[:, :])
                        last.then_inc(turned, 1)

                    turn(0)
                    pe.wait_ge(loaded, 16 * (len(weights) + len(attention)))
                    pe.wait_ge(columns_made, 1)
                    for t in range(NT):
                        if t + 1 < NT:
                            turn(t + 1)
                        pe.wait_ge(f_ready, t + 1)
                        if t >= 2:
                            pe.wait_ge(taken, n_puts * (t - 1))
                        for k in range(K2):
                            last = nc.tensor.matmul(ps_h[t % 2][:, 0:cols], f_t[:, t % 2, k * P:(k + 1) * P], W_sb[:, k, 0:cols],
                                                    start=(k == 0), stop=(k == K2 - 1))
                        last.then_inc(product, 1)

                @block.vector
                def _(dve):
                    v = Chain(dve, sv)
                    if f_of is None:
                        norm_statistics(v, stats, mv, var, rstd, shift, var_made, dev, dev_made)
                        dve.sem_inc(scale_made, 1)
                    if attention:
                        dve.wait_ge(loaded, 16 * (len(weights) + len(attention)))
                        for k in range(K2):
                            for n in range(2):
                                v.step(dve.tensor_tensor(prod[:, n, :], W_sb[:, k, 0:F], vec[:, n, :], ALU.mult))
                            dve.wait_ge(sv, v.n)
                            for n in range(2):
                                v.step(dve.tensor_reduce(W_sb[:, k, F + n * nh:F + (n + 1) * nh],
                                                         prod[:, n, :].rearrange("p (h c) -> p h c", h=nh), X, ALU.add))
                            dve.wait_ge(sv, v.n)
                    dve.sem_inc(columns_made, 1)
                    LAG = 2
                    for t in range(NT + LAG):
                        if t < NT and not after:
                            dve.wait_ge(turned, t + 1)
                            if t >= 2:
                                dve.wait_ge(product, t - 1)
                            dve.tensor_copy(f_t[:, t % 2, :], ps_t[t % 2][:, 0:F]).then_inc(f_ready, 1)
                        done = t - LAG
                        if after and done >= 0 and (done % 2 or done == NT - 1):
                            dve.wait_ge(taken, n_puts * (done + 1))
                            after(v, (done - 1, done) if done % 2 else (done,), best, left, finished)

                @block.scalar
                def _(act):
                    if f_of is None:
                        act.wait_ge(var_made, 1)
                        act.activation(dev[:, :], var[:, :], ACT.Sqrt).then_inc(dev_made, 1)
                        act.wait_ge(scale_made, 1)
                    lead = 0 if f_of is not None else RT - 1
                    for t in range(NT + lead):
                        if f_of is None and t < NT:
                            if t >= RT:
                                act.wait_ge(turned, t - RT + 1)
                            act.activation(normed[:, t % RT, :], x_sb[:, t, :], ACT.Relu, bias=shift[:, t:t + 1],
                                           scale=rstd[:, t:t + 1]).then_inc(norm_made, 1)
                        if after and 1 <= t <= NT:
                            u = t - 1
                            act.wait_ge(turned, u + 1)
                            if u >= 2:
                                act.wait_ge(product, u - 1)
                            act.activation(f_t[:, u % 2, :], ps_t[u % 2][:, 0:F], ACT.Copy).then_inc(f_ready, 1)
                        if t >= lead:
                            act.wait_ge(product, t - lead + 1)
                            put(act, t - lead, ps_h[(t - lead) % 2], taken)

                if after:
                    @block.gpsimd
                    def _(pool):
                        for t in range(NT):
                            pool.wait_ge(taken, n_puts * (t + 1))
                            pool.tensor_tensor(x_sb[:, t, :], x_sb[:, t, :], h_sb[:, t, :], ALU.add)

        def split(v, parts, rest, table):
            dve = v.engine
            v.link(dve.tensor_copy(parts[:, 0, :, :], table))
            v.link(dve.tensor_tensor(rest[:, 0, :, :], table, parts[:, 0, :, :], ALU.subtract))
            v.link(dve.tensor_copy(parts[:, 1, :, :], rest[:, 0, :, :]))
            v.link(dve.tensor_tensor(rest[:, 1, :, :], rest[:, 0, :, :], parts[:, 1, :, :], ALU.subtract))
            v.link(dve.tensor_copy(parts[:, 2, :, :], rest[:, 1, :, :]))

        def for_begins(engine, body):
            for t0 in range(0, NT - 1, 8):
                n = min(8, NT - 1 - t0)
                _, at = nc.values_load_multi_w_load_instructions(
                    begin_d[0:1, t0:t0 + n], engines=(engine,), min_val=0, max_val=C - 1,
                    skip_runtime_bounds_check_because="a place in the edge list, shifted")
                for k in range(n):
                    body(t0 + k, at[k])

        def look_up(nh, at_src, dst_parts, beyond):
            W = NT * nh
            G = 4 if nh > 1 else GROUP
            per_piece = GROUP // G
            BANKS = 5

            def since_last(n):
                turn = RING * per_piece
                return BANKS if n >= BANKS else next(turn + n - m for m in reversed(range(turn)) if m % BANKS == n)

            KD = 3 * nh
            folds = nh > 1
            left = NT - NT // 2 if folds else NT
            lag = 3 if folds else 1
            with ExitStack() as st, nc.Block() as block:
                parts = sb(st, "parts", [P, 3, NT, nh], bf16)
                turned_parts = sb(st, "turned_parts", [NT, 3, nh, P], bf16)
                met = sb(st, "met", [P, CX, 3, nh], bf16)
                met_piece = sb(st, "met_piece", [P, RING, GROUP, KD], bf16)
                hot_s = sb(st, "hot_s", [P, RING, PIECE], bf16)
                hot_d = sb(st, "hot_d", [P, RING, PIECE], bf16)
                picked = sb(st, "picked", [P, RING, G, nh, NT], fp32)
                flat = picked[:, :, :, :, :].rearrange("p r g h t -> p (r g h t)")
                turned_al = flat[0:NT, 0:nh * P].rearrange("t (h p) -> t h p", h=nh)
                turned_rest = flat[0:NT, nh * P:3 * nh * P].rearrange("t (k h p) -> t k h p", k=2, h=nh)
                rest = flat[:, 3 * nh * P:3 * nh * P + 2 * NT * nh].rearrange("p (k t h) -> p k t h", k=2, h=nh)
                ps_s = banks(st, "ps_s", BANKS)
                ps_d = banks(st, "ps_d", 2)
                ps_m = banks(st, "ps_m", 1)[0]
                src_in = [sem(st, f"src_in{r}") for r in range(RING)]
                dst_in = [sem(st, f"dst_in{r}") for r in range(RING)]
                src_product = sem(st, "src_product")
                dst_product = sem(st, "dst_product")
                begin_product = sem(st, "begin_product")
                turned = sem(st, "turned")
                split_made = sem(st, "split_made")
                tile_product = sem(st, "tile_product")
                met_made = sem(st, "met_made")
                met_in = sem(st, "met_in")
                masked = sem(st, "masked")
                folded = sem(st, "folded")
                src_summed = sem(st, "src_summed")
                dst_taken = sem(st, "dst_taken")
                sv = sem(st, "dve_chain")

                @block.sync
                def _(sp):
                    with sp.Fori(0, PN // RING) as i:
                        for r in range(RING):
                            n = RING * i + r
                            sp.wait_ge(src_product, per_piece * (n + 1))
                            sp.dma_start(hot_s[:, r, :], one_hots[0, bass.ds(n, 1), :, :].rearrange("o p e -> p (o e)")).then_inc(src_in[r], 16)

                @block.scalar
                def _(act):
                    for n in range(KD):
                        act.wait_ge(tile_product, n + 1)
                        act.activation(met[:, :, n // nh, n % nh], ps_s[n % BANKS][:, 0:CX], ACT.Copy).then_inc(met_made, 1)
                    act.wait_ge(met_made, KD)

                    def load(n, r):
                        act.dma_start(hot_d[:, r, :], one_hots[1, bass.ds(n, 1), :, :].rearrange("o p e -> p (o e)")).then_inc(dst_in[r], 16)
                        act.activation(met_piece[:, r, :, :], met[:, bass.ds(n * GROUP, GROUP), :, :].rearrange("p c k h -> p c (k h)"),
                                       ACT.Copy).then_inc(met_in, 1)

                    def take(n, r):
                        act.wait_ge(dst_product, n + 1)
                        act.activation(dst_parts[:, bass.ds(n * GROUP, GROUP), :], ps_d[r % 2][:, 0:GROUP * KD].rearrange("p (c k) -> p c k", c=GROUP),
                                       ACT.Copy).then_inc(dst_taken, 1)

                    for r in range(RING - 1):
                        load(r, r)
                    with act.Fori(0, PN // RING - 1) as i:
                        for r in range(RING):
                            take(RING * i + r, r)
                            load(RING * i + r + RING - 1, (r + RING - 1) % RING)
                    for r in range(RING):
                        take(PN - RING + r, r)
                        if r == 0:
                            load(PN - 1, RING - 1)

                @block.vector
                def _(dve):
                    v = Chain(dve, sv)
                    v.link(dve.memset(beyond[:, 0, :], 0.0))
                    dve.sem_inc(src_product, RING * per_piece)
                    dve.sem_inc(dst_taken, 2)
                    dve.wait_ge(turned, 1)
                    v.link(dve.tensor_copy(flat[0:NT, 0:nh * P], ps_m[0:NT, 0:nh * P]))
                    split(v, turned_parts, turned_rest, turned_al)
                    dve.sem_inc(split_made, 1)
                    split(v, parts, rest, alphas[:, :, 0:nh])
                    dve.sem_inc(split_made, 1)
                    dve.sem_inc(src_summed, RING)
                    dve.sem_inc(masked, RING)

                    def add_up(k, at):
                        if folds:
                            dve.wait_ge(folded, k + 1)
                        else:
                            dve.wait_ge(masked, RING + k + 1)
                        dve.tensor_reduce(at_src[:, bass.ds(k * G, G), 0:nh], picked[:, at, :, :, 0:left], X, ALU.add).then_inc(src_summed, 1)

                    with dve.Fori(0, PN // RING) as i:
                        for n in range(RING * per_piece):
                            k = RING * per_piece * i + n
                            at = n % RING
                            dve.wait_ge(src_product, RING * per_piece + k + 1)
                            dve.wait_ge(src_summed, k + 1)
                            dve.tensor_tensor(
                                picked[:, at, :, :, :].rearrange("p c h t -> p c t h"),
                                ps_s[n % BANKS][:, 0:G * W].rearrange("p (c t h) -> p c t h", c=G, h=nh),
                                hot_hi[0][:, :, bass.ds(k * G, G)].rearrange("p t c -> p c t").unsqueeze(3).broadcast_to([P, G, NT, nh]),
                                ALU.mult).then_inc(masked, 1)
                            if n >= lag:
                                add_up(k - lag, (n - lag) % RING)
                        for n in range(RING * per_piece - lag, RING * per_piece):
                            add_up(RING * per_piece * i + n, n % RING)
                    dve.wait_ge(begin_product, 1)
                    v.link(dve.tensor_reduce(beyond[:, :, :], ps_m[:, 0:(NT - 1) * KD].rearrange("p (c k h) -> p c h k", k=3, h=nh), X, ALU.add))
                    dve.wait_ge(dst_taken, PN + 2)
                    dve.wait_ge(src_summed, RING + PN * per_piece)

                if folds:
                    @block.gpsimd
                    def _(pool):
                        with pool.Fori(0, PN // RING) as i:
                            for n in range(RING * per_piece):
                                k = RING * per_piece * i + n
                                of = picked[:, n % RING, :, :, :]
                                pool.wait_ge(masked, RING + k + 1)
                                pool.tensor_tensor(of[:, :, :, 0:NT - left], of[:, :, :, 0:NT - left], of[:, :, :, left:NT], ALU.add).then_inc(folded, 1)

                @block.tensor
                def _(pe):
                    for h in range(nh):
                        last = nc.tensor.transpose(ps_m[0:NT, h * P:(h + 1) * P], alphas[:, :, nh + h], ident[:, :])
                    last.then_inc(turned, 1)
                    pe.wait_ge(split_made, 1)
                    for n in range(KD):
                        if n >= BANKS:
                            pe.wait_ge(met_made, n - BANKS + 1)
                        nc.tensor.matmul(ps_s[n % BANKS][:, 0:CX], turned_parts[:, n // nh, n % nh, :], hot_tile[:, :],
                                         start=True, stop=True).then_inc(tile_product, 1)
                    pe.wait_ge(met_made, KD)
                    pe.wait_ge(split_made, 2)
                    for t in range(NT - 1):
                        last = nc.tensor.matmul(ps_m[:, t * KD:(t + 1) * KD], hot_begin[:, t, :],
                                                met[:, C + t, :, :].rearrange("p k h -> p (k h)"), start=True, stop=True)
                    last.then_inc(begin_product, 1)

                    def destinations(turn, r):
                        pe.wait_ge(dst_in[r], 16 * turn + 16)
                        pe.wait_ge(met_in, RING * turn + r + 1)
                        pe.wait_ge(dst_taken, RING * turn + r + (2 if r == 0 else 1))
                        for g in range(GROUP):
                            last = nc.tensor.matmul(ps_d[r % 2][:, g * KD:(g + 1) * KD], hot_d[:, r, g * P:(g + 1) * P],
                                                    met_piece[:, r, g, :], start=True, stop=True)
                        last.then_inc(dst_product, 1)

                    with pe.Fori(0, PN // RING) as i:
                        for r in range(RING):
                            pe.wait_ge(src_in[r], 16 * i + 16)
                            for j in range(per_piece):
                                n = per_piece * r + j
                                at = n % BANKS
                                pe.wait_ge(masked, RING * per_piece * i + n + 1 + RING - since_last(n))
                                for g in range(G):
                                    for k in range(3):
                                        last = nc.tensor.matmul(ps_s[at][:, g * W:(g + 1) * W], hot_s[:, r, (j * G + g) * P:(j * G + g + 1) * P],
                                                                parts[:, k, :, :].rearrange("p t h -> p (t h)"), start=(k == 0), stop=(k == 2))
                                last.then_inc(src_product, 1)
                            destinations(i, r)

        def edge_softmax(nh, at_src, at_dst, dst_parts, beyond, table, gathered, i_slot):
            L = nh * QB * P
            with ExitStack() as st, nc.Block() as block:
                ps = banks(st, "ps", 8)
                rows = sb(st, "rows", [Q, H * QB * P], fp32)
                run_f = sb(st, "run_f", [Q, H * QB * P], fp32)
                run_b = sb(st, "run_b", [Q, H * QB * P], fp32)
                ends = sb(st, "ends", [H, 2, C], fp32)
                carry = sb(st, "carry", [H, 2, C], fp32)
                top_src = sb(st, "top_src", [P, C, H], fp32)
                turned = sem(st, "turned")
                ran = sem(st, "ran")
                carried = sem(st, "carried")
                ready = sem(st, "ready")
                exped = sem(st, "exped")
                copied = sem(st, "copied")
                half_copied = sem(st, "half_copied")
                top_made = sem(st, "top_made")
                aux_made = sem(st, "aux_made")
                dst_summed = sem(st, "dst_summed")
                dst_added = sem(st, "dst_added")
                staged = sem(st, "staged")
                sv = sem(st, "dve_chain")

                def stage_first(act):
                    for s in range(U):
                        act.activation(i_slot[:, s:s + 1], gidx_d[:, s:s + 1], ACT.Copy).then_inc(staged, 1)

                def first_gathers(pool):
                    for s in range(U):
                        pool.wait_ge(staged, s + 1)
                        pool.indirect_dma_start(out=gathered[:, s, 0:F], out_offset=None, in_=table,
                                                in_offset=bass.IndirectOffsetOnAxis(ap=i_slot[:, s:s + 1], axis=0)).then_inc(slot_done[s], 16)

                def rows_v(tile):
                    return tile[:, 0:L].rearrange("q (h b p) -> q h b p", h=nh, p=P)

                @block.tensor
                def _(pe):
                    for h in range(nh):
                        for b in range(QB):
                            last = nc.tensor.transpose(ps[h][0:Q, b * P:(b + 1) * P], at_src[:, b * Q:(b + 1) * Q, h], ident[:, :])
                    last.then_inc(turned, 1)
                    pe.wait_ge(ran, 1)
                    for n, (tile, p) in enumerate(((run_f, P - 1), (run_b, 0))):
                        for b in range(QB):
                            last = nc.tensor.transpose(ps[4 + n][0:nh, b * Q:(b + 1) * Q], rows_v(tile)[:, :, b, p], ident[0:Q, 0:Q])
                    last.then_inc(turned, 1)
                    pe.wait_ge(carried, 1)
                    for n in range(2):
                        for b in range(QB):
                            last = nc.tensor.transpose(ps[6 + n][0:Q, b * nh:(b + 1) * nh], carry[0:nh, n, b * Q:(b + 1) * Q],
                                                       ident[0:nh, 0:nh])
                    last.then_inc(turned, 1)
                    pe.wait_ge(ran, 2)
                    for h in range(nh):
                        for b in range(QB):
                            last = nc.tensor.transpose(ps[h][:, b * Q:(b + 1) * Q], rows_v(run_f)[:, h, b, :], ident[0:Q, 0:Q])
                    last.then_inc(turned, 1)

                @block.vector
                def _(dve):
                    v = Chain(dve, sv)

                    def runs():
                        v.step(dve.tensor_tensor_scan(run_f[:, 0:L], reset_f[:, 0:L], rows[:, 0:L], -BIG, ALU.add, ALU.max))
                        v.link(dve.tensor_tensor_scan(run_b[:, 0:L][:, ::-1], reset_b[:, 0:L][:, ::-1], rows[:, 0:L][:, ::-1], -BIG,
                                                      ALU.add, ALU.max))

                    v.link(dve.tensor_reduce(at_dst[:, :, :], dst_parts[:, :, :].rearrange("p c (k h) -> p c h k", k=3), X, ALU.add))
                    dve.sem_inc(dst_summed, 1)
                    dve.wait_ge(turned, 1)
                    for h in range(0, nh, 2):
                        v.step(dve.tensor_copy(rows[:, h * QB * P:(h + 1) * QB * P], ps[h][0:Q, 0:QB * P]))
                    dve.wait_ge(sv, v.n)
                    dve.wait_ge(copied, 1)
                    runs()
                    dve.sem_inc(ran, 1)
                    dve.wait_ge(turned, 2)
                    v.link(dve.tensor_tensor_scan(ends[0:nh, 0, :], gate_f[0:nh, :], ps[4][0:nh, 0:C], -BIG, ALU.add, ALU.max))
                    v.link(dve.tensor_tensor_scan(ends[0:nh, 1, ::-1], gate_b[0:nh, ::-1], ps[5][0:nh, 0:C][:, ::-1], -BIG, ALU.add, ALU.max))
                    v.step(dve.tensor_tensor(carry[0:nh, 0, 1:C], ends[0:nh, 0, 0:C - 1], join_f[0:nh, 1:C], ALU.add))
                    v.step(dve.memset(carry[0:nh, 0, 0:1], -BIG))
                    v.step(dve.tensor_tensor(carry[0:nh, 1, 0:C - 1], ends[0:nh, 1, 1:C], join_b[0:nh, 0:C - 1], ALU.add))
                    v.link(dve.memset(carry[0:nh, 1, C - 1:C], -BIG))
                    dve.sem_inc(carried, 1)
                    dve.wait_ge(turned, 3)
                    for n, p in ((0, 0), (1, P - 1)):
                        v.link(dve.tensor_tensor(rows_v(rows)[:, :, :, p], rows_v(rows)[:, :, :, p],
                                                 ps[6 + n][0:Q, 0:QB * nh].rearrange("q (b h) -> q h b", h=nh), ALU.max))
                    runs()
                    v.link(dve.tensor_tensor(run_f[:, 0:L], run_f[:, 0:L], run_b[:, 0:L], ALU.max))
                    dve.sem_inc(ran, 1)
                    s, d, m = at_src[:, :, 0:nh], at_dst[:, :, 0:nh], top_src[:, :, 0:nh]
                    dve.wait_ge(dst_added, NT - 1)
                    v.link(dve.tensor_tensor(s, s, d, ALU.add))
                    v.link(dve.scalar_tensor_tensor(s, s, NEG_SLOPE, s, ALU.mult, ALU.max))
                    dve.wait_ge(turned, 4)
                    for h in range(0, nh, 2):
                        v.step(dve.tensor_copy(top_src[:, :, h], ps[h][:, 0:C]))
                    dve.wait_ge(sv, v.n)
                    dve.sem_inc(top_made, 1)
                    dve.wait_ge(copied, 2)
                    v.link(dve.tensor_tensor(d, m, d, ALU.add))
                    v.link(dve.scalar_tensor_tensor(d, d, NEG_SLOPE, d, ALU.mult, ALU.max))
                    v.link(dve.tensor_tensor(s, s, d, ALU.subtract))
                    dve.sem_inc(ready, 1)
                    dve.wait_ge(exped, 1)
                    dve.wait_ge(aux_made, 3)
                    for_begins(mybir.EngineType.DVE, lambda t, c: v.step(
                        dve.tensor_copy(edge_aux[:, C + t:C + t + 1, :], edge_aux[:, bass.ds(c, 1), :])))
                    dve.wait_ge(sv, v.n)

                @block.gpsimd
                def _(pool):
                    first_gathers(pool)
                    pool.wait_ge(dst_summed, 1)

                    def add_beyond(t, c):
                        if t:
                            pool.wait_ge(dst_added, t)
                        pool.tensor_tensor(at_dst[:, bass.ds(c, 1), 0:nh], at_dst[:, bass.ds(c, 1), 0:nh], beyond[:, t:t + 1, :],
                                           ALU.add).then_inc(dst_added, 1)

                    for_begins(mybir.EngineType.Pool, add_beyond)
                    pool.tensor_copy(edge_aux[:, 0:C, 2 * nh], is_last[:, :]).then_inc(aux_made, 1)
                    pool.memset(edge_aux[:, C:CX, :], 0.0).then_inc(aux_made, 1)
                    pool.wait_ge(top_made, 1)
                    pool.wait_ge(copied, 2)
                    pool.tensor_tensor(edge_aux[:, 0:C, nh:2 * nh], top_src[:, :, 0:nh], is_last[:, :].unsqueeze(2).broadcast_to([P, C, nh]),
                                       ALU.mult).then_inc(aux_made, 1)

                @block.scalar
                def _(act):
                    stage_first(act)
                    act.wait_ge(turned, 1)
                    for h in range(1, nh, 2):
                        act.activation(rows[:, h * QB * P:(h + 1) * QB * P], ps[h][0:Q, 0:QB * P], ACT.Copy).then_inc(half_copied, 1)
                    if nh > 1:
                        act.wait_ge(half_copied, nh // 2)
                    act.sem_inc(copied, 1)
                    act.wait_ge(turned, 4)
                    for h in range(1, nh, 2):
                        act.activation(top_src[:, :, h], ps[h][:, 0:C], ACT.Copy).then_inc(half_copied, 1)
                    if nh > 1:
                        act.wait_ge(half_copied, nh // 2 * 2)
                    act.sem_inc(copied, 1)
                    act.wait_ge(ready, 1)
                    act.activation(edge_aux[:, 0:C, 0:nh], at_src[:, :, 0:nh], ACT.Exp).then_inc(exped, 1)

        def aggregate(acc, table, index, local, tiles, weight=None, nh=0, aux=None, n_aux=0, begun=None, start=None):
            W = F + n_aux
            with ExitStack() as st, nc.Block() as block:
                ps = banks(st, "ps", U)
                weighted = weight is not None or nh > 0
                rows = begun[0] if begun else sb(st, "rows", [P, U, F if weighted else W], fp32)
                msg = sb(st, "msg", [P, U, W], fp32) if weighted else rows
                hot = sb(st, "hot", [P, U, P], fp32)
                i_slot = begun[1] if begun else sb(st, "i_slot", [P, U], i32)
                skip = 1 if begun else 0
                row_in, base = slot_done, 16 * slots_used[0]
                slots_used[0] += CX // U
                staged = sem(st, "staged")
                hot_made = sem(st, "hot_made")
                msg_made = sem(st, "msg_made")
                product = sem(st, "product")
                added = sem(st, "added")
                aux_put = sem(st, "aux_put")
                if start is not None:
                    start_row = sb(st, "start_row", [P, F], fp32)
                    start_in = sem(st, "start_in")

                    @block.sync
                    def _(sp):
                        sp.dma_start(start_row[:, :], row_broadcast(start)).then_inc(start_in, 16)

                row_used = msg_made if weighted else product
                iters = CX // U
                AHEAD = U // 2

                @block.scalar
                def _(act):
                    def put_aux(c, s):
                        act.wait_ge(product, c + 1)
                        act.activation(msg[:, s:s + 1, F:W], aux[:, bass.ds(c, 1), 0:n_aux], ACT.Copy).then_inc(aux_put, 1)

                    if begun:
                        for s in range(U):
                            put_aux(s, s)
                    with act.Fori(skip, iters) as i:
                        for s in range(U):
                            act.wait_ge(row_used, U * i + s + 1)
                            act.activation(i_slot[:, s:s + 1], index[:, bass.ds(U * i + s, 1)], ACT.Copy).then_inc(staged, 1)
                            if nh:
                                put_aux(U * i + s, s)

                @block.gpsimd
                def _(pool):
                    with pool.Fori(skip, iters) as i:
                        for s in range(U):
                            pool.wait_ge(staged, U * (i - skip) + s + 1)
                            pool.nop(nofuse=True)
                            pool.indirect_dma_start(out=rows[:, s, 0:F], out_offset=None, in_=table,
                                                    in_offset=bass.IndirectOffsetOnAxis(ap=i_slot[:, s:s + 1], axis=0)).then_inc(row_in[s], 16)

                @block.vector
                def _(dve):
                    def prepare(c, s, turn):
                        dve.tensor_scalar(hot[:, s, :], iota[:, :], local[:, bass.ds(c, 1)], None, ALU.is_equal).then_inc(hot_made, 1)
                        if not weighted:
                            return
                        dve.wait_ge(row_in[s], base + 16 * turn + 16)
                        if nh > 1:
                            m = dve.tensor_tensor(msg[:, s, 0:F].rearrange("p (h c) -> p h c", h=nh),
                                                  rows[:, s, :].rearrange("p (h c) -> p h c", h=nh),
                                                  aux[:, bass.ds(c, 1), 0:nh].rearrange("p o h -> p h o").broadcast_to([P, nh, CH]), ALU.mult)
                        elif nh == 1:
                            m = dve.tensor_scalar(msg[:, s, 0:F], rows[:, s, :], aux[:, bass.ds(c, 1), 0:1].rearrange("p o h -> p (o h)"), None, ALU.mult)
                        else:
                            m = dve.tensor_scalar(msg[:, s, 0:F], rows[:, s, :], weight[:, bass.ds(c, 1)], None, ALU.mult)
                        m.then_inc(msg_made, 1)

                    def tiles_of(c):
                        _, values = nc.values_load_multi_w_load_instructions(
                            tiles[0:1, bass.ds(c, U)], engines=(mybir.EngineType.DVE,), min_val=0, max_val=NT - 1,
                            skip_runtime_bounds_check_because="a tile is a node's number shifted, or below NT by its place")
                        return values

                    def add(c, s, t):
                        dve.wait_ge(product, c + 1 + U)
                        dve.wait_ge(added, c + U)
                        dve.tensor_tensor(acc[:, bass.ds(t, 1), 0:W], acc[:, bass.ds(t, 1), 0:W], ps[s][:, 0:W].unsqueeze(1),
                                          ALU.add).then_inc(added, 1)

                    if n_aux and not nh:
                        dve.memset(rows[:, :, F:W], 1.0).then_inc(aux_put, 1)
                    dve.memset(hot[:, 0, 0:1], 0.0).then_inc(msg_made, U)
                    dve.memset(hot[:, 0, 1:2], 0.0).then_inc(product, U)
                    dve.wait_ge(msg_made, U)
                    dve.wait_ge(product, U)
                    for s in range(AHEAD):
                        prepare(s, s, 0)
                    if start is None:
                        dve.memset(acc[:, :, :], 0.0).then_inc(added, U)
                    else:
                        dve.wait_ge(start_in, 16)
                        dve.tensor_copy(acc[:, :, 0:F], start_row[:, :].unsqueeze(1).broadcast_to([P, NT, F])).then_inc(added, U)
                    dve.wait_ge(added, U)
                    with dve.Fori(0, iters - 1) as i:
                        at = tiles_of(U * i)
                        for s in range(U):
                            n = s + AHEAD
                            prepare(U * i + n, n % U, i + n // U)
                            add(U * i + s, s, at[s])
                    at = tiles_of(U * (iters - 1))
                    for s in range(U):
                        c = U * (iters - 1) + s
                        if s < AHEAD:
                            prepare(c + AHEAD, s + AHEAD, iters - 1)
                        add(c, s, at[s])

                @block.tensor
                def _(pe):
                    if n_aux and not nh:
                        pe.wait_ge(aux_put, 1)
                    with pe.Fori(0, iters) as i:
                        for s in range(U):
                            c = U * i + s
                            pe.wait_ge(hot_made, c + 1)
                            if weighted:
                                pe.wait_ge(msg_made, c + 1 + U)
                            else:
                                pe.wait_ge(row_in[s], base + 16 * i + 16)
                            pe.wait_ge(added, c + 1)
                            if nh:
                                pe.wait_ge(aux_put, c + 1)
                            nc.tensor.matmul(ps[s][:, 0:W], hot[:, s, :], msg[:, s, :], start=True, stop=True).then_inc(product, 1)

        def gat_combine(acc, nh, bias, finish, temps, store):
            ch = F // nh
            with ExitStack() as st, nc.Block() as block:
                vec = sb(st, "vec", [P, F], fp32)
                small = sb(st, "small", [P, 6, NT, nh], fp32)
                loaded = sem(st, "loaded")
                ready = sem(st, "ready")
                exped = sem(st, "exped")
                sv = sem(st, "dve_chain")
                scales_made = sem(st, "scales_made")
                stored = sem(st, "stored")
                own_made = sem(st, "own_made")
                finish_sem = [sem(st, f"finish{n}") for n in range(2)]
                SHARE = NT * 3 // 5

                @block.sync
                def _(sp):
                    sp.dma_start(vec[:, :], row_broadcast(bias)).then_inc(loaded, 16)
                    if store:
                        store(sp, finish_sem, stored)

                @block.scalar
                def _(act):
                    act.wait_ge(ready, 1)
                    act.activation(small[:, 0:2, :, :], small[:, 0:2, :, :], ACT.Exp).then_inc(exped, 1)
                    act.wait_ge(scales_made, 1)
                    for t in range(SHARE, NT):
                        for h in range(nh):
                            cols = slice(h * ch, (h + 1) * ch)
                            act.activation(temps[:, t, cols], h_sb[:, t, cols], ACT.Copy, scale=small[:, 1, t, h:h + 1]).then_inc(own_made, 1)
                    finish(None, act, None, None, finish_sem)

                @block.gpsimd
                def _(pool):
                    pool.wait_ge(scales_made, 1)
                    pool.tensor_tensor(temps[:, 0:SHARE, :].rearrange("p t (h c) -> p t h c", h=nh),
                                       h_sb[:, 0:SHARE, :].rearrange("p t (h c) -> p t h c", h=nh),
                                       small[:, 1, 0:SHARE, :].unsqueeze(3).broadcast_to([P, SHARE, nh, ch]), ALU.mult).then_inc(own_made, 1)

                @block.vector
                def _(dve):
                    v = Chain(dve, sv)
                    edge_max, self_max, both, den, own, tmp = (small[:, k, :, :] for k in range(6))
                    a_s, a_d = alphas[:, :, 0:nh], alphas[:, :, nh:2 * nh]
                    any_edge = acc[:, :, F + 2 * nh:F + 2 * nh + 1].broadcast_to([P, NT, nh])
                    v.step(dve.tensor_tensor(self_max, a_s, a_d, ALU.add))
                    v.link(dve.tensor_tensor(edge_max, acc[:, :, F + nh:F + 2 * nh], a_d, ALU.add))
                    v.step(dve.scalar_tensor_tensor(self_max, self_max, NEG_SLOPE, self_max, ALU.mult, ALU.max))
                    v.step(dve.scalar_tensor_tensor(edge_max, edge_max, NEG_SLOPE, edge_max, ALU.mult, ALU.max))
                    v.link(dve.tensor_scalar(tmp, any_edge, -1.0, BIG, ALU.add, ALU.mult))
                    v.link(dve.tensor_tensor(edge_max, edge_max, tmp, ALU.add))
                    v.link(dve.tensor_tensor(both, edge_max, self_max, ALU.max))
                    v.step(dve.tensor_tensor(edge_max, edge_max, both, ALU.subtract))
                    v.link(dve.tensor_tensor(self_max, self_max, both, ALU.subtract))
                    dve.sem_inc(ready, 1)
                    dve.wait_ge(exped, 1)
                    v.link(dve.tensor_tensor(den, acc[:, :, F:F + nh], edge_max, ALU.mult))
                    v.link(dve.tensor_tensor(den, den, self_max, ALU.add))
                    v.link(dve.tensor_scalar(den, den, EPS_DEN, None, ALU.add))
                    v.link(dve.reciprocal(own, den))
                    v.step(dve.tensor_tensor(edge_max, edge_max, own, ALU.mult))
                    v.link(dve.tensor_tensor(self_max, self_max, own, ALU.mult))
                    dve.wait_ge(loaded, 16)
                    work = temps
                    dve.sem_inc(scales_made, 1)
                    edges = acc[:, :, 0:F].rearrange("p t (h c) -> p t h c", h=nh)
                    v.link(dve.tensor_tensor(edges, edges, edge_max.unsqueeze(3).broadcast_to([P, NT, nh, ch]), ALU.mult))
                    v.link(dve.tensor_tensor(acc[:, :, 0:F], acc[:, :, 0:F], vec[:, :].unsqueeze(1).broadcast_to([P, NT, F]), ALU.add))
                    dve.wait_ge(own_made, (NT - SHARE) * nh + 1)
                    v.link(dve.tensor_tensor(work[:, :, :], work[:, :, :], acc[:, :, 0:F], ALU.add))
                    finish(v, None, dve, work, finish_sem)

        def put_h(act, t, bank, taken, nh):
            act.activation(h_sb[:, t, :], bank[:, 0:F], ACT.Copy).then_inc(taken, 1)
            act.activation(alphas[:, t, 0:2 * nh], bank[:, F:F + 2 * nh], ACT.Copy).then_inc(taken, 1)

        def attention_layer(table, nh, temps_scope, bias, finish, store=None):
            index_slots = sb(temps_scope, "index_slots", [P, U], i32)
            gathered = sb(temps_scope, "gathered", [P, U, F], fp32)
            with ExitStack() as st:
                at_src = sb(st, "at_src", [P, C, nh], fp32)
                at_dst = sb(st, "at_dst", [P, C, nh], fp32)
                dst_parts = sb(st, "dst_parts", [P, C, 3 * nh], bf16)
                beyond = sb(st, "beyond", [P, NT - 1, nh], fp32)
                look_up(nh, at_src, dst_parts, beyond)
                edge_softmax(nh, at_src, at_dst, dst_parts, beyond, table, gathered, index_slots)
            acc = sb(temps_scope, "acc", [P, NT, F + 2 * nh + 1], fp32)
            aggregate(acc, table, gidx_d, local_d, tile_d, nh=nh, aux=edge_aux, n_aux=2 * nh + 1,
                      begun=(gathered, index_slots))
            work = sb(temps_scope, "work", [P, NT, F], fp32)
            gat_combine(acc, nh, bias, finish, work, store)

        with ExitStack() as ls:
            acc = sb(ls, "acc", [P, NT, F], fp32)
            aggregate(acc, tables[0], gidx_s, local_s, tile_s, weight=w_s, start=a["L0_gnn_bias"])
            with ExitStack() as st, nc.Block() as block:
                sv = sem(st, "dve_chain")

                @block.vector
                def _(dve):
                    v = Chain(dve, sv)
                    v.link(dve.scalar_tensor_tensor(x_sb[:, :, :], acc[:, :, :], 0.0, x_sb[:, :, :], ALU.max, ALU.add))

        with ExitStack() as ls:
            project(None, [a["L1_gnn_W1"]], (a["L1_gnn_att_src1"], a["L1_gnn_att_dst1"]), H,
                    lambda act, t, bank, taken: put_h(act, t, bank, taken, H), 2, tables[1], h_sb)

            def finish_elu(v, act, dve, work, done):
                halves = (slice(0, NT // 2), slice(NT // 2, NT))
                for n, part_of in enumerate(halves):
                    if act is not None:
                        act.wait_ge(done[0], n + 1)
                        act.activation(h_sb[:, part_of, :], h_sb[:, part_of, :], ACT.Exp).then_inc(done[1], 1)
                    else:
                        v.link(dve.tensor_scalar(h_sb[:, part_of, :], work[:, part_of, :], 0.0, None, ALU.min))
                        dve.sem_inc(done[0], 1)
                if dve is not None:
                    v.link(dve.tensor_scalar(work[:, :, :], work[:, :, :], 0.0, -1.0, ALU.max, ALU.add))
                    for n, part_of in enumerate(halves):
                        dve.wait_ge(done[1], n + 1)
                        v.step(dve.tensor_tensor(h_sb[:, part_of, :], work[:, part_of, :], h_sb[:, part_of, :], ALU.add))
                    dve.wait_ge(v.sem, v.n)

            with ExitStack() as ts:
                attention_layer(tables[1], H, ts, a["L1_gnn_b1"], finish_elu)

        with ExitStack() as ls:
            project(h_sb, [a["L1_gnn_W2"]], (a["L1_gnn_att_src2"], a["L1_gnn_att_dst2"]), 1,
                    lambda act, t, bank, taken: put_h(act, t, bank, taken, 1), 2, tables[2], h_sb)

            def finish_add(v, act, dve, work, done):
                if dve is not None:
                    v.link(dve.tensor_tensor(x_sb[:, :, :], x_sb[:, :, :], work[:, :, :], ALU.add))

            with ExitStack() as ts:
                attention_layer(tables[2], 1, ts, a["L1_gnn_b2"], finish_add)

        with ExitStack() as ls:
            with ExitStack() as fs:
                neigh = sb(fs, "neigh", [P, NT, F], fp32)

                def put_both(act, t, bank, taken):
                    act.activation(h_sb[:, t, :], bank[:, 0:F], ACT.Copy).then_inc(taken, 1)
                    act.activation(neigh[:, t, :], bank[:, F:2 * F], ACT.Copy).then_inc(taken, 1)

                def keep_32(v, tiles, best, left, finished):
                    dve = v.engine

                    def of(t, r):
                        return neigh[:, t, :] if r == 0 else left[:, t % 2, (r - 1) % 2, :]

                    for r in range(4):
                        for take_out in (False, True):
                            for k, t in enumerate(tiles):
                                if r or take_out:
                                    dve.wait_ge(v.sem, v.n - len(tiles) + 1)
                                if take_out:
                                    v.step(dve.match_replace(left[:, t % 2, r % 2, :], best[:, t % 2, :], of(t, r), -BIG))
                                else:
                                    v.step(dve.max(best[:, t % 2, :], of(t, r)))
                    for t in tiles:
                        dve.wait_ge(v.sem, v.n)
                        dve.scalar_tensor_tensor(neigh[:, t, :], left[:, t % 2, 1, :], -BIG, neigh[:, t, :], ALU.is_le,
                                                 ALU.mult).then_inc(finished, 1)

                project(None, [a["L2_gnn_W_self"], a["L2_gnn_W_neigh"]], (), 0, put_both, 2, tables[3], neigh, after=keep_32)
            acc = sb(ls, "acc", [P, NT, F + 1], fp32)
            aggregate(acc, tables[3], gidx_d, local_d, tile_d, n_aux=1)
            with ExitStack() as st, nc.Block() as block:
                deg = sb(st, "deg", [P, NT], fp32)
                sv = sem(st, "dve_chain")

                @block.vector
                def _(dve):
                    v = Chain(dve, sv)
                    v.link(dve.tensor_scalar(deg[:, :], acc[:, :, F], 1.0, None, ALU.max))
                    v.link(dve.reciprocal(deg[:, :], deg[:, :]))
                    for t in range(NT):
                        v.step(dve.scalar_tensor_tensor(x_sb[:, t, :], acc[:, t, 0:F], deg[:, t:t + 1], x_sb[:, t, :], ALU.mult, ALU.add))
                    dve.wait_ge(sv, v.n)

        with ExitStack() as ls:
            project(None, [a["L3_gnn_W"]], (a["L3_gnn_att_src"], a["L3_gnn_att_dst"]), H,
                    lambda act, t, bank, taken: put_h(act, t, bank, taken, H), 2, tables[4], h_sb)

            OUT_PARTS = (0, 7, 14, 20, NT)

            def finish_relu(v, act, dve, work, done):
                if dve is not None:
                    for t0, t1 in zip(OUT_PARTS, OUT_PARTS[1:]):
                        dve.scalar_tensor_tensor(x_sb[:, t0:t1, :], work[:, t0:t1, :], 0.0, x_sb[:, t0:t1, :], ALU.max,
                                                 ALU.add).then_inc(done[0], 1)

            def store_out(sp, done, stored):
                for n, (t0, t1) in enumerate(zip(OUT_PARTS, OUT_PARTS[1:])):
                    sp.wait_ge(done[0], n + 1)
                    full = min(t1, NT - 1)
                    sp.dma_start(out[t0 * P:full * P, :].rearrange("(t p) f -> p t f", p=P), x_sb[:, t0:full, :]).then_inc(stored, 16)
                sp.dma_start(out[(NT - 1) * P:N, :], x_sb[0:LAST, NT - 1, :]).then_inc(stored, 16)
                sp.wait_ge(stored, 16 * len(OUT_PARTS))

            with ExitStack() as ts:
                attention_layer(tables[4], H, ts, a["L3_gnn_bias"], finish_relu, store_out)



_INS = ["x", "src", "dst", "edge_weight", "node_vec1", "L0_gnn_weight", "L0_gnn_bias", "L1_gnn_W1", "L1_gnn_att_src1",
        "L1_gnn_att_dst1", "L1_gnn_b1", "L1_gnn_W2", "L1_gnn_att_src2", "L1_gnn_att_dst2", "L1_gnn_b2", "L2_gnn_W_self",
        "L2_gnn_W_neigh", "L3_gnn_W", "L3_gnn_att_src", "L3_gnn_att_dst", "L3_gnn_bias"]


def kernel(**inputs):
    import concourse.bacc as bacc
    from concourse.bass_utils import run_bass_kernel_spmd

    nc = bacc.Bacc("TRN2", target_bir_lowering=False, num_devices=1)
    arrays, args = {}, {}
    for name in _INS:
        array = np.ascontiguousarray(inputs[name])
        arrays[f"in_{name}"] = array
        args[name] = nc.dram_tensor(f"in_{name}", array.shape, mybir.dt.from_np(array.dtype), kind="ExternalInput").ap()
    out = nc.dram_tensor("out_x", arrays["in_x"].shape, fp32, kind="ExternalOutput").ap()
    gnn_kernel(nc, args, out)
    r = run_bass_kernel_spmd(nc, [arrays], core_ids=[0])
    return r.results[0]["out_x"]
```
